# Optimizing a Trainium2 kernel written in Bass

```python
import numpy as np
import jax
import jax.numpy as jnp

def _softmax(x, axis=-1):
    return jax.nn.softmax(x, axis=axis)

def _gelu(x):
    return jax.nn.gelu(x, approximate=True)

def _silu(x):
    return jax.nn.silu(x)

def _sigmoid(x):
    return jax.nn.sigmoid(x)

def _layernorm(x, axis=-1, eps=1e-05):
    m = jnp.mean(x, axis=axis, keepdims=True)
    v = jnp.var(x, axis=axis, keepdims=True)
    return (x - m) / jnp.sqrt(v + eps)

def _scatter_add(tgt, idx, src, axis=0):
    return tgt.at[idx].add(src)

def _segment_sum(src, seg, n):
    return jax.ops.segment_sum(src, seg, n)
kernel_name = 'mk_decoder_preln_d1_seqx_r8_68dd58'

def setup_inputs(seed: int=0):
    np.random.seed(seed)
    _w = jnp.asarray

    def _rec_inputs():
        import jax
        import jax.numpy as jnp
        _rk = jax.random.key(seed)
        x = -0.000125 + 0.9999 * jax.random.normal(jax.random.fold_in(_rk, 1), (4, 256, 256), jnp.float32)
        _lenS = 256 - jax.random.randint(jax.random.fold_in(_rk, 7), (4,), 0, max(1, 256 // 4) + 1, jnp.int32)
        _lenS2 = 256 - jax.random.randint(jax.random.fold_in(_rk, 8), (4,), 0, max(1, 256 // 4) + 1, jnp.int32)
        itok_BxS_13_99985 = jax.random.randint(jax.random.fold_in(_rk, 11), (4, 256), 13, 99986, jnp.int32)
        _ctx_2048P = jax.random.normal(jax.random.fold_in(_rk, 12), (4, 16, 256), jnp.float32)
        _ctx_2048c = jax.random.dirichlet(jax.random.fold_in(_rk, 512), 0.3 * jnp.ones((16,), jnp.float32), (4, 256))
        _ctx_2048t = jnp.einsum('bsk,bkd->bsd', _ctx_2048c, _ctx_2048P)
        _ctx_2048t = _ctx_2048t * jax.lax.rsqrt(jnp.mean(jnp.square(_ctx_2048t)) + 1e-12) * 0.953939
        ctx_2048 = 6.82029e-06 + 0.0200006 * (_ctx_2048t + 0.3 * jax.random.normal(jax.random.fold_in(_rk, 612), (4, 256, 256), jnp.float32))
        return (x, itok_BxS_13_99985, ctx_2048)
    x, itok_BxS_13_99985, ctx_2048 = _rec_inputs()

    def _L0_attn_setup():
        import jax, jax.numpy as jnp
        import numpy as np
        N_HEAD = 16
        D_MODEL = 256
        key = jax.random.key(seed)
        ks = jax.random.split(key, 9)
        B, T, C = (2, 256, D_MODEL)
        s = 1.0 / np.sqrt(C)
        return {'idx': jax.random.normal(ks[0], (B, T, C), dtype=jnp.float32), 'Wq': jax.random.normal(ks[1], (C, C), dtype=jnp.float32) * s, 'bq': jnp.zeros((C,), dtype=jnp.float32), 'Wk': jax.random.normal(ks[2], (C, C), dtype=jnp.float32) * s, 'bk': jnp.zeros((C,), dtype=jnp.float32), 'Wv': jax.random.normal(ks[3], (C, C), dtype=jnp.float32) * s, 'bv': jnp.zeros((C,), dtype=jnp.float32), 'Wo': jax.random.normal(ks[4], (C, C), dtype=jnp.float32) * s, 'bo': jnp.zeros((C,), dtype=jnp.float32)}
    _L0_attn_all = _L0_attn_setup()
    _L0_attn_in = {k: v for k, v in _L0_attn_all.items() if k in ('Wq', 'bq', 'Wk', 'bk', 'Wv', 'bv', 'Wo', 'bo')}
    del _L0_attn_all

    def _L0_xattn_setup():
        import jax, jax.numpy as jnp
        import numpy as np
        B, S, D = (4, 512, 256)
        E = 4
        F = 1024 // E
        VOCAB = 12500
        key = jax.random.key(seed)
        k1, k2, k3, k4, k5 = jax.random.split(key, 5)
        hidden_states = jax.random.normal(k1, (B, S, D), dtype=jnp.float32)
        token_ids = jax.random.randint(k2, (B, S), 0, VOCAB, dtype=jnp.int64)
        Wg = jax.random.normal(k3, (E, F, D), dtype=jnp.float32) * 0.02
        Wu = jax.random.normal(k4, (E, F, D), dtype=jnp.float32) * 0.02
        Wd = jax.random.normal(k5, (E, D, F), dtype=jnp.float32) * 0.02
        return {'hidden_states': hidden_states, 'token_ids': token_ids, 'Wg': Wg, 'Wu': Wu, 'Wd': Wd}
    _L0_xattn_all = _L0_xattn_setup()
    _L0_xattn_in = {k: v for k, v in _L0_xattn_all.items() if k in ()}
    del _L0_xattn_all

    def _L0_ffn_setup():
        import jax, jax.numpy as jnp
        import numpy as np
        H = 256
        NH = 16
        NOPE = 128
        ROPE = 64
        VD = 128
        QHD = NOPE + ROPE
        E = 16
        I = 176
        TOPK = 4
        NSH = 2
        SHI = I * NSH
        EPS = 1e-06
        B, S = (2, 128)

        def rmsnorm(x, w):
            return x * jax.lax.rsqrt(jnp.mean(x * x, axis=-1, keepdims=True) + EPS) * w
        key = jax.random.key(seed)
        ks = jax.random.split(key, 12)
        sd = lambda fan_in: 1.0 / np.sqrt(fan_in)
        return {'hidden_states': jax.random.normal(ks[0], (B, S, H), jnp.float32), 'positions': jnp.broadcast_to(jnp.arange(S, dtype=jnp.int32), (B, S)), 'ln1_w': jnp.ones((H,), jnp.float32), 'ln2_w': jnp.ones((H,), jnp.float32), 'q_w': jax.random.normal(ks[1], (NH * QHD, H), jnp.float32) * sd(H), 'kv_w': jax.random.normal(ks[2], (NH * (NOPE + VD) + ROPE, H), jnp.float32) * sd(H), 'o_w': jax.random.normal(ks[3], (H, NH * VD), jnp.float32) * sd(NH * VD), 'gate_w': jax.random.normal(ks[4], (E, H), jnp.float32) * sd(H), 'w1': jax.random.normal(ks[5], (E, 2 * I, H), jnp.float32) * sd(H), 'w2': jax.random.normal(ks[6], (E, H, I), jnp.float32) * sd(I), 'sh_gu_w': jax.random.normal(ks[7], (2 * SHI, H), jnp.float32) * sd(H), 'sh_down_w': jax.random.normal(ks[8], (H, SHI), jnp.float32) * sd(SHI)}
    _L0_ffn_all = _L0_ffn_setup()
    _L0_ffn_in = {k: v for k, v in _L0_ffn_all.items() if k in ('positions', 'ln1_w', 'ln2_w', 'q_w', 'kv_w', 'o_w', 'gate_w', 'w1', 'w2', 'sh_gu_w', 'sh_down_w')}
    del _L0_ffn_all
    return {'x': x, 'itok_BxS_13_99985': itok_BxS_13_99985, 'ctx_2048': ctx_2048, 'L0_attn_Wq': _L0_attn_in['Wq'], 'L0_attn_bq': _L0_attn_in['bq'], 'L0_attn_Wk': _L0_attn_in['Wk'], 'L0_attn_bk': _L0_attn_in['bk'], 'L0_attn_Wv': _L0_attn_in['Wv'], 'L0_attn_bv': _L0_attn_in['bv'], 'L0_attn_Wo': _L0_attn_in['Wo'], 'L0_attn_bo': _L0_attn_in['bo'], 'L0_ffn_positions': _L0_ffn_in['positions'], 'L0_ffn_ln1_w': _L0_ffn_in['ln1_w'], 'L0_ffn_ln2_w': _L0_ffn_in['ln2_w'], 'L0_ffn_q_w': _L0_ffn_in['q_w'], 'L0_ffn_kv_w': _L0_ffn_in['kv_w'], 'L0_ffn_o_w': _L0_ffn_in['o_w'], 'L0_ffn_gate_w': _L0_ffn_in['gate_w'], 'L0_ffn_w1': _L0_ffn_in['w1'], 'L0_ffn_w2': _L0_ffn_in['w2'], 'L0_ffn_sh_gu_w': _L0_ffn_in['sh_gu_w'], 'L0_ffn_sh_down_w': _L0_ffn_in['sh_down_w']}

def reference(x, itok_BxS_13_99985, ctx_2048, L0_attn_Wq, L0_attn_bq, L0_attn_Wk, L0_attn_bk, L0_attn_Wv, L0_attn_bv, L0_attn_Wo, L0_attn_bo, L0_ffn_positions, L0_ffn_ln1_w, L0_ffn_ln2_w, L0_ffn_q_w, L0_ffn_kv_w, L0_ffn_o_w, L0_ffn_gate_w, L0_ffn_w1, L0_ffn_w2, L0_ffn_sh_gu_w, L0_ffn_sh_down_w):
    import jax
    import jax.numpy as jnp

    def _L0_attn_ref(idx, Wq, bq, Wk, bk, Wv, bv, Wo, bo):
        import jax, jax.numpy as jnp
        import numpy as np
        N_HEAD = 16
        D_MODEL = 256
        B, T, C = idx.shape
        hs = C // N_HEAD

        def split_heads(x):
            return x.reshape(B, T, N_HEAD, hs).transpose(0, 2, 1, 3)
        q = split_heads(idx @ Wq + bq)
        k = split_heads(idx @ Wk + bk)
        v = split_heads(idx @ Wv + bv)
        scale = 1.0 / jnp.sqrt(jnp.asarray(hs, dtype=idx.dtype))
        scores = jnp.einsum('bhqd,bhkd->bhqk', q, k) * scale
        causal = jnp.tril(jnp.ones((T, T), dtype=bool))
        scores = jnp.where(causal, scores, -jnp.inf)
        attn = jax.nn.softmax(scores, axis=-1)
        out = jnp.einsum('bhqk,bhkd->bhqd', attn, v)
        out = out.transpose(0, 2, 1, 3).reshape(B, T, C)
        return out @ Wo + bo

    def _L0_xattn_ref(hidden_states, token_ids, Wg, Wu, Wd):
        import jax, jax.numpy as jnp
        import numpy as np
        B, S, D = (4, 512, 256)
        E = 4
        F = 1024 // E
        VOCAB = 12500
        tokens_per_expert = VOCAB // E
        tid = jnp.clip(token_ids, 0, VOCAB - 1)
        expert_ids = jnp.minimum(tid // tokens_per_expert, E - 1)
        out = jnp.zeros_like(hidden_states)
        for e in range(E):
            g = jax.nn.silu(jnp.einsum('bsd,fd->bsf', hidden_states, Wg[e]))
            u = jnp.einsum('bsd,fd->bsf', hidden_states, Wu[e])
            y = jnp.einsum('bsf,df->bsd', g * u, Wd[e])
            out = jnp.where((expert_ids == e)[..., None], y, out)
        return out

    def _L0_ffn_ref(hidden_states, positions, ln1_w, ln2_w, q_w, kv_w, o_w, gate_w, w1, w2, sh_gu_w, sh_down_w):
        import jax, jax.numpy as jnp
        import numpy as np
        H = 256
        NH = 16
        NOPE = 128
        ROPE = 64
        VD = 128
        QHD = NOPE + ROPE
        E = 16
        I = 176
        TOPK = 4
        NSH = 2
        SHI = I * NSH
        EPS = 1e-06
        B, S = (2, 128)

        def rmsnorm(x, w):
            return x * jax.lax.rsqrt(jnp.mean(x * x, axis=-1, keepdims=True) + EPS) * w
        b, s, h = hidden_states.shape
        x = rmsnorm(hidden_states, ln1_w)
        q = jnp.einsum('bsh,dh->bsd', x, q_w).reshape(b, s, NH, QHD)[..., :NOPE]
        kv = jnp.einsum('bsh,dh->bsd', x, kv_w)
        k = kv[..., :NH * NOPE].reshape(b, s, NH, NOPE)
        v = kv[..., NH * NOPE:NH * (NOPE + VD)].reshape(b, s, NH, VD)
        scale = QHD ** (-0.5)
        scores = jnp.einsum('bqnd,bknd->bnqk', q, k) * scale
        causal = jnp.tril(jnp.ones((s, s), bool))
        scores = jnp.where(causal, scores, -1000000000.0)
        p = jax.nn.softmax(scores, axis=-1)
        attn = jnp.einsum('bnqk,bknd->bqnd', p, v).reshape(b, s, NH * VD)
        attn_out = jnp.einsum('bsd,hd->bsh', attn, o_w)
        hid = hidden_states + attn_out
        x2 = rmsnorm(hid, ln2_w).reshape(-1, h)
        logits = x2 @ gate_w.T
        probs = jax.nn.softmax(logits, axis=-1)
        top_w, top_i = jax.lax.top_k(probs, TOPK)
        top_w = top_w / jnp.sum(top_w, axis=-1, keepdims=True)
        wfull = jnp.sum(jax.nn.one_hot(top_i, E, dtype=x2.dtype) * top_w[..., None], axis=1)
        gu = jnp.einsum('th,eih->tei', x2, w1)
        g, u = (gu[..., :I], gu[..., I:])
        act = jax.nn.silu(g) * u
        down = jnp.einsum('tei,ehi->teh', act, w2)
        routed = jnp.einsum('te,teh->th', wfull, down)
        sgu = x2 @ sh_gu_w.T
        sg, su = (sgu[..., :SHI], sgu[..., SHI:])
        shared = jax.nn.silu(sg) * su @ sh_down_w.T
        return hid + (routed + shared).reshape(b, s, h)
    x = x + _L0_attn_ref(_layernorm(x, axis=-1), L0_attn_Wq, L0_attn_bq, L0_attn_Wk, L0_attn_bk, L0_attn_Wv, L0_attn_bv, L0_attn_Wo, L0_attn_bo)
    x = x + _L0_xattn_ref(_layernorm(x, axis=-1), itok_BxS_13_99985, ctx_2048, ctx_2048, ctx_2048)
    x = x + _L0_ffn_ref(_layernorm(x, axis=-1), L0_ffn_positions, L0_ffn_ln1_w, L0_ffn_ln2_w, L0_ffn_q_w, L0_ffn_kv_w, L0_ffn_o_w, L0_ffn_gate_w, L0_ffn_w1, L0_ffn_w2, L0_ffn_sh_gu_w, L0_ffn_sh_down_w)
    return x

_drawn_inputs = setup_inputs


def setup_inputs(seed=0):
    import zlib

    import numpy as np

    out = dict(_drawn_inputs(seed))
    spreads = {'L0_attn_bq': (0.0, 0.316),
     'L0_attn_bk': (0.0, 0.8),
     'L0_attn_bv': (0.0, 0.1),
     'L0_attn_bo': (0.0, 0.1),
     'L0_ffn_ln1_w': (1.0, 0.2),
     'L0_ffn_ln2_w': (1.0, 0.2)}
    factors = {}
    for name, (base, spread) in spreads.items():
        noise = np.random.default_rng([zlib.crc32(name.encode()), seed]).standard_normal(out[name].shape)
        drawn = base * np.exp(spread * noise) if base else spread * noise
        out[name] = jnp.asarray(drawn.astype(out[name].dtype))
    for name, factor in factors.items():
        out[name] = (out[name] * factor).astype(out[name].dtype)
    return out
```

```python
from contextlib import ExitStack

import concourse.bass as bass
from concourse import mybir

F32 = mybir.dt.float32
BF16 = mybir.dt.bfloat16
I32 = mybir.dt.int32
ALU = mybir.AluOpType
ACT = mybir.ActivationFunctionType
AX = mybir.AxisListType

P = 128
B, T, D = 4, 256, 256
N = B * T
NT = N // P
KC = D // P
LN_EPS, RMS_EPS = 1e-5, 1e-6
H1, HD1 = 16, 16
HC = P // HD1
CH = H1 // HC
VP = HC * (P + HD1)
XE, VOCAB = 4, 12500
PER_EXPERT = VOCAB // XE
XB = 256
H3, HD3, QHD = 16, 128, 192
PAIRS = H3 // 2
E3, INNER, SHARED, TOPK = 16, 176, 352, 4
CHANNELS = E3 * INNER + SHARED
NCH = -(-CHANNELS // P)
HALF = 512
WSLOTS = 4
MASKED = -1.0e30


def decoder_kernel(nc, x_in, tok_in, ctxT_in, wqT_in, wkT_in, wvT_in, woT_in, vec_in, bo_in, ffn_qkv_in, ffn_o_in,
                   gate_in, moe_in, ident_in, tri_in, headmask_in, sel_in, out):
    with ExitStack() as ctx:
        def sb(name, shape, dt=F32):
            return ctx.enter_context(nc.sbuf_tensor(name, shape, dt))

        def sem(name):
            return ctx.enter_context(nc.semaphore(name))

        bank = [ctx.enter_context(nc.psum_tensor(f"bank{i}", [P, 512], F32)) for i in range(8)]
        S_PS, PT_PS, O_PS, F_PS = bank[0:2], bank[2:4], bank[4:6], bank[6:8]

        ident = sb("ident", [P, P])
        identb = sb("identb", [P, P], BF16)
        tri = sb("tri", [P, P])
        trib = sb("trib", [P, P], BF16)
        headmask = sb("headmask", [P, HC])
        vec = sb("vec", [P, 10])
        bqs = sb("bqs", [P, 2])
        bo = sb("bo", [P, D])
        pw = sb("pw", [P, NT])
        zb = sb("zb", [P, 512], BF16)
        x = sb("x", [P, NT, D])
        h = sb("h", [P, NT, D])
        acc = sb("acc", [P, NT, D])
        hT = sb("hT", [P, KC, N])
        st = sb("st", [P, NT, 6])
        mv = sb("mv", [P, NT, 2])
        ve = sb("ve", [P, NT])
        rstd = sb("rstd", [P, NT])
        ss = sb("ss", [P, NT])
        sq = sb("sq", [P, D])
        p_sb = sb("p_sb", [P, 2, 384])
        pt_sb = sb("pt_sb", [P, 2, 384])
        nmax = sb("nmax", [P, 2, 2])
        psum_ = sb("psum_", [P, 2, 2])
        prec = sb("prec", [P, 2, 2])

        s_const = sem("s_const")
        s_castc = sem("s_castc")
        s_init = sem("s_init")
        ONE = 1
        credit = sb("credit", [P, 6])

        block = ctx.enter_context(nc.Block())

        class Norm:

            def __init__(self, tag):
                self.stat = sem(f"{tag}_stat")
                self.var = sem(f"{tag}_var")
                self.h = sem(f"{tag}_h")
                self.tr = sem(f"{tag}_tr")
                self.hT = sem(f"{tag}_hT")

        n1, n2, n3, n3r, n4 = Norm("n1"), Norm("n2"), Norm("n3"), Norm("n3r"), Norm("n4")

        def ln_vector(dve, s, src, dst):
            for t in range(NT):
                dve.bn_stats(st[:, t, :], src[:, t, :]).then_inc(s.stat, 1)
            for t in range(NT):
                dve.wait_ge(s.stat, t + 1)
                dve.bn_aggr(mv[:, t, :], st[:, t, :]).then_inc(s.stat, 1)
            dve.wait_ge(s.var, 2)
            for t in range(NT):
                dve.tensor_scalar(dst[:, t, :], src[:, t, :], mv[:, t, 0:1], rstd[:, t:t + 1],
                                  ALU.subtract, ALU.mult).then_inc(s.h, 1)

        def ln_gpsimd(pool, s):
            pool.wait_ge(s.stat, 2 * NT)
            pool.tensor_scalar(ve[:, :], mv[:, :, 1], LN_EPS, 1.0, ALU.add, ALU.mult).then_inc(s.var, 1)
            pool.wait_ge(s.var, 1)
            pool.tensor_tensor(rstd[:, :], ve[:, :], pw[:, :], ALU.pow).then_inc(s.var, 1)

        def rms_scalar(act, s, src, made=None):
            for t in range(NT):
                if made is not None:
                    act.wait_ge(made.h, t + 1)
                if t:
                    act.wait_ge(s.stat, t)
                act.activation(sq[:, :], src[:, t, :], ACT.Square, accum_out=ss[:, t:t + 1]).then_inc(s.stat, 1)

        def rms_gpsimd(pool, s):
            pool.wait_ge(s.stat, NT)
            pool.tensor_scalar(ve[:, :], ss[:, :], 1.0 / D, RMS_EPS, ALU.mult, ALU.add).then_inc(s.var, 1)
            pool.wait_ge(s.var, 1)
            pool.tensor_tensor(rstd[:, :], ve[:, :], pw[:, :], ALU.pow).then_inc(s.var, 1)

        def rms_vector(dve, s, src, dst):
            dve.wait_ge(s.var, 2)
            for t in range(NT):
                dve.tensor_scalar(dst[:, t, :], src[:, t, :], rstd[:, t:t + 1], None, ALU.mult).then_inc(s.h, 1)

        def transposes(pe, s, src, base=0):
            for g in range(2):
                for c in range(KC):
                    for j in range(4):
                        pe.wait_ge(s.h, 4 * g + j + 1)
                        mm = pe.transpose(bank[4 + 2 * g + c][:, j * P:(j + 1) * P],
                                          src[:, 4 * g + j, c * P:(c + 1) * P], ident[:, :])
                    mm.then_inc(s.tr, 1)

        def hT_scalar(act, s, weight=None):
            for g in range(2):
                for c in range(KC):
                    act.wait_ge(s.tr, 2 * g + c + 1)
                    dst = hT[:, c, g * 512:(g + 1) * 512]
                    if weight is None:
                        act.activation(dst, bank[4 + 2 * g + c][:, :], ACT.Copy).then_inc(s.hT, 1)
                    else:
                        act.activation(dst, bank[4 + 2 * g + c][:, :], ACT.Copy,
                                       scale=vec[:, weight + c:weight + c + 1]).then_inc(s.hT, 1)

        class Unit:
            def __init__(self, tag):
                self.s = sem(f"{tag}_s")
                self.nm = sem(f"{tag}_nm")
                self.ex = sem(f"{tag}_ex")
                self.rs = sem(f"{tag}_rs")
                self.pn = sem(f"{tag}_pn")
                self.t = sem(f"{tag}_t")
                self.pt = sem(f"{tag}_pt")
                self.o = sem(f"{tag}_o")

        def pe_scores(pe, u, n, k, qT, keys, first):
            if not first:
                pe.wait_ge(u.ex, 2 * (n - 1))
            s_ps = S_PS[k]
            pe.matmul(s_ps[:, 0:256], qT[:, P:2 * P], keys, start=True, stop=False, skip_group_check=True)
            pe.matmul(s_ps[:, 256:384], qT[:, 0:P], keys[:, 0:P], start=False, stop=False, skip_group_check=True)
            pe.matmul(s_ps[:, 128:256], identb[:, :], trib[:, :], start=False, stop=False, skip_group_check=True)
            pe.matmul(s_ps[:, 256:384], identb[:, :], trib[:, :], start=False, stop=True,
                      skip_group_check=True).then_inc(u.s, 1)

        def dve_max(dve, u, n, k):
            dve.wait_ge(u.s, n + 1)
            dve.tensor_reduce(nmax[:, k, 0:1], S_PS[k][:, 0:256], AX.X, ALU.max, negate=True).then_inc(u.nm, 1)
            dve.tensor_reduce(nmax[:, k, 1:2], S_PS[k][:, 256:384], AX.X, ALU.max, negate=True).then_inc(u.nm, 1)

        def act_exp(act, u, n, k, first):
            act.wait_ge(u.nm, 2 * n + 2)
            if not first:
                act.wait_ge(u.t, n - 1)
            act.activation(p_sb[:, k, 0:256], S_PS[k][:, 0:256], ACT.Exp, bias=nmax[:, k, 0:1],
                           accum_out=psum_[:, k, 0:1]).then_inc(u.ex, 1)
            act.activation(p_sb[:, k, 256:384], S_PS[k][:, 256:384], ACT.Exp, bias=nmax[:, k, 1:2],
                           accum_out=psum_[:, k, 1:2]).then_inc(u.ex, 1)

        def dve_recip(dve, u, n, k):
            dve.wait_ge(u.ex, 2 * n + 2)
            dve.reciprocal(prec[:, k, :], psum_[:, k, :]).then_inc(u.rs, 1)

        def pool_normalise(pool, u, n, k):
            pool.wait_ge(u.rs, n + 1)
            for cols, r in ((slice(0, 256), prec[:, k, 0:1]), (slice(256, 384), prec[:, k, 1:2])):
                p = p_sb[:, k, cols]
                pool.tensor_tensor(p, p, r.to_broadcast(p.shape), ALU.mult).then_inc(u.pn, 1)

        def pe_transpose(pe, u, n, k, first):
            pe.wait_ge(u.pn, 2 * n + 2)
            if not first:
                pe.wait_ge(u.pt, n - 1)
            pe.transpose(PT_PS[k][:, 0:128], p_sb[:, k, 256:384], ident[:, :])
            pe.transpose(PT_PS[k][:, 128:256], p_sb[:, k, 0:128], ident[:, :])
            pe.transpose(PT_PS[k][:, 256:384], p_sb[:, k, 128:256], ident[:, :]).then_inc(u.t, 1)

        def dve_pt(dve, u, n, k, first):
            dve.wait_ge(u.t, n + 1)
            if not first:
                dve.wait_ge(u.o, n - 1)
            dve.tensor_copy(pt_sb[:, k, :], PT_PS[k][:, 0:384]).then_inc(u.pt, 1)

        def pe_pv(pe, u, n, k, o_ps, v0, v1, start=True, stop=True):
            pe.wait_ge(u.pt, n + 1)
            pe.matmul(o_ps[:, 0:256], v0, pt_sb[:, k, 0:256], start=start, stop=False, skip_group_check=True)
            pe.matmul(o_ps[:, 128:256], v1, pt_sb[:, k, 256:384], start=False, stop=stop,
                      skip_group_check=True).then_inc(u.o, 1)

        wq = sb("wq", [P, KC, D])
        wk = sb("wk", [P, KC, D])
        wv = sb("wv", [P, KC, D])
        wo = sb("wo", [P, KC, D])
        hb = sb("hb", [P, KC, T])
        q1 = sb("q1", [P, CH, T])
        k1 = sb("k1", [P, T])
        kbd = sb("kbd", [P, CH, HC, T])
        vbd = sb("vbd", [P, CH, 2, VP])
        o1 = sb("o1", [P, CH, T])

        u1 = Unit("u1")
        s_x = sem("s_x")
        s_w1 = sem("s_w1")
        s_hb = sem("s_hb")
        s_qk1 = sem("s_qk1")
        s_v1 = sem("s_v1")
        s_qe1 = sem("s_qe1")
        s_kbd = sem("s_kbd")
        s_ve1 = sem("s_ve1")
        s_oe1 = sem("s_oe1")
        s_wo1 = sem("s_wo1")
        s_x1 = sem("s_x1")
        s_bo = sem("s_bo")

        def body1(eng_part, b, first, last):
            for c in range(CH):
                m = CH * b + c
                for j in range(HC):
                    n = (CH * HC) * b + HC * c + j
                    i = HC * c + j
                    end = last and i == CH * HC - 1
                    eng_part(b, m, c, j, n, i % 2, i, first, last, end)

        def pe_qkv1(pe, b, m, c, first=False, x1_before=None):
            cols = slice(c * P, (c + 1) * P)
            if not first:
                pe.wait_ge(s_qe1, 2 * m)
            for q in range(KC):
                pe.matmul(F_PS[0][:, 0:T], wq[:, q, cols], hT[:, q, bass.ds(b * T, T)], start=(q == 0),
                          stop=(q == KC - 1), skip_group_check=True)
            for q in range(KC):
                mm = pe.matmul(F_PS[0][:, T:2 * T], wk[:, q, cols], hT[:, q, bass.ds(b * T, T)], start=(q == 0),
                               stop=(q == KC - 1), skip_group_check=True)
            mm.then_inc(s_qk1, 1)
            pe.wait_ge(s_hb, b + 1)
            if not first:
                pe.wait_ge(s_ve1, 2 * m)
            if x1_before is not None:
                pe.wait_ge(s_x1, x1_before)
            for t in range(2):
                for q in range(KC):
                    mm = pe.matmul(F_PS[1][:, t * P:(t + 1) * P], hb[:, q, t * P:(t + 1) * P], wv[:, q, cols],
                                   start=(q == 0), stop=(q == KC - 1), skip_group_check=True)
            mm.then_inc(s_v1, 1)

        def pe_wo1(pe, b, ve_before):
            pe.wait_ge(s_oe1, 2 * b + 2)
            pe.wait_ge(s_ve1, ve_before)
            for t in range(2):
                for c in range(CH):
                    mm = pe.matmul(F_PS[1][:, t * D:(t + 1) * D], o1[:, c, t * P:(t + 1) * P], wo[:, c, :],
                                   start=(c == 0), stop=(c == CH - 1), skip_group_check=True)
            mm.then_inc(s_wo1, 1)

        def pe_s1(pe, n, i, m, c, j, first):
            if j == 0:
                pe.wait_ge(s_kbd, m + 1)
            pe_scores(pe, u1, n, i % 2, q1[:, c, :], kbd[:, c, j, :], first)

        def pe_pv1(pe, n, i, m, c, j, nofree):
            if j == 0:
                pe.wait_ge(s_ve1, 2 * m + 2)
                if not nofree:
                    pe.wait_ge(s_oe1, m - 1)
            v = vbd[:, c, :, :]
            pe_pv(pe, u1, n, i % 2, O_PS[c], v[:, 0, j * P:(j + 1) * P], v[:, 1, j * P:(j + 1) * P],
                  start=(j == 0), stop=(j == HC - 1))

        def pe_slot1(pe):
            def slot(b, m, c, j, n, k, i, first, last, end):
                if not end:
                    i2 = (i + 1) % (CH * HC)
                    c2, j2 = divmod(i2, HC)
                    pe_s1(pe, n + 1, i2, (m + 1) if j == HC - 1 else m, c2, j2, first and i == 0)
                if not (first and i == 0):
                    i0 = (i - 1) % (CH * HC)
                    c0, j0 = divmod(i0, HC)
                    pe_pv1(pe, n - 1, i0, (m - 1) if j == 0 else m, c0, j0, first)
                if j == 1 and not (last and c == CH - 1):
                    pe_qkv1(pe, b if c == 0 else b + 1, m + 1, 1 - c,
                            x1_before=b if (c == 1 and not first) else None)
                if j == 4 and c == 0 and not first:
                    pe_wo1(pe, b - 1, 4 * b + 4)
                pe_transpose(pe, u1, n, k, first and i < 2)
            return slot

        def act_q1(act, m, c):
            act.wait_ge(s_qk1, m + 1)
            act.activation(q1[:, c, :], F_PS[0][:, 0:T], ACT.Identity, bias=bqs[:, c:c + 1],
                           scale=float(HD1) ** -0.5).then_inc(s_qe1, 1)
            if not (isinstance(m, int) and m == 0):
                act.wait_ge(s_kbd, m)
            act.activation(k1[:, :], F_PS[0][:, T:2 * T], ACT.Identity, bias=vec[:, 2 + c:3 + c]).then_inc(s_qe1, 1)

        def act_v1(act, m, c):
            act.wait_ge(s_v1, m + 1)
            for t in range(2):
                dst = vbd[:, c, t, :].rearrange("p (j y) -> p j y", y=P + HD1)[:, :, 0:HD1]
                act.activation(dst, F_PS[1][:, t * P:(t + 1) * P].rearrange("p (j d) -> p j d", d=HD1),
                               ACT.Copy).then_inc(s_ve1, 1)

        def act_o1(act, n_done, c, projected):
            act.wait_ge(u1.o, n_done)
            if projected is not None:
                act.wait_ge(s_wo1, ONE + projected)
            act.activation(o1[:, c, :], O_PS[c][:, 0:T], ACT.Identity, bias=vec[:, 4 + c:5 + c]).then_inc(s_oe1, 1)

        def act_slot1(act):
            def slot(b, m, c, j, n, k, i, first, last, end):
                if not end:
                    act_exp(act, u1, n + 1, 1 - k, first and i == 0)
                if j == 1 and not (first and c == 0):
                    act_o1(act, n - 1, 1 - c, None if first else (b if c == 1 else b - 1))
                if j == 2 and not (last and c == CH - 1):
                    act_q1(act, m + 1, 1 - c)
                if j == 3 and not (last and c == CH - 1):
                    act_v1(act, m + 1, 1 - c)
            return slot

        def dve_kbd(dve, m, c):
            dve.wait_ge(s_qe1, 2 * m + 2)
            dve.tensor_tensor(kbd[:, c, :, :], k1[:, :].unsqueeze(1).to_broadcast([P, HC, T]),
                              headmask[:, :].unsqueeze(2).to_broadcast([P, HC, T]), ALU.mult).then_inc(s_kbd, 1)

        def dve_hb(dve, b):
            dve.tensor_copy(hb[:, :, :], hT[:, :, bass.ds(b * T, T)]).then_inc(s_hb, 1)

        def dve_x1(dve, b):
            dve.wait_ge(s_wo1, ONE + b + 1)
            dve.wait_ge(s_bo, 1)
            xs = x[:, bass.ds(2 * b, 2), :].rearrange("p t d -> p (t d)")
            dve.tensor_tensor(xs, xs, F_PS[1][:, :], ALU.add).then_inc(s_x1, 1)

        def dve_slot1(dve):
            def slot(b, m, c, j, n, k, i, first, last, end):
                if not (first and i == 0):
                    dve_pt(dve, u1, n - 1, 1 - k, first and i < 3)
                if not end:
                    dve_max(dve, u1, n + 1, 1 - k)
                if j == 3 and not (last and c == CH - 1):
                    dve_kbd(dve, m + 1, 1 - c)
                if j == 5 and c == 0 and not last:
                    dve.wait_ge(s_v1, m + 2)
                    dve_hb(dve, b + 1)
                if j == 5 and c == 0 and not first:
                    dve_x1(dve, b - 1)
                if not end:
                    dve_recip(dve, u1, n + 1, 1 - k)
            return slot

        def pool_slot1(pool):
            def slot(b, m, c, j, n, k, i, first, last, end):
                if not end:
                    pool_normalise(pool, u1, n + 1, 1 - k)
            return slot

        def run1(eng, slot):
            body1(slot, 0, True, False)
            with eng.Fori(1, B - 1) as b:
                body1(slot, b, False, False)
            body1(slot, B - 1, False, True)

        ctxT = sb("ctxT", [P, XE, KC, D])
        tid = sb("tid", [P, N], I32)
        onehot = sb("onehot", [P, XE, N])
        GX = XE * KC
        zs = sb("zs", [P, 2, XB])
        gu = sb("gu", [P, GX, XB])
        s_ctx = sem("s_ctx")
        s_tid = sem("s_tid")
        s_oh = sem("s_oh")
        s_z = sem("s_z")
        s_zs = sem("s_zs")
        s_zz = sem("s_zz")
        s_gu = sem("s_gu")
        s_y = sem("s_y")
        s_x2 = sem("s_x2")

        def pe_experts(pe):
            pe.wait_ge(s_ctx, 16)
            pe.wait_ge(n2.hT, 4)
            with pe.Fori(0, N // XB) as t:
                def z(g):
                    e, f = divmod(g, KC)
                    if g < 2:
                        pe.wait_ge(s_zz, ONE + GX * t)
                    else:
                        pe.wait_ge(s_zz, ONE + GX * t + g - 1)
                    for q in range(KC):
                        mm = pe.matmul(F_PS[g % 2][:, 0:XB], ctxT[:, e, q, f * P:(f + 1) * P],
                                       hT[:, q, bass.ds(t * XB, XB)], start=(q == 0), stop=(q == KC - 1))
                    mm.then_inc(s_z, 1)

                def down(g):
                    e, f = divmod(g, KC)
                    pe.wait_ge(s_gu, ONE + GX * t + g + 1)
                    if g == 0:
                        pe.wait_ge(s_x2, ONE + 2 * t)
                    for i in range(2):
                        mm = pe.matmul(O_PS[i][:, 0:D], gu[:, g, i * P:(i + 1) * P], ctxT[:, e, f, :],
                                       start=(g == 0), stop=(g == GX - 1))
                    if g == GX - 1:
                        mm.then_inc(s_y, 1)

                z(0)
                z(1)
                for g in range(2, GX):
                    z(g)
                    down(g - 2)
                down(GX - 2)
                down(GX - 1)

        def act_experts(act):
            with act.Fori(0, N // XB) as t:
                for g in range(GX):
                    act.wait_ge(s_z, GX * t + g + 1)
                    if g < 2:
                        act.wait_ge(s_gu, ONE + GX * t)
                    else:
                        act.wait_ge(s_gu, ONE + GX * t + g - 1)
                    act.activation(zs[:, g % 2, :], F_PS[g % 2][:, 0:XB], ACT.Silu).then_inc(s_zs, 1)

        def dve_onehot(dve):
            dve.wait_ge(s_tid, 16)
            dve.tensor_scalar(onehot[:, 0, :], tid[:, :], float(PER_EXPERT), None, ALU.is_lt).then_inc(s_oh, 1)
            for e in range(1, XE):
                dve.tensor_scalar(onehot[:, e, :], tid[:, :], float(PER_EXPERT * e), None, ALU.is_ge).then_inc(s_oh, 1)
            dve.wait_ge(s_oh, XE)
            for e in range(1, XE - 1):
                dve.tensor_tensor(onehot[:, e, :], onehot[:, e, :], onehot[:, e + 1, :], ALU.subtract)\
                   .then_inc(s_oh, 1)
                dve.wait_ge(s_oh, XE + e)

        def dve_experts(dve):
            with dve.Fori(0, N // XB) as t:
                for g in range(GX):
                    dve.wait_ge(s_zs, GX * t + g + 1)
                    dve.tensor_tensor(zs[:, g % 2, :], zs[:, g % 2, :], F_PS[g % 2][:, 0:XB], ALU.mult)\
                       .then_inc(s_zz, 1)
                    dve.wait_ge(s_zz, ONE + GX * t + g + 1)
                    if g == 0:
                        dve.wait_ge(s_y, ONE + t)
                    dve.tensor_tensor(gu[:, g, :], zs[:, g % 2, :], onehot[:, g // KC, bass.ds(t * XB, XB)],
                                      ALU.mult).then_inc(s_gu, 1)
                dve.wait_ge(s_y, ONE + t + 1)
                for i in range(2):
                    xs = x[:, bass.ds(2 * t + i, 1), :].rearrange("p t d -> p (t d)")
                    dve.tensor_tensor(xs, xs, O_PS[i][:, 0:D], ALU.add).then_inc(s_x2, 1)

        w3 = sb("w3", [P, 2, 3, KC, HD3])
        wo3 = sb("wo3", [P, 2, D])
        q3 = sb("q3", [P, 2, N])
        k3 = sb("k3", [P, 2, N])
        v3 = sb("v3", [P, 2, NT, HD3])
        o3 = sb("o3", [P, 2, N])
        u3 = Unit("u3")
        s_w3 = [sem("s_w3a"), sem("s_w3b")]
        s_wo3 = sem("s_wo3")
        s_f3 = sem("s_f3")
        s_fe3 = sem("s_fe3")
        s_oe3 = sem("s_oe3")
        s_wd3 = sem("s_wd3")
        s_acc = sem("s_acc")

        def pe_proj3(pe, head, a, part, acc_before=None):
            for i in range(2):
                f = 6 * head + 2 * part + i
                if not (isinstance(f, int) and f < 2):
                    pe.wait_ge(s_fe3, f - 1)
                if acc_before is not None:
                    pe.wait_ge(s_acc, acc_before - 1 + i)
                if part < 2:
                    for q in range(KC):
                        mm = pe.matmul(F_PS[i][:, :], w3[:, a, part, q, :], hT[:, q, i * 512:(i + 1) * 512],
                                       start=(q == 0), stop=(q == KC - 1))
                else:
                    for t in range(4):
                        for q in range(KC):
                            mm = pe.matmul(F_PS[i][:, t * P:(t + 1) * P],
                                           hT[:, q, (4 * i + t) * P:(4 * i + t + 1) * P], w3[:, a, 2, q, :],
                                           start=(q == 0), stop=(q == KC - 1), skip_group_check=True)
                mm.then_inc(s_f3, 1)

        def act_proj3(act, head, a, part):
            for i in range(2):
                act.wait_ge(s_f3, 6 * head + 2 * part + i + 1)
                half = slice(i * 512, (i + 1) * 512)
                if part == 0:
                    act.activation(q3[:, a, half], F_PS[i][:, :], ACT.Copy, scale=float(QHD) ** -0.5)\
                       .then_inc(s_fe3, 1)
                elif part == 1:
                    act.activation(k3[:, a, half], F_PS[i][:, :], ACT.Copy).then_inc(s_fe3, 1)
                else:
                    act.activation(v3[:, a, 4 * i:4 * i + 4, :].rearrange("p t d -> p (t d)"), F_PS[i][:, :],
                                   ACT.Copy).then_inc(s_fe3, 1)

        def pe_wo3(pe, p, fe_before):
            pe.wait_ge(s_wo3, 16 * (p + 1))
            pe.wait_ge(s_oe3, 4 * (p + 1))
            for g in range(4):
                if g < 2:
                    pe.wait_ge(s_fe3, fe_before - 1 + g)
                else:
                    pe.wait_ge(s_acc, 4 * p + g - 1)
                for t in range(2):
                    for a in range(2):
                        mm = pe.matmul(F_PS[g % 2][:, t * D:(t + 1) * D],
                                       o3[:, a, (2 * g + t) * P:(2 * g + t + 1) * P], wo3[:, a, :],
                                       start=(a == 0), stop=(a == 1), skip_group_check=True)
                mm.then_inc(s_wd3, 1)

        def dve_wo3(dve, p):
            for g in range(4):
                dve.wait_ge(s_wd3, 4 * p + g + 1)
                dst = acc[:, 2 * g:2 * g + 2, :].rearrange("p t d -> p (t d)")
                dve.tensor_tensor(dst, dst, F_PS[g % 2][:, :], ALU.add).then_inc(s_acc, 1)

        def body3(slot, p, first, last):
            for a in range(2):
                for b in range(B):
                    u = 4 * a + b
                    slot(p, a, b, u, first, last, last and u == 7)

        def pe_slot3(pe):
            def slot(p, a, b, u, first, last, end):
                n = 8 * p + u
                if not end:
                    a2, b2 = divmod((u + 1) % 8, 4)
                    head2 = 2 * p + (u + 1) // 4
                    if b2 == 0:
                        pe.wait_ge(s_fe3, 6 * head2 + 4)
                    pe_scores(pe, u3, n + 1, (u + 1) % 2, q3[:, a2, b2 * T:(b2 + 1) * T],
                              k3[:, a2, b2 * T:(b2 + 1) * T], first and u == 0)
                if not (first and u == 0):
                    a0, b0 = divmod((u - 1) % 8, 4)
                    head0 = 2 * p + (u - 1) // 4
                    pe_pv3(pe, n - 1, a0, b0, head0, first and 0 < u <= 4)
                if a == 0 and b == 1 and not first:
                    pe_wo3(pe, p - 1, 6 * (2 * p + 1) + 2)
                if b < 3 and not (last and a == 1):
                    wait_w3(pe, p, a, b)
                    pe_proj3(pe, 2 * p + a + 1, 1 - a, b,
                             acc_before=(4 * p if (a == 0 and b == 1 and not first) else None))
                pe_transpose(pe, u3, n, u % 2, first and u < 2)
            return slot

        def wait_w3(pe, p, a, b):
            if b == 0:
                pe.wait_ge(s_w3[1 - a], 16 * (p + a + 1))

        def pe_pv3(pe, n, a, b, head, nofree):
            if b == 0:
                pe.wait_ge(s_fe3, 6 * head + 6)
            if b % 2 == 0 and not nofree:
                pe.wait_ge(s_oe3, 2 * head + b // 2 - 1)
            o_ps = O_PS[b // 2][:, (b % 2) * T:(b % 2 + 1) * T]
            pe_pv(pe, u3, n, (n_par(b)), o_ps, v3[:, a, 2 * b, :], v3[:, a, 2 * b + 1, :])

        def n_par(b):
            return b % 2

        def act_o3(act, head, a, i):
            act.wait_ge(u3.o, 4 * head + 2 * i + 2)
            act.activation(o3[:, a, i * 512:(i + 1) * 512], O_PS[i][:, :], ACT.Copy).then_inc(s_oe3, 1)

        def act_slot3(act):
            def slot(p, a, b, u, first, last, end):
                n = 8 * p + u
                if not end:
                    act_exp(act, u3, n + 1, (u + 1) % 2, first and u == 0)
                if b == 0 and not (first and a == 0):
                    act_o3(act, 2 * p + a - 1, 1 - a, 1)
                if b == 2:
                    act_o3(act, 2 * p + a, a, 0)
                if b < 3 and not (last and a == 1):
                    act_proj3(act, 2 * p + a + 1, 1 - a, b)
            return slot

        def dve_slot3(dve):
            def slot(p, a, b, u, first, last, end):
                n = 8 * p + u
                if not (first and u == 0):
                    dve_pt(dve, u3, n - 1, (u + 1) % 2, first and u < 3)
                if not end:
                    dve_max(dve, u3, n + 1, (u + 1) % 2)
                    dve_recip(dve, u3, n + 1, (u + 1) % 2)
                if a == 0 and b == 1 and not first:
                    dve_wo3(dve, p - 1)
            return slot

        def pool_slot3(pool):
            def slot(p, a, b, u, first, last, end):
                if not end:
                    pool_normalise(pool, u3, 8 * p + u + 1, (u + 1) % 2)
            return slot

        def run3(eng, slot):
            body3(slot, 0, True, False)
            with eng.Fori(1, PAIRS - 1) as p:
                body3(slot, p, False, False)
            body3(slot, PAIRS - 1, False, True)

        gate = sb("gate", [P, KC, E3])
        sel = sb("sel", [96, NCH * P], BF16)
        lg = sb("lg", [P, NT, E3])
        mx = sb("mx", [P, NT])
        pr = sb("pr", [P, NT, E3])
        top = sb("top", [P, NT, 8])
        left = sb("left", [P, NT, E3])
        wt = sb("wt", [P, NT, 32])
        wsp = sb("wsp", [96, N], BF16)
        wr = sb("wr", [32, N])
        wmid = sb("wmid", [32, N], BF16)
        wm = sb("wm", [P, WSLOTS, 6, P])
        gs, am, yT = (kbd[:, :, :, :].rearrange("p c j t -> p (c j t)")[:, i * 2 * HALF:(i + 1) * 2 * HALF]
                      .rearrange("p (k n) -> p k n", k=2) for i in range(3))
        G_PS, U_PS, WB_PS, Y_PS = bank[0:2], bank[2:4], bank[4:6], bank[6:8]
        SH = NCH * P // 2
        staged = [a[0:96, :, :].rearrange("p a n -> p (a n)")[:, 0:SH] for a in (q3, k3)]
        s_gate = sem("s_gate")
        s_sel = sem("s_sel")
        s_lg = sem("s_lg")
        s_rt = sem("s_rt")
        s_rx = sem("s_rx")
        s_wt = sem("s_wt")
        s_wsp = sem("s_wsp")
        s_wm = [sem(f"s_wm{i}") for i in range(WSLOTS)]
        s_free = sem("s_free")
        s_gup = sem("s_gup")
        s_gs = sem("s_gs")
        s_gm = sem("s_gm")
        s_am = sem("s_am")
        s_yT = sem("s_yT")
        s_yt = sem("s_yt")
        s_fin = sem("s_fin")
        s_xh = sem("s_xh")
        s_out = sem("s_out")
        TURNS = (NCH - 1) // WSLOTS
        assert NCH == TURNS * WSLOTS + 1

        def channels(eng, work, hf):
            base = NCH * hf
            work(hf, 0, base, base, base // WSLOTS + 1)
            with eng.Fori(0, TURNS) as i:
                for r in range(1, WSLOTS + 1):
                    work(hf, WSLOTS * i + r, WSLOTS * i + base + r, base + r, i + (base + r) // WSLOTS + 1)

        def load_work(sp):
            def work(hf, c, u, r, load):
                slot = r % WSLOTS
                sp.wait_ge(s_free, u + 1)
                sp.dma_start(wm[:, slot, :, :].rearrange("p s n -> p (s n)"),
                             moe_in[bass.ds(c, 1)].rearrange("a p n -> (a p) n")).then_inc(s_wm[slot], 16)
            return work

        def pe_gup(pe, hf, c, u, r, load):
            slot, k = r % WSLOTS, r % 2
            pe.wait_ge(s_wm[slot], 16 * load)
            if r:
                pe.wait_ge(s_am, ONE + u - 1)
            for ps, w in ((G_PS[k], 0), (U_PS[k], 2)):
                for q in range(KC):
                    pe.matmul(ps[:, :], wm[:, slot, w + q, :], hT[:, q, hf * HALF:(hf + 1) * HALF],
                              start=(q == 0), stop=(q == KC - 1))
            if r == 0:
                pe.wait_ge(s_wsp, 6)
                pe.wait_ge(s_sel, 34)
            pe.matmul(WB_PS[k][:, :], sel[:, bass.ds(c * P, P)], wsp[:, hf * HALF:(hf + 1) * HALF],
                      start=True, stop=True).then_inc(s_gup, 1)

        def pe_down(pe, u, r):
            pe.wait_ge(s_am, ONE + u + 1)
            for q in range(KC):
                mm = pe.matmul(Y_PS[q][:, :], wm[:, r % WSLOTS, 4 + q, :], am[:, r % 2, :], start=False,
                               stop=False, skip_group_check=True)
            mm.then_inc(s_free, 1)

        def pe_channels(pe, hf):
            if hf:
                pe.wait_ge(s_yT, KC)
                pe.wait_ge(s_fin, 2)
            for q in range(KC):
                pe.matmul(Y_PS[q][:, :], zb[:, 0:P], zb[:, :], start=True, stop=False, skip_group_check=True)

            def work(hf, c, u, r, load):
                pe_gup(pe, hf, c, u, r, load)
                if r != NCH * hf:
                    pe_down(pe, u - 1, r - 1)
            channels(pe, work, hf)
            pe.wait_ge(s_am, ONE + NCH * (hf + 1))
            for q in range(KC):
                mm = pe.matmul(Y_PS[q][:, :], wm[:, (NCH * (hf + 1) - 1) % WSLOTS, 4 + q, :],
                               am[:, (NCH * (hf + 1) - 1) % 2, :], start=False, stop=True, skip_group_check=True)
            mm.then_inc(s_free, 1)
            pe.wait_ge(s_yT, KC * (hf + 1))
            for g in range(2):
                for t in range(2):
                    for q in range(KC):
                        mm = pe.transpose(WB_PS[g][:, t * D + q * P:t * D + (q + 1) * P],
                                          yT[:, q, (2 * g + t) * P:(2 * g + t + 1) * P], ident[:, :])
                mm.then_inc(s_yt, 1)

        def act_channels(act, hf):
            def work(hf, c, u, r, load):
                act.wait_ge(s_gup, u + 1)
                if r:
                    act.wait_ge(s_am, ONE + u - 1)
                act.activation(gs[:, r % 2, :], G_PS[r % 2][:, :], ACT.Silu).then_inc(s_gs, 1)
            channels(act, work, hf)
            act.wait_ge(s_free, WSLOTS + NCH * (hf + 1))
            if hf:
                act.wait_ge(s_yt, 2)
            for q in range(KC):
                act.activation(yT[:, q, :], Y_PS[q][:, :], ACT.Copy).then_inc(s_yT, 1)

        def dve_channels(dve, hf):
            def work(hf, c, u, r, load):
                k = r % 2
                dve.wait_ge(s_gs, u + 1)
                dve.tensor_tensor(gs[:, k, :], gs[:, k, :], U_PS[k][:, :], ALU.mult).then_inc(s_gm, 1)
                dve.wait_ge(s_gm, u + 1)
                if r:
                    dve.wait_ge(s_free, u + WSLOTS - 1)
                dve.tensor_tensor(am[:, k, :], gs[:, k, :], WB_PS[k][:, :], ALU.mult).then_inc(s_am, 1)
            channels(dve, work, hf)
            dve.wait_ge(s_xh, 1)
            for g in range(2):
                dve.wait_ge(s_yt, 2 * hf + g + 1)
                xs = x[:, 4 * hf + 2 * g:4 * hf + 2 * g + 2, :].rearrange("p t d -> p (t d)")
                dve.tensor_tensor(xs, xs, WB_PS[g][:, :], ALU.add).then_inc(s_fin, 1)

        def pe_routing(pe):
            pe.wait_ge(s_gate, 16)
            pe.wait_ge(n4.hT, 4)
            for t in range(NT):
                for q in range(KC):
                    mm = pe.matmul(WB_PS[0][:, t * E3:(t + 1) * E3], hT[:, q, t * P:(t + 1) * P], gate[:, q, :],
                                   start=(q == 0), stop=(q == KC - 1), skip_group_check=True)
            mm.then_inc(s_lg, 1)

        def pe_routing_transposes(pe):
            pe.wait_ge(s_rt, ROUTED)
            for t in range(NT):
                mm = pe.transpose(WB_PS[t // 4][0:32, (t % 4) * P:(t % 4 + 1) * P], wt[:, t, :], ident[:, :])
            mm.then_inc(s_wt, 1)

        ROUTED = 5 + NT + 1 + NT + 4

        def dve_routing(dve):
            steps = [0]

            def step(ins):
                steps[0] += 1
                ins.then_inc(s_rt, 1)
                dve.wait_ge(s_rt, steps[0])

            def wide(a):
                return a.unsqueeze(2).to_broadcast([P, NT, E3])

            logits = WB_PS[0][:, 0:NT * E3].rearrange("p (t e) -> p t e", e=E3)
            dve.wait_ge(s_lg, 1)
            step(dve.tensor_reduce(mx[:, :], logits, AX.X, ALU.max))
            step(dve.tensor_tensor(lg[:, :, :], logits, wide(mx[:, :]), ALU.subtract))
            dve.wait_ge(s_rx, 1)
            step(dve.tensor_reduce(mx[:, :], pr[:, :, :], AX.X, ALU.add))
            step(dve.reciprocal(mx[:, :], mx[:, :]))
            step(dve.tensor_tensor(pr[:, :, :], pr[:, :, :], wide(mx[:, :]), ALU.mult))
            for t in range(NT):
                step(dve.max(top[:, t, :], pr[:, t, :]))
            step(dve.memset(top[:, :, TOPK:8], -2.0))
            for t in range(NT):
                step(dve.match_replace(left[:, t, :], top[:, t, :], pr[:, t, :], -1.0))
            step(dve.scalar_tensor_tensor(wt[:, :, 0:E3], left[:, :, :], 0.0, pr[:, :, :], ALU.is_lt, ALU.mult))
            step(dve.tensor_reduce(mx[:, :], wt[:, :, 0:E3], AX.X, ALU.add))
            step(dve.reciprocal(mx[:, :], mx[:, :]))
            step(dve.tensor_tensor(wt[:, :, 0:E3], wt[:, :, 0:E3], wide(mx[:, :]), ALU.mult))
            dve.wait_ge(s_wt, 1)
            for g in range(2):
                cols = slice(g * 512, (g + 1) * 512)
                step(dve.tensor_copy(wsp[0:32, cols], WB_PS[g][0:32, :]))
                step(dve.tensor_tensor(wr[:, cols], WB_PS[g][0:32, :], wsp[0:32, cols], ALU.subtract))
            step(dve.tensor_copy(wmid[:, :], wr[:, :]))
            dve.tensor_copy(wsp[32:64, :], wmid[:, :]).then_inc(s_wsp, 3)
            step(dve.tensor_tensor(wr[:, :], wr[:, :], wmid[:, :], ALU.subtract))
            dve.tensor_copy(wsp[64:96, :], wr[:, :]).then_inc(s_wsp, 3)

        @block.sync
        def _(sp):
            for t in range(4):
                sp.dma_start(x[:, 2 * t:2 * t + 2, :],
                             x_in[t * 256:(t + 1) * 256, :].rearrange("(t p) d -> p t d", p=P)).then_inc(s_x, 16)
            for dst, src in ((ident, ident_in), (tri, tri_in), (headmask, headmask_in), (vec, vec_in)):
                sp.dma_start(dst[:, :], src).then_inc(s_const, 16)
            sp.dma_start(bo[:, :], bo_in.partition_broadcast(P)).then_inc(s_const, 16)
            for dst, src in ((wq, wqT_in), (wk, wkT_in), (wv, wvT_in), (wo, woT_in)):
                sp.dma_start(dst[:, :, :], src.rearrange("(q p) n -> p q n", p=P)).then_inc(s_w1, 16)
            sp.dma_start(tid[:, :], tok_in.partition_broadcast(P)).then_inc(s_tid, 16)
            sp.dma_start(ctxT[:, :, :, :].rearrange("p e q n -> p (e q) n"),
                         ctxT_in.rearrange("(g p) n -> p g n", p=P)).then_inc(s_ctx, 16)
            sp.dma_start(gate[:, :, :], gate_in.rearrange("(q p) n -> p q n", p=P)).then_inc(s_gate, 16)
            for a in range(2):
                sp.dma_start(w3[:, a, :, :, :].rearrange("p s q n -> p (s q n)"), ffn_qkv_in[a]).then_inc(s_w3[a], 16)
            sp.dma_start(wo3[:, :, :], ffn_o_in[0]).then_inc(s_wo3, 16)
            with sp.Fori(0, PAIRS - 1) as p:
                for a in range(2):
                    sp.wait_ge(s_f3, 6 * (2 * p + a + 1))
                    sp.dma_start(w3[:, a, :, :, :].rearrange("p s q n -> p (s q n)"),
                                 ffn_qkv_in[bass.ds(2 * p + 2 + a, 1)].rearrange("a p n -> (a p) n"))\
                      .then_inc(s_w3[a], 16)
                sp.wait_ge(s_wd3, 4 * p + 4)
                sp.dma_start(wo3[:, :, :].rearrange("p a n -> p (a n)"),
                             ffn_o_in[bass.ds(p + 1, 1)].rearrange("a p b n -> (a p) (b n)")).then_inc(s_wo3, 16)
            for hf in range(2):
                channels(sp, load_work(sp), hf)
            for g in range(4):
                sp.wait_ge(s_fin, g + 1)
                sp.dma_start(out[g * 256:(g + 1) * 256, :].rearrange("(t p) d -> p t d", p=P),
                             x[:, 2 * g:2 * g + 2, :]).then_inc(s_out, 16)
            sp.wait_ge(s_out, 64)

        @block.gpsimd
        def _(pool):
            pool.memset(pw[:, :], -0.5).then_inc(s_init, 1)
            pool.memset(vbd[:, :, :, :], 0.0).then_inc(s_init, 1)
            pool.wait_ge(s_init, 1)
            ln_gpsimd(pool, n1)
            pool.memset(zb[:, :], 0.0).then_inc(s_init, 1)
            for i, s in enumerate((s_wo1, s_zz, s_gu, s_y, s_x2, s_am)):
                pool.memset(credit[:, i:i + 1], 0.0).then_inc(s, ONE)
            for i in range(WSLOTS):
                pool.memset(wt[:, 2 * i:2 * i + 2, :], 0.0).then_inc(s_free, 1)
            pool.wait_ge(s_free, WSLOTS)
            pool.memset(wt[:, :, E3:E3 + 1], 1.0).then_inc(s_init, 1)
            pool.wait_ge(s_const, 16 * 5)
            pool.wait_ge(n1.h, NT)
            pool.tensor_tensor(x[:, :, :], x[:, :, :], bo[:, :].unsqueeze(1).to_broadcast([P, NT, D]),
                               ALU.add).then_inc(s_bo, 1)
            pool_normalise(pool, u1, 0, 0)
            run1(pool, pool_slot1(pool))
            ln_gpsimd(pool, n2)
            ln_gpsimd(pool, n3)
            rms_gpsimd(pool, n3r)
            pool_normalise(pool, u3, 0, 0)
            run3(pool, pool_slot3(pool))
            rms_gpsimd(pool, n4)
            pool.tensor_tensor(x[:, :, :], x[:, :, :], acc[:, :, :], ALU.add).then_inc(s_xh, 1)

        @block.scalar
        def _(act):
            for i in range(2):
                act.dma_start(staged[i], sel_in[:, i * SH:(i + 1) * SH]).then_inc(s_sel, 16)
            act.wait_ge(s_const, 16 * 5)
            act.activation(bqs[:, :], vec[:, 0:2], ACT.Copy, scale=float(HD1) ** -0.5).then_inc(s_castc, 1)
            act.wait_ge(s_castc, 3)
            hT_scalar(act, n1)
            act.wait_ge(s_init, 2)
            act_q1(act, 0, 0)
            act_v1(act, 0, 0)
            act_exp(act, u1, 0, 0, True)
            run1(act, act_slot1(act))
            act_o1(act, CH * HC * B, CH - 1, B - 1)
            hT_scalar(act, n2)
            act_experts(act)
            rms_scalar(act, n3r, acc, n3)
            hT_scalar(act, n3r, weight=6)
            for part in range(3):
                act_proj3(act, 0, 0, part)
            act_exp(act, u3, 0, 0, True)
            run3(act, act_slot3(act))
            act_o3(act, H3 - 1, 1, 1)
            act.wait_ge(s_acc, 4 * PAIRS)
            rms_scalar(act, n4, acc)
            hT_scalar(act, n4, weight=8)
            act.wait_ge(s_rt, 2)
            act.activation(pr[:, :, :], lg[:, :, :], ACT.Exp).then_inc(s_rx, 1)
            for hf in range(2):
                act_channels(act, hf)

        @block.tensor
        def _(pe):
            pe.wait_ge(s_castc, 3)
            transposes(pe, n1, h)
            pe.wait_ge(s_w1, 64)
            pe.wait_ge(n1.hT, 4)
            pe_qkv1(pe, 0, 0, 0, first=True)
            pe_s1(pe, 0, 0, 0, 0, 0, True)
            run1(pe, pe_slot1(pe))
            pe_pv1(pe, CH * HC * B - 1, CH * HC - 1, CH * B - 1, CH - 1, HC - 1, False)
            pe_wo1(pe, B - 1, 4 * B)
            transposes(pe, n2, h)
            pe_experts(pe)
            transposes(pe, n3r, h)
            pe.wait_ge(s_w3[0], 16)
            pe.wait_ge(n3r.hT, 4)
            for part in range(3):
                pe_proj3(pe, 0, 0, part)
            pe.wait_ge(s_fe3, 4)
            pe_scores(pe, u3, 0, 0, q3[:, 0, 0:T], k3[:, 0, 0:T], True)
            run3(pe, pe_slot3(pe))
            pe_pv3(pe, 4 * H3 - 1, 1, 3, H3 - 1, False)
            pe_wo3(pe, PAIRS - 1, 6 * H3)
            transposes(pe, n4, h)
            pe_routing(pe)
            pe_routing_transposes(pe)
            for hf in range(2):
                pe_channels(pe, hf)

        @block.vector
        def _(dve):
            dve.wait_ge(s_x, 64)
            ln_vector(dve, n1, x, h)
            dve.wait_ge(s_const, 16 * 5)
            dve.tensor_copy(identb[:, :], ident[:, :]).then_inc(s_castc, 1)
            dve.tensor_copy(trib[:, :], tri[:, :]).then_inc(s_castc, 1)
            dve.wait_ge(n1.hT, 4)
            dve_hb(dve, 0)
            dve_kbd(dve, 0, 0)
            dve_max(dve, u1, 0, 0)
            dve_recip(dve, u1, 0, 0)
            dve_onehot(dve)
            dve.wait_ge(s_sel, 32)
            for i in range(2):
                dve.tensor_copy(sel[:, i * SH:(i + 1) * SH], staged[i]).then_inc(s_sel, 1)
            run1(dve, dve_slot1(dve))
            dve_pt(dve, u1, CH * HC * B - 1, 1, False)
            dve_x1(dve, B - 1)
            dve.wait_ge(s_x1, B)
            ln_vector(dve, n2, x, h)
            dve_experts(dve)
            dve.wait_ge(s_x2, ONE + NT)
            ln_vector(dve, n3, x, acc)
            rms_vector(dve, n3r, acc, h)
            dve_max(dve, u3, 0, 0)
            dve_recip(dve, u3, 0, 0)
            run3(dve, dve_slot3(dve))
            dve_pt(dve, u3, 4 * H3 - 1, 1, False)
            dve_wo3(dve, PAIRS - 1)
            rms_vector(dve, n4, acc, h)
            dve_routing(dve)
            for hf in range(2):
                dve_channels(dve, hf)


def _constants():
    import numpy as np

    ident = np.eye(P, dtype=np.float32)
    tri = np.where(np.arange(P)[None, :] <= np.arange(P)[:, None], 0.0, MASKED).astype(np.float32)
    headmask = (np.arange(P)[:, None] // HD1 == np.arange(HC)[None, :]).astype(np.float32)
    channel = np.arange(NCH * P)
    row = np.where(channel < E3 * INNER, channel // INNER, E3)
    sel = np.zeros((3, 32, NCH * P), np.float32)
    sel[:, row[:CHANNELS], channel[:CHANNELS]] = 1.0
    return {"ident": ident, "tri": tri, "headmask": headmask, "sel": sel.reshape(96, NCH * P)}


def _layout(i):
    import numpy as np

    a = {k: np.asarray(v) for k, v in i.items()}
    f = {k[len("L0_ffn_"):]: v for k, v in a.items() if k.startswith("L0_ffn_")}

    def chunks(w):
        return w.T.reshape(KC, P, -1).transpose(1, 0, 2)

    q = f["q_w"].reshape(H3, QHD, D)[:, :HD3]
    kv = f["kv_w"]
    k = kv[:H3 * HD3].reshape(H3, HD3, D)
    v = kv[H3 * HD3:2 * H3 * HD3].reshape(H3, HD3, D)
    qkv = np.stack([np.stack([chunks(s[n]) for s in (q, k, v)], 1).reshape(P, -1) for n in range(H3)])
    o = f["o_w"].T.reshape(PAIRS, 2, HD3, D).transpose(0, 2, 1, 3)

    def padded(w):
        out = np.zeros((NCH * P, D), np.float32)
        out[:CHANNELS] = w
        return out

    g = padded(np.concatenate([f["w1"][:, :INNER].reshape(-1, D), f["sh_gu_w"][:SHARED]]))
    u = padded(np.concatenate([f["w1"][:, INNER:].reshape(-1, D), f["sh_gu_w"][SHARED:]]))
    d = padded(np.concatenate([f["w2"].transpose(0, 2, 1).reshape(-1, D), f["sh_down_w"].T]))
    moe = np.stack([np.concatenate([chunks(g[c * P:(c + 1) * P]).reshape(P, -1),
                                    chunks(u[c * P:(c + 1) * P]).reshape(P, -1),
                                    d[c * P:(c + 1) * P]], 1) for c in range(NCH)])
    vec = np.stack([a[n].reshape(KC, P)[c] for n in ("L0_attn_bq", "L0_attn_bk", "L0_attn_bv", "L0_ffn_ln1_w",
                                                     "L0_ffn_ln2_w") for c in range(KC)], 1)
    con = _constants()
    return [a["x"].reshape(N, D), a["itok_BxS_13_99985"].reshape(N),
            a["ctx_2048"].transpose(0, 2, 1).reshape(XE * D, D),
            a["L0_attn_Wq"], a["L0_attn_Wk"], a["L0_attn_Wv"], a["L0_attn_Wo"], vec, a["L0_attn_bo"], qkv, o,
            f["gate_w"].T, moe, con["ident"], con["tri"], con["headmask"], con["sel"]]


def kernel(**inputs):
    import numpy as np
    import concourse.bacc as bacc
    from concourse.bass_utils import run_bass_kernel_spmd

    nc = bacc.Bacc("TRN2", target_bir_lowering=False, num_devices=1)
    arrays, args = {}, []
    for n, v in enumerate(_layout(inputs)):
        name = f"in_{n}"
        arrays[name] = np.ascontiguousarray(v)
        args.append(nc.dram_tensor(name, arrays[name].shape, mybir.dt.from_np(arrays[name].dtype),
                                   kind="ExternalInput").ap())
    out = nc.dram_tensor("out", (N, D), F32, kind="ExternalOutput").ap()
    decoder_kernel(nc, *args, out)
    r = run_bass_kernel_spmd(nc, [arrays], core_ids=[0])
    return r.results[0]["out"].reshape(B, T, D)
```

```python
from contextlib import ExitStack

import concourse.bass as bass
from concourse import mybir

F32 = mybir.dt.float32
F32R = mybir.dt.float32r
BF16 = mybir.dt.bfloat16
I32 = mybir.dt.int32
ALU = mybir.AluOpType
ACT = mybir.ActivationFunctionType
AX = mybir.AxisListType

P = 128
B, T, D = 4, 256, 256
N = B * T
NT = N // P
KC = D // P
LN_EPS, RMS_EPS = 1e-5, 1e-6
H1, HD1 = 16, 16
HC = P // HD1
CH = H1 // HC
VP = HC * (P + HD1)
XE, VOCAB = 4, 12500
PER_EXPERT = VOCAB // XE
XB = 256
H3, HD3, QHD = 16, 128, 192
PAIRS = H3 // 2
E3, INNER, SHARED, TOPK = 16, 176, 352, 4
CHANNELS = E3 * INNER + SHARED
NCH = -(-CHANNELS // P)
HALF = 512
WSLOTS = 2
GROUP = 16
MASKED = -1.0e30


def decoder_kernel(nc, x_in, tok_in, ctxT_in, wqT_in, wkT_in, wvT_in, woT_in, vec_in, bo_in, ffn_qkv_in, ffn_o_in,
                   gate_in, moe_in, ident_in, tri_in, headmask_in, out):
    with ExitStack() as ctx:
        def sb(name, shape, dt=F32):
            return ctx.enter_context(nc.sbuf_tensor(name, shape, dt))

        def sem(name):
            return ctx.enter_context(nc.semaphore(name))

        shared = ExitStack()

        def tmp(name, shape, dt=F32):
            return shared.enter_context(nc.sbuf_tensor(name, shape, dt))

        bank = [ctx.enter_context(nc.psum_tensor(f"bank{i}", [P, 512], F32)) for i in range(8)]
        S_PS, PT_PS, O_PS, F_PS = bank[0:2], bank[2:4], bank[4:6], bank[6:8]

        ident = sb("ident", [P, P])
        identb = sb("identb", [P, P], BF16)
        tri = sb("tri", [P, P])
        trib = sb("trib", [P, 2, P], BF16)
        headmask = sb("headmask", [P, HC])
        vec = sb("vec", [P, 10])
        bqs = sb("bqs", [P, 2])
        bo = sb("bo", [P, D])
        pw = sb("pw", [P, NT])
        zb = sb("zb", [P, 512], BF16)
        x = sb("x", [P, NT, D])
        h = sb("h", [P, NT, D])
        acc = sb("acc", [P, NT, D])
        hT = sb("hT", [P, KC, N])
        hTh = sb("hTh", [P, KC, N], F32R)
        hTl = sb("hTl", [P, KC, N], F32R)
        st = sb("st", [P, NT, 6])
        mv = sb("mv", [P, NT, 2])
        ve = sb("ve", [P, NT])
        rstd = sb("rstd", [P, NT])
        ss = sb("ss", [P, NT])
        sq = sb("sq", [P, D])
        p_sb = sb("p_sb", [P, 2, 384])
        pt_sb = sb("pt_sb", [P, 2, 384])
        nmax = sb("nmax", [P, 2, 2])
        psum_ = sb("psum_", [P, 2, 2])
        prec = sb("prec", [P, 2, 2])

        ctxT = sb("ctxT", [P, XE, KC, D])
        tid = sb("tid", [P, N], I32)
        onehot = sb("onehot", [P, XE, N])
        w3 = sb("w3", [P, 2, 3, KC, HD3])
        wo3 = sb("wo3", [P, 2, D])
        gate = sb("gate", [P, KC, E3])
        wt = sb("wt", [P, NT, 32])
        wm = sb("wm", [P, WSLOTS, 6, P])

        s_const = sem("s_const")
        s_castc = sem("s_castc")
        s_init = sem("s_init")
        ONE, AM0, DN0 = 1, 3, 2
        credit = sb("credit", [P, 7])

        block = ctx.enter_context(nc.Block())

        class Norm:

            def __init__(self, tag):
                self.stat = sem(f"{tag}_stat")
                self.var = sem(f"{tag}_var")
                self.h = sem(f"{tag}_h")
                self.tr = sem(f"{tag}_tr")
                self.hT = sem(f"{tag}_hT")
                self.hh = sem(f"{tag}_hh")
                self.hl = sem(f"{tag}_hl")

        n1, n2, n3, n3r, n4 = Norm("n1"), Norm("n2"), Norm("n3"), Norm("n3r"), Norm("n4")

        def ln_vector(dve, s, src, dst):
            for t in range(NT):
                dve.bn_stats(st[:, t, :], src[:, t, :]).then_inc(s.stat, 1)
            for t in range(NT):
                dve.wait_ge(s.stat, t + 1)
                dve.bn_aggr(mv[:, t, :], st[:, t, :]).then_inc(s.stat, 1)
            dve.wait_ge(s.var, 2)
            for t in range(NT):
                dve.tensor_scalar(dst[:, t, :], src[:, t, :], mv[:, t, 0:1], rstd[:, t:t + 1],
                                  ALU.subtract, ALU.mult).then_inc(s.h, 1)

        def ln_gpsimd(pool, s):
            pool.wait_ge(s.stat, 2 * NT)
            pool.tensor_scalar(ve[:, :], mv[:, :, 1], LN_EPS, 1.0, ALU.add, ALU.mult).then_inc(s.var, 1)
            pool.wait_ge(s.var, 1)
            pool.tensor_tensor(rstd[:, :], ve[:, :], pw[:, :], ALU.pow).then_inc(s.var, 1)

        def rms_scalar(act, s, src, made=None):
            for t in range(NT):
                if made is not None:
                    act.wait_ge(made.h, t + 1)
                if t:
                    act.wait_ge(s.stat, t)
                act.activation(sq[:, :], src[:, t, :], ACT.Square, accum_out=ss[:, t:t + 1]).then_inc(s.stat, 1)

        def rms_gpsimd(pool, s):
            pool.wait_ge(s.stat, NT)
            pool.tensor_scalar(ve[:, :], ss[:, :], 1.0 / D, RMS_EPS, ALU.mult, ALU.add).then_inc(s.var, 1)
            pool.wait_ge(s.var, 1)
            pool.tensor_tensor(rstd[:, :], ve[:, :], pw[:, :], ALU.pow).then_inc(s.var, 1)

        def rms_vector(dve, s, src, dst):
            dve.wait_ge(s.var, 2)
            for t in range(NT):
                dve.tensor_scalar(dst[:, t, :], src[:, t, :], rstd[:, t:t + 1], None, ALU.mult).then_inc(s.h, 1)

        def transposes(pe, s, src, base=0):
            for g in range(2):
                for c in range(KC):
                    for j in range(4):
                        pe.wait_ge(s.h, 4 * g + j + 1)
                        mm = pe.transpose(bank[4 + 2 * g + c][:, j * P:(j + 1) * P],
                                          src[:, 4 * g + j, c * P:(c + 1) * P], ident[:, :])
                    mm.then_inc(s.tr, 1)

        def hT_scalar(act, s, weight=None, split=False):
            for g in range(2):
                for c in range(KC):
                    act.wait_ge(s.tr, 2 * g + c + 1)
                    cols = slice(g * 512, (g + 1) * 512)
                    ps = bank[4 + 2 * g + c][:, :]
                    scale = 1.0 if weight is None else vec[:, weight + c:weight + c + 1]
                    act.activation(hT[:, c, cols], ps, ACT.Copy, scale=scale).then_inc(s.hT, 1)
                    if split:
                        act.activation(hTh[:, c, cols], ps, ACT.Copy, scale=scale).then_inc(s.hh, 1)

        def hT_vector(dve, s):
            for g in range(2):
                for c in range(KC):
                    dve.wait_ge(s.hh, 2 * g + c + 1)
                    cols = slice(g * 512, (g + 1) * 512)
                    dve.tensor_tensor(hTl[:, c, cols], hT[:, c, cols], hTh[:, c, cols].bitcast(F32),
                                      ALU.subtract).then_inc(s.hl, 1)

        def matmul3(pe, out, lhs, rhs, start, stop, check=False):
            for i, (a, b) in enumerate(((0, 0), (0, 1), (1, 0))):
                mm = pe.matmul(out, lhs[a], rhs[b], start=(start and i == 0), stop=(stop and i == 2),
                               skip_group_check=check)
            return mm

        class Unit:
            def __init__(self, tag):
                self.s = sem(f"{tag}_s")
                self.nm = sem(f"{tag}_nm")
                self.ex = sem(f"{tag}_ex")
                self.rs = sem(f"{tag}_rs")
                self.pn = sem(f"{tag}_pn")
                self.t = sem(f"{tag}_t")
                self.pt = sem(f"{tag}_pt")
                self.o = sem(f"{tag}_o")

        def pe_scores(pe, u, n, k, qT, keys, first):
            if not first:
                pe.wait_ge(u.ex, 2 * (n - 1))
            s_ps = S_PS[k]
            pe.matmul(s_ps[:, 0:256], qT[:, P:2 * P], keys, start=True, stop=False, skip_group_check=True)
            pe.matmul(s_ps[:, 256:384], qT[:, 0:P], keys[:, 0:P], start=False, stop=False, skip_group_check=True)
            pe.matmul(s_ps[:, 128:384], identb[:, :], trib[:, :, :].rearrange("p a k -> p (a k)"), start=False,
                      stop=True, skip_group_check=True).then_inc(u.s, 1)

        def dve_max(dve, u, n, k):
            dve.wait_ge(u.s, n + 1)
            dve.tensor_reduce(nmax[:, k, 0:1], S_PS[k][:, 0:256], AX.X, ALU.max, negate=True).then_inc(u.nm, 1)
            dve.tensor_reduce(nmax[:, k, 1:2], S_PS[k][:, 256:384], AX.X, ALU.max, negate=True).then_inc(u.nm, 1)

        def act_exp(act, u, n, k, first, sums=None):
            sums = sums or (psum_[:, k, 0:1], psum_[:, k, 1:2])
            act.wait_ge(u.nm, 2 * n + 2)
            if not first:
                act.wait_ge(u.t, n - 1)
            act.activation(p_sb[:, k, 0:256], S_PS[k][:, 0:256], ACT.Exp, bias=nmax[:, k, 0:1],
                           accum_out=sums[0]).then_inc(u.ex, 1)
            act.activation(p_sb[:, k, 256:384], S_PS[k][:, 256:384], ACT.Exp, bias=nmax[:, k, 1:2],
                           accum_out=sums[1]).then_inc(u.ex, 1)

        def dve_recip(dve, u, n, k):
            dve.wait_ge(u.ex, 2 * n + 2)
            dve.reciprocal(prec[:, k, :], psum_[:, k, :]).then_inc(u.rs, 1)

        def pool_normalise(pool, u, n, k):
            pool.wait_ge(u.rs, n + 1)
            for cols, r in ((slice(0, 256), prec[:, k, 0:1]), (slice(256, 384), prec[:, k, 1:2])):
                p = p_sb[:, k, cols]
                pool.tensor_tensor(p, p, r.to_broadcast(p.shape), ALU.mult).then_inc(u.pn, 1)

        def pe_transpose(pe, u, n, k, first, normalised=True):
            if normalised:
                pe.wait_ge(u.pn, 2 * n + 2)
            else:
                pe.wait_ge(u.ex, 2 * n + 2)
            if not first:
                pe.wait_ge(u.pt, 2 * (n - 1))
            pe.transpose(PT_PS[k][:, 0:128], p_sb[:, k, 256:384], ident[:, :])
            pe.transpose(PT_PS[k][:, 128:256], p_sb[:, k, 0:128], ident[:, :])
            pe.transpose(PT_PS[k][:, 256:384], p_sb[:, k, 128:256], ident[:, :]).then_inc(u.t, 1)

        def dve_pt(dve, u, n, k, first):
            dve.wait_ge(u.t, n + 1)
            if not first:
                dve.wait_ge(u.o, n - 1)
            for cols in (slice(0, 256), slice(256, 384)):
                dve.tensor_copy(pt_sb[:, k, cols], PT_PS[k][:, cols]).then_inc(u.pt, 1)

        def pe_pv(pe, u, n, k, o_ps, v0, v1):
            pe.wait_ge(u.pt, 2 * n + 1)
            pe.matmul(o_ps[:, 0:256], v0, pt_sb[:, k, 0:256], start=True, stop=False, skip_group_check=True)
            pe.wait_ge(u.pt, 2 * n + 2)
            pe.matmul(o_ps[:, 128:256], v1, pt_sb[:, k, 256:384], start=False, stop=True,
                      skip_group_check=True).then_inc(u.o, 1)

        wq = tmp("wq", [P, KC, D])
        wk = tmp("wk", [P, KC, D])
        wv = tmp("wv", [P, KC, D])
        wo = tmp("wo", [P, KC, D])
        hb = tmp("hb", [P, KC, T])
        q1 = tmp("q1", [P, CH, T])
        k1 = tmp("k1", [P, T])
        kbd = tmp("kbd", [P, CH, HC, T])
        vbd = tmp("vbd", [P, CH, 2, VP])
        sums1 = tmp("sums1", [P, CH, 2, HC])
        rec1 = tmp("rec1", [P, CH, 2, HC])
        on1 = tmp("on1", [P, CH, 2, P])
        o1 = tmp("o1", [P, CH, T])

        u1 = Unit("u1")
        s_x = sem("s_x")
        s_w1 = sem("s_w1")
        s_hb = sem("s_hb")
        s_qk1 = sem("s_qk1")
        s_v1 = sem("s_v1")
        s_qe1 = sem("s_qe1")
        s_kbd = sem("s_kbd")
        s_ve1 = sem("s_ve1")
        s_rc1 = sem("s_rc1")
        s_on1 = sem("s_on1")
        s_ot1 = sem("s_ot1")
        s_oe1 = sem("s_oe1")
        s_wo1 = sem("s_wo1")
        s_x1 = sem("s_x1")
        s_bo = sem("s_bo")

        def body1(eng_part, b, first, last):
            for c in range(CH):
                m = CH * b + c
                for j in range(HC):
                    n = (CH * HC) * b + HC * c + j
                    i = HC * c + j
                    end = last and i == CH * HC - 1
                    eng_part(b, m, c, j, n, i % 2, i, first, last, end)

        def pe_qkv1(pe, b, m, c, first=False, x1_before=None):
            cols = slice(c * P, (c + 1) * P)
            if not first:
                pe.wait_ge(s_qe1, 2 * m)
            for q in range(KC):
                pe.matmul(F_PS[0][:, 0:T], wq[:, q, cols], hT[:, q, bass.ds(b * T, T)], start=(q == 0),
                          stop=(q == KC - 1), skip_group_check=True)
            for q in range(KC):
                mm = pe.matmul(F_PS[0][:, T:2 * T], wk[:, q, cols], hT[:, q, bass.ds(b * T, T)], start=(q == 0),
                               stop=(q == KC - 1), skip_group_check=True)
            mm.then_inc(s_qk1, 1)
            pe.wait_ge(s_hb, b + 1)
            if not first:
                pe.wait_ge(s_ve1, 2 * m)
            if x1_before is not None:
                pe.wait_ge(s_x1, x1_before)
            for t in range(2):
                for q in range(KC):
                    mm = pe.matmul(F_PS[1][:, t * P:(t + 1) * P], hb[:, q, t * P:(t + 1) * P], wv[:, q, cols],
                                   start=(q == 0), stop=(q == KC - 1), skip_group_check=True)
            mm.then_inc(s_v1, 1)

        def pe_wo1(pe, b, ve_before):
            pe.wait_ge(s_oe1, 2 * b + 2)
            pe.wait_ge(s_ve1, ve_before)
            for t in range(2):
                for c in range(CH):
                    mm = pe.matmul(F_PS[1][:, t * D:(t + 1) * D], o1[:, c, t * P:(t + 1) * P], wo[:, c, :],
                                   start=(c == 0), stop=(c == CH - 1), skip_group_check=True)
            mm.then_inc(s_wo1, 1)

        def pe_s1(pe, n, i, m, c, j, first):
            if j == 0:
                pe.wait_ge(s_kbd, m + 1)
            pe_scores(pe, u1, n, i % 2, q1[:, c, :], kbd[:, c, j, :], first)

        def pe_pv1(pe, n, i, m, c, j, nofree):
            if j == 0:
                pe.wait_ge(s_ve1, 2 * m + 2)
                if not nofree:
                    pe.wait_ge(s_oe1, m - 1)
            pe.wait_ge(u1.pt, 2 * n + 1)
            pt, out0, out1 = pt_sb[:, i % 2, :], O_PS[c][:, 0:P], O_PS[c][:, P:2 * P]
            va, vb = vbd[:, c, 0, j * P:(j + 1) * P], vbd[:, c, 1, j * P:(j + 1) * P]
            stop = j == HC - 1
            pe.matmul(out0, pt[:, 0:128], va, start=(j == 0), stop=stop, skip_group_check=True)
            pe.matmul(out1, pt[:, 128:256], va, start=False, stop=False, skip_group_check=True)
            pe.wait_ge(u1.pt, 2 * n + 2)
            pe.matmul(out1, pt[:, 256:384], vb, start=False, stop=stop, skip_group_check=True).then_inc(u1.o, 1)

        def pe_ot1(pe, m, c):
            pe.wait_ge(s_on1, m + 1)
            for t in range(2):
                mm = pe.transpose(O_PS[c][:, 2 * P + t * P:2 * P + (t + 1) * P], on1[:, c, t, :], ident[:, :])
            mm.then_inc(s_ot1, 1)

        def pe_slot1(pe):
            def slot(b, m, c, j, n, k, i, first, last, end):
                if not end:
                    i2 = (i + 1) % (CH * HC)
                    c2, j2 = divmod(i2, HC)
                    pe_s1(pe, n + 1, i2, (m + 1) if j == HC - 1 else m, c2, j2, first and i == 0)
                if not (first and i == 0):
                    i0 = (i - 1) % (CH * HC)
                    c0, j0 = divmod(i0, HC)
                    pe_pv1(pe, n - 1, i0, (m - 1) if j == 0 else m, c0, j0, first)
                if j == 1 and not (last and c == CH - 1):
                    pe_qkv1(pe, b if c == 0 else b + 1, m + 1, 1 - c,
                            x1_before=b if (c == 1 and not first) else None)
                if j == 2 and not (first and c == 0):
                    pe_ot1(pe, m - 1, 1 - c)
                if j == 5 and c == 0 and not first:
                    pe_wo1(pe, b - 1, 4 * b + 4)
                pe_transpose(pe, u1, n, k, first and i < 2, normalised=False)
            return slot

        def act_q1(act, m, c):
            act.wait_ge(s_qk1, m + 1)
            act.activation(q1[:, c, :], F_PS[0][:, 0:T], ACT.Identity, bias=bqs[:, c:c + 1],
                           scale=float(HD1) ** -0.5).then_inc(s_qe1, 1)
            if not (isinstance(m, int) and m == 0):
                act.wait_ge(s_kbd, m)
            act.activation(k1[:, :], F_PS[0][:, T:2 * T], ACT.Identity, bias=vec[:, 2 + c:3 + c]).then_inc(s_qe1, 1)

        def act_v1(act, m, c):
            act.wait_ge(s_v1, m + 1)
            for t in range(2):
                dst = vbd[:, c, t, :].rearrange("p (j y) -> p j y", y=P + HD1)[:, :, 0:HD1]
                act.activation(dst, F_PS[1][:, t * P:(t + 1) * P].rearrange("p (j d) -> p j d", d=HD1),
                               ACT.Copy).then_inc(s_ve1, 1)

        def act_exp1(act, n, k, c, j, first):
            act_exp(act, u1, n, k, first, sums=(sums1[:, c, 1, j:j + 1], sums1[:, c, 0, j:j + 1]))

        def act_o1(act, m, c, projected):
            act.wait_ge(s_ot1, m + 1)
            if projected is not None:
                act.wait_ge(s_wo1, ONE + projected)
            act.activation(o1[:, c, :], O_PS[c][:, T:2 * T], ACT.Identity, bias=vec[:, 4 + c:5 + c]).then_inc(s_oe1, 1)

        def act_slot1(act):
            def slot(b, m, c, j, n, k, i, first, last, end):
                if not end:
                    c2, j2 = divmod((i + 1) % (CH * HC), HC)
                    act_exp1(act, n + 1, 1 - k, c2, j2, first and i == 0)
                if j == 2 and not (last and c == CH - 1):
                    act_q1(act, m + 1, 1 - c)
                if j == 3 and not (last and c == CH - 1):
                    act_v1(act, m + 1, 1 - c)
                if j == 3 and not (first and c == 0):
                    act_o1(act, m - 1, 1 - c, None if first else (b if c == 1 else b - 1))
            return slot

        def make_kbd(eng, m, c):
            eng.wait_ge(s_qe1, 2 * m + 2)
            eng.tensor_tensor(kbd[:, c, :, :], k1[:, :].unsqueeze(1).to_broadcast([P, HC, T]),
                              headmask[:, :].unsqueeze(2).to_broadcast([P, HC, T]), ALU.mult).then_inc(s_kbd, 1)

        def dve_hb(dve, b):
            dve.tensor_copy(hb[:, :, :], hT[:, :, bass.ds(b * T, T)]).then_inc(s_hb, 1)

        def dve_on1(dve, m, n_done, c):
            dve.wait_ge(u1.ex, 2 * n_done)
            dve.reciprocal(rec1[:, c, :, :], sums1[:, c, :, :]).then_inc(s_rc1, 1)
            dve.wait_ge(s_rc1, m + 1)
            dve.wait_ge(u1.o, n_done)
            dve.tensor_tensor(on1[:, c, :, :].rearrange("p t (j d) -> p (t j) d", d=HD1),
                              O_PS[c][:, 0:2 * P].rearrange("p (g d) -> p g d", d=HD1),
                              rec1[:, c, :, :].rearrange("p t j -> p (t j)").unsqueeze(2)
                              .to_broadcast([P, 2 * HC, HD1]), ALU.mult).then_inc(s_on1, 1)

        def dve_x1(dve, b):
            dve.wait_ge(s_wo1, ONE + b + 1)
            dve.wait_ge(s_bo, 1)
            xs = x[:, bass.ds(2 * b, 2), :].rearrange("p t d -> p (t d)")
            dve.tensor_tensor(xs, xs, F_PS[1][:, :], ALU.add).then_inc(s_x1, 1)

        def dve_slot1(dve):
            def slot(b, m, c, j, n, k, i, first, last, end):
                if not (first and i == 0):
                    dve_pt(dve, u1, n - 1, 1 - k, first and i < 3)
                if not end:
                    dve_max(dve, u1, n + 1, 1 - k)
                if j == 5 and c == 0 and not last:
                    dve.wait_ge(s_v1, m + 2)
                    dve_hb(dve, b + 1)
                if j == 1 and not (first and c == 0):
                    dve_on1(dve, m - 1, n - 1, 1 - c)
                if j == 6 and c == 0 and not first:
                    dve_x1(dve, b - 1)
            return slot

        def pool_slot1(pool):
            def slot(b, m, c, j, n, k, i, first, last, end):
                if j == 3 and not (last and c == CH - 1):
                    make_kbd(pool, m + 1, 1 - c)
            return slot

        def run1(eng, slot):
            body1(slot, 0, True, False)
            with eng.Fori(1, B - 1) as b:
                body1(slot, b, False, False)
            body1(slot, B - 1, False, True)

        GX = XE * KC
        shared.close()
        zs = tmp("zs", [P, 2, XB])
        gu = tmp("gu", [P, GX, XB])
        s_ctx = sem("s_ctx")
        s_tid = sem("s_tid")
        s_oh = sem("s_oh")
        s_z = sem("s_z")
        s_zs = sem("s_zs")
        s_zz = sem("s_zz")
        s_gu = sem("s_gu")
        s_y = sem("s_y")
        s_x2 = sem("s_x2")

        def pe_experts(pe):
            pe.wait_ge(s_ctx, 16)
            pe.wait_ge(n2.hT, 4)
            with pe.Fori(0, N // XB) as t:
                def z(g):
                    e, f = divmod(g, KC)
                    if g < 2:
                        pe.wait_ge(s_zz, ONE + GX * t)
                    else:
                        pe.wait_ge(s_zz, ONE + GX * t + g - 1)
                    for q in range(KC):
                        mm = pe.matmul(F_PS[g % 2][:, 0:XB], ctxT[:, e, q, f * P:(f + 1) * P],
                                       hT[:, q, bass.ds(t * XB, XB)], start=(q == 0), stop=(q == KC - 1))
                    mm.then_inc(s_z, 1)

                def down(g):
                    e, f = divmod(g, KC)
                    pe.wait_ge(s_gu, ONE + GX * t + g + 1)
                    if g == 0:
                        pe.wait_ge(s_x2, ONE + 2 * t)
                    for i in range(2):
                        mm = pe.matmul(O_PS[i][:, 0:D], gu[:, g, i * P:(i + 1) * P], ctxT[:, e, f, :],
                                       start=(g == 0), stop=(g == GX - 1))
                    if g == GX - 1:
                        mm.then_inc(s_y, 1)

                z(0)
                z(1)
                for g in range(2, GX):
                    z(g)
                    down(g - 2)
                down(GX - 2)
                down(GX - 1)

        def act_experts(act):
            with act.Fori(0, N // XB) as t:
                for g in range(GX):
                    act.wait_ge(s_z, GX * t + g + 1)
                    if g < 2:
                        act.wait_ge(s_gu, ONE + GX * t)
                    else:
                        act.wait_ge(s_gu, ONE + GX * t + g - 1)
                    act.activation(zs[:, g % 2, :], F_PS[g % 2][:, 0:XB], ACT.Silu).then_inc(s_zs, 1)

        def dve_onehot(dve):
            dve.wait_ge(s_tid, 16)
            dve.tensor_scalar(onehot[:, 0, :], tid[:, :], float(PER_EXPERT), None, ALU.is_lt).then_inc(s_oh, 1)
            for e in range(1, XE):
                dve.tensor_scalar(onehot[:, e, :], tid[:, :], float(PER_EXPERT * e), None, ALU.is_ge).then_inc(s_oh, 1)
            dve.wait_ge(s_oh, XE)
            for e in range(1, XE - 1):
                dve.tensor_tensor(onehot[:, e, :], onehot[:, e, :], onehot[:, e + 1, :], ALU.subtract)\
                   .then_inc(s_oh, 1)
                dve.wait_ge(s_oh, XE + e)

        def dve_experts(dve):
            with dve.Fori(0, N // XB) as t:
                for g in range(GX):
                    dve.wait_ge(s_zs, GX * t + g + 1)
                    dve.tensor_tensor(zs[:, g % 2, :], zs[:, g % 2, :], F_PS[g % 2][:, 0:XB], ALU.mult)\
                       .then_inc(s_zz, 1)
                    dve.wait_ge(s_zz, ONE + GX * t + g + 1)
                    if g == 0:
                        dve.wait_ge(s_y, ONE + t)
                    dve.tensor_tensor(gu[:, g, :], zs[:, g % 2, :], onehot[:, g // KC, bass.ds(t * XB, XB)],
                                      ALU.mult).then_inc(s_gu, 1)
                dve.wait_ge(s_y, ONE + t + 1)
                for i in range(2):
                    xs = x[:, bass.ds(2 * t + i, 1), :].rearrange("p t d -> p (t d)")
                    dve.tensor_tensor(xs, xs, O_PS[i][:, 0:D], ALU.add).then_inc(s_x2, 1)

        shared.close()
        q3 = tmp("q3", [P, 2, N])
        k3 = tmp("k3", [P, 2, N])
        v3 = tmp("v3", [P, 2, NT, HD3])
        o3 = tmp("o3", [P, 2, N])
        u3 = Unit("u3")
        s_w3 = [sem("s_w3a"), sem("s_w3b")]
        s_wo3 = sem("s_wo3")
        s_f3 = sem("s_f3")
        s_fe3 = sem("s_fe3")
        s_oe3 = sem("s_oe3")
        s_wd3 = sem("s_wd3")
        s_acc = sem("s_acc")

        def pe_proj3(pe, head, a, part, acc_before=None):
            for i in range(2):
                f = 6 * head + 2 * part + i
                if not (isinstance(f, int) and f < 2):
                    pe.wait_ge(s_fe3, f - 1)
                if acc_before is not None:
                    pe.wait_ge(s_acc, acc_before - 1 + i)
                if part < 2:
                    for q in range(KC):
                        mm = pe.matmul(F_PS[i][:, :], w3[:, a, part, q, :], hT[:, q, i * 512:(i + 1) * 512],
                                       start=(q == 0), stop=(q == KC - 1))
                else:
                    for t in range(4):
                        for q in range(KC):
                            mm = pe.matmul(F_PS[i][:, t * P:(t + 1) * P],
                                           hT[:, q, (4 * i + t) * P:(4 * i + t + 1) * P], w3[:, a, 2, q, :],
                                           start=(q == 0), stop=(q == KC - 1), skip_group_check=True)
                mm.then_inc(s_f3, 1)

        def act_proj3(act, head, a, part):
            for i in range(2):
                act.wait_ge(s_f3, 6 * head + 2 * part + i + 1)
                half = slice(i * 512, (i + 1) * 512)
                if part == 0:
                    act.activation(q3[:, a, half], F_PS[i][:, :], ACT.Copy, scale=float(QHD) ** -0.5)\
                       .then_inc(s_fe3, 1)
                elif part == 1:
                    act.activation(k3[:, a, half], F_PS[i][:, :], ACT.Copy).then_inc(s_fe3, 1)
                else:
                    act.activation(v3[:, a, 4 * i:4 * i + 4, :].rearrange("p t d -> p (t d)"), F_PS[i][:, :],
                                   ACT.Copy).then_inc(s_fe3, 1)

        def pe_wo3(pe, p, fe_before):
            pe.wait_ge(s_wo3, 16 * (p + 1))
            pe.wait_ge(s_oe3, 4 * (p + 1))
            for g in range(4):
                if g < 2:
                    pe.wait_ge(s_fe3, fe_before - 1 + g)
                else:
                    pe.wait_ge(s_acc, 4 * p + g - 1)
                for t in range(2):
                    for a in range(2):
                        mm = pe.matmul(F_PS[g % 2][:, t * D:(t + 1) * D],
                                       o3[:, a, (2 * g + t) * P:(2 * g + t + 1) * P], wo3[:, a, :],
                                       start=(a == 0), stop=(a == 1), skip_group_check=True)
                mm.then_inc(s_wd3, 1)

        def dve_wo3(dve, p):
            for g in range(4):
                dve.wait_ge(s_wd3, 4 * p + g + 1)
                dst = acc[:, 2 * g:2 * g + 2, :].rearrange("p t d -> p (t d)")
                dve.tensor_tensor(dst, dst, F_PS[g % 2][:, :], ALU.add).then_inc(s_acc, 1)

        def body3(slot, p, first, last):
            for a in range(2):
                for b in range(B):
                    u = 4 * a + b
                    slot(p, a, b, u, first, last, last and u == 7)

        def pe_slot3(pe):
            def slot(p, a, b, u, first, last, end):
                n = 8 * p + u
                if not end:
                    a2, b2 = divmod((u + 1) % 8, 4)
                    head2 = 2 * p + (u + 1) // 4
                    if b2 == 0:
                        pe.wait_ge(s_fe3, 6 * head2 + 4)
                    pe_scores(pe, u3, n + 1, (u + 1) % 2, q3[:, a2, b2 * T:(b2 + 1) * T],
                              k3[:, a2, b2 * T:(b2 + 1) * T], first and u == 0)
                if not (first and u == 0):
                    a0, b0 = divmod((u - 1) % 8, 4)
                    head0 = 2 * p + (u - 1) // 4
                    pe_pv3(pe, n - 1, a0, b0, head0, first and 0 < u <= 4)
                if a == 0 and b == 1 and not first:
                    pe_wo3(pe, p - 1, 6 * (2 * p + 1) + 2)
                if b < 3 and not (last and a == 1):
                    wait_w3(pe, p, a, b)
                    pe_proj3(pe, 2 * p + a + 1, 1 - a, b,
                             acc_before=(4 * p if (a == 0 and b == 1 and not first) else None))
                pe_transpose(pe, u3, n, u % 2, first and u < 2)
            return slot

        def wait_w3(pe, p, a, b):
            if b == 0:
                pe.wait_ge(s_w3[1 - a], 16 * (p + a + 1))

        def pe_pv3(pe, n, a, b, head, nofree):
            if b == 0:
                pe.wait_ge(s_fe3, 6 * head + 6)
            if b % 2 == 0 and not nofree:
                pe.wait_ge(s_oe3, 2 * head + b // 2 - 1)
            o_ps = O_PS[b // 2][:, (b % 2) * T:(b % 2 + 1) * T]
            pe_pv(pe, u3, n, (n_par(b)), o_ps, v3[:, a, 2 * b, :], v3[:, a, 2 * b + 1, :])

        def n_par(b):
            return b % 2

        def act_o3(act, head, a, i):
            act.wait_ge(u3.o, 4 * head + 2 * i + 2)
            act.activation(o3[:, a, i * 512:(i + 1) * 512], O_PS[i][:, :], ACT.Copy).then_inc(s_oe3, 1)

        def act_slot3(act):
            def slot(p, a, b, u, first, last, end):
                n = 8 * p + u
                if not end:
                    act_exp(act, u3, n + 1, (u + 1) % 2, first and u == 0)
                if b == 0 and not (first and a == 0):
                    act_o3(act, 2 * p + a - 1, 1 - a, 1)
                if b == 2:
                    act_o3(act, 2 * p + a, a, 0)
                if b < 3 and not (last and a == 1):
                    act_proj3(act, 2 * p + a + 1, 1 - a, b)
            return slot

        def dve_slot3(dve):
            def slot(p, a, b, u, first, last, end):
                n = 8 * p + u
                if not (first and u == 0):
                    dve_pt(dve, u3, n - 1, (u + 1) % 2, first and u < 3)
                if not end:
                    dve_max(dve, u3, n + 1, (u + 1) % 2)
                    dve_recip(dve, u3, n + 1, (u + 1) % 2)
                if a == 0 and b == 1 and not first:
                    dve_wo3(dve, p - 1)
            return slot

        def pool_slot3(pool):
            def slot(p, a, b, u, first, last, end):
                if not end:
                    pool_normalise(pool, u3, 8 * p + u + 1, (u + 1) % 2)
            return slot

        def run3(eng, slot):
            body3(slot, 0, True, False)
            with eng.Fori(1, PAIRS - 1) as p:
                body3(slot, p, False, False)
            body3(slot, PAIRS - 1, False, True)

        shared.close()
        lg = tmp("lg", [P, NT, E3])
        mx = tmp("mx", [P, NT])
        pr = tmp("pr", [P, NT, E3])
        top = tmp("top", [P, NT, 8])
        left = tmp("left", [P, NT, E3])
        wr = tmp("wr", [32, N])
        wmh = tmp("wmh", [P, WSLOTS, 6, P], F32R)
        wml = tmp("wml", [P, WSLOTS, 6, P], F32R)
        wb = tmp("wb", [P, WSLOTS, N])
        gs = tmp("gs", [P, 2, HALF])
        am = tmp("am", [P, 2, HALF])
        amh = tmp("amh", [P, 2, HALF], F32R)
        aml = tmp("aml", [P, 2, HALF], F32R)
        yT = tmp("yT", [P, KC, N])
        by_expert = nc.dram_tensor("by_expert", [32, N], F32, kind="Internal").ap()
        by_group = nc.dram_tensor("by_group", [NCH * P // GROUP, N], F32, kind="Internal").ap()
        G_PS, U_PS, Y_PS = bank[0:2], bank[2:4], bank[4:8]
        s_gate = sem("s_gate")
        s_lg = sem("s_lg")
        s_rt = sem("s_rt")
        s_rx = sem("s_rx")
        s_wt = sem("s_wt")
        s_wr = sem("s_wr")
        s_be = sem("s_be")
        s_bg = sem("s_bg")
        s_wb = [sem(f"s_wb{i}") for i in range(WSLOTS)]
        s_wm = [sem(f"s_wm{i}") for i in range(WSLOTS)]
        s_wh = sem("s_wh")
        s_wl = sem("s_wl")
        s_gu3 = sem("s_gu3")
        s_gs = sem("s_gs")
        s_gm = sem("s_gm")
        s_am = sem("s_am")
        s_ah = sem("s_ah")
        s_al = sem("s_al")
        s_dn = sem("s_dn")
        s_yT = sem("s_yT")
        s_yt = sem("s_yt")
        s_fin = sem("s_fin")
        s_xh = sem("s_xh")
        s_out = sem("s_out")
        TURNS = (NCH - 1) // WSLOTS
        assert NCH == TURNS * WSLOTS + 1

        def channels(eng, work):
            with eng.Fori(0, TURNS) as i:
                for r in range(WSLOTS):
                    work(WSLOTS * i + r, r, i, False)
            work(NCH - 1, 0, TURNS, True)

        def sp_channels(sp):
            def weights(c, r):
                sp.dma_start(wm[:, r, :, :].rearrange("p s n -> p (s n)"),
                             moe_in[bass.ds(c, 1)].rearrange("a p n -> (a p) n")).then_inc(s_wm[r], 16)

            def routing(c, r):
                sp.wait_ge(s_am, AM0 + 2 * (c - 1))
                n = P // GROUP
                sp.dma_start(wb[:, r, :], by_group[bass.ds(c * n, n), :].unsqueeze(1).to_broadcast([n, GROUP, N]))\
                  .then_inc(s_wb[r], 16)

            for c in range(WSLOTS):
                weights(c, c)
            sp.wait_ge(s_wr, 1)
            sp.dma_start(by_expert[0:E3 + 1, :], wr[0:E3 + 1, :]).then_inc(s_be, 16)
            sp.wait_ge(s_be, 16)
            n = INNER // GROUP
            sp.dma_start(by_group[0:E3 * n, :].rearrange("(e g) t -> e g t", g=n),
                         by_expert[0:E3, :].unsqueeze(1).to_broadcast([E3, n, N])).then_inc(s_bg, 16)
            rest = NCH * P // GROUP - E3 * n
            sp.dma_start(by_group[E3 * n:E3 * n + rest, :],
                         by_expert[E3:E3 + 1, :].to_broadcast([rest, N])).then_inc(s_bg, 16)
            sp.wait_ge(s_bg, 32)

            def work(c, r, more):
                routing(c, r)
                if more:
                    sp.wait_ge(s_wl, 2 * (c + 1))
                    weights(c + WSLOTS, r)
            with sp.Fori(0, TURNS - 1) as i:
                for r in range(WSLOTS):
                    work(WSLOTS * i + r, r, True)
            for c in range(NCH - 3, NCH):
                work(c, c % WSLOTS, c < NCH - WSLOTS)

        def act_split(act, c, r, load, part):
            if part == 0:
                act.wait_ge(s_wm[r], 16 * load)
                cols = slice(0, 4)
            else:
                if not (isinstance(c, int) and c == 0):
                    act.wait_ge(s_dn, DN0 + 2 * (c - 1))
                cols = slice(4, 6)
            act.activation(wmh[:, r, cols, :], wm[:, r, cols, :], ACT.Copy).then_inc(s_wh, 1)

        def pool_channels(pool):
            def work(c, r, i, last):
                for part, cols in enumerate((slice(0, 4), slice(4, 6))):
                    pool.wait_ge(s_wh, 2 * c + part + 1)
                    pool.tensor_tensor(wml[:, r, cols, :], wm[:, r, cols, :], wmh[:, r, cols, :].bitcast(F32),
                                       ALU.subtract).then_inc(s_wl, 1)
            channels(pool, work)

        def act_channels(act):
            def half(c, r, hf):
                v = 2 * c + hf
                act.wait_ge(s_gu3, v + 1)
                act.wait_ge(s_am, AM0 + v - 1)
                act.activation(gs[:, hf, :], G_PS[hf][:, :], ACT.Silu).then_inc(s_gs, 1)

            def high(c, r, hf):
                v = 2 * c + hf
                act.wait_ge(s_am, AM0 + v + 1)
                act.wait_ge(s_dn, DN0 + v - 1)
                act.activation(amh[:, hf, :], am[:, hf, :], ACT.Copy).then_inc(s_ah, 1)

            def work(c, r, i, last):
                nxt = (1 - r, i + 1 + r)
                half(c, r, 0)
                if not last:
                    act_split(act, c + 1, *nxt, 0)
                high(c, r, 0)
                half(c, r, 1)
                high(c, r, 1)
                if not last:
                    act_split(act, c + 1, *nxt, 1)
            channels(act, work)
            for hf in range(2):
                act.wait_ge(s_dn, DN0 + 2 * (NCH - 1) + hf + 1)
                for q in range(KC):
                    act.activation(yT[:, q, hf * HALF:(hf + 1) * HALF], Y_PS[2 * hf + q][:, :],
                                   ACT.Copy).then_inc(s_yT, 1)

        def pe_gate_up(pe, c, r, hf):
            v = 2 * c + hf
            pe.wait_ge(s_wl, 2 * c + 1)
            if not (isinstance(c, int) and c == 0):
                pe.wait_ge(s_gm, v - 1)
            cols = slice(hf * HALF, (hf + 1) * HALF)
            for ps, w in ((G_PS[hf], 0), (U_PS[hf], 2)):
                for q in range(KC):
                    mm = matmul3(pe, ps[:, :], (wmh[:, r, w + q, :], wml[:, r, w + q, :]),
                                 (hTh[:, q, cols], hTl[:, q, cols]), q == 0, q == KC - 1)
            mm.then_inc(s_gu3, 1)

        def pe_down(pe, c, r, hf):
            pe.wait_ge(s_al, 2 * c + hf + 1)
            pe.wait_ge(s_wl, 2 * c + 2)
            for q in range(KC):
                mm = matmul3(pe, Y_PS[2 * hf + q][:, :], (wmh[:, r, 4 + q, :], wml[:, r, 4 + q, :]),
                             (amh[:, hf, :], aml[:, hf, :]), False, False, check=True)
            mm.then_inc(s_dn, 1)

        def pe_channels(pe):
            pe.wait_ge(s_wr, 1)
            for q in range(4):
                pe.matmul(Y_PS[q][:, :], zb[:, 0:P], zb[:, :], start=True, stop=False, skip_group_check=True)

            def work(c, r, i, last):
                for hf in range(2):
                    if not last:
                        pe_gate_up(pe, c + 1, 1 - r, hf)
                    pe_down(pe, c, r, hf)
            channels(pe, work)
            pe.wait_ge(s_gm, 2 * NCH)
            for g in range(4):
                pe.wait_ge(s_yT, KC * (g // 2 + 1))
                for t in range(2):
                    for q in range(KC):
                        mm = pe.transpose(bank[g][:, t * D + q * P:t * D + (q + 1) * P],
                                          yT[:, q, (2 * g + t) * P:(2 * g + t + 1) * P], ident[:, :])
                mm.then_inc(s_yt, 1)

        def dve_channels(dve):
            def work(c, r, i, last):
                for hf in range(2):
                    v = 2 * c + hf
                    dve.wait_ge(s_gs, v + 1)
                    dve.tensor_tensor(gs[:, hf, :], gs[:, hf, :], U_PS[hf][:, :], ALU.mult).then_inc(s_gm, 1)
                    dve.wait_ge(s_gm, v + 1)
                    if hf == 0:
                        dve.wait_ge(s_wb[r], 16 * (i + 1))
                    dve.tensor_tensor(am[:, hf, :], gs[:, hf, :], wb[:, r, hf * HALF:(hf + 1) * HALF],
                                      ALU.mult).then_inc(s_am, 1)
                    dve.wait_ge(s_ah, v + 1)
                    dve.wait_ge(s_dn, DN0 + v - 1)
                    dve.tensor_tensor(aml[:, hf, :], am[:, hf, :], amh[:, hf, :].bitcast(F32),
                                      ALU.subtract).then_inc(s_al, 1)
            channels(dve, work)
            dve.wait_ge(s_xh, 1)
            for g in range(4):
                dve.wait_ge(s_yt, g + 1)
                xs = x[:, 2 * g:2 * g + 2, :].rearrange("p t d -> p (t d)")
                dve.tensor_tensor(xs, xs, bank[g][:, :], ALU.add).then_inc(s_fin, 1)

        def pe_routing(pe):
            pe.wait_ge(s_gate, 16)
            pe.wait_ge(n4.hT, 4)
            for t in range(NT):
                for q in range(KC):
                    mm = pe.matmul(Y_PS[0][:, t * E3:(t + 1) * E3], hT[:, q, t * P:(t + 1) * P], gate[:, q, :],
                                   start=(q == 0), stop=(q == KC - 1), skip_group_check=True)
            mm.then_inc(s_lg, 1)

        def pe_routing_transposes(pe):
            pe.wait_ge(s_rt, ROUTED)
            for t in range(NT):
                mm = pe.transpose(Y_PS[t // 4][0:32, (t % 4) * P:(t % 4 + 1) * P], wt[:, t, :], ident[:, :])
            mm.then_inc(s_wt, 1)

        ROUTED = 5 + NT + 1 + NT + 4

        def dve_routing(dve):
            steps = [0]

            def step(ins):
                steps[0] += 1
                ins.then_inc(s_rt, 1)
                dve.wait_ge(s_rt, steps[0])

            def wide(a):
                return a.unsqueeze(2).to_broadcast([P, NT, E3])

            logits = Y_PS[0][:, 0:NT * E3].rearrange("p (t e) -> p t e", e=E3)
            dve.wait_ge(s_lg, 1)
            step(dve.tensor_reduce(mx[:, :], logits, AX.X, ALU.max))
            step(dve.tensor_tensor(lg[:, :, :], logits, wide(mx[:, :]), ALU.subtract))
            dve.wait_ge(s_rx, 1)
            step(dve.tensor_reduce(mx[:, :], pr[:, :, :], AX.X, ALU.add))
            step(dve.reciprocal(mx[:, :], mx[:, :]))
            step(dve.tensor_tensor(pr[:, :, :], pr[:, :, :], wide(mx[:, :]), ALU.mult))
            for t in range(NT):
                step(dve.max(top[:, t, :], pr[:, t, :]))
            step(dve.memset(top[:, :, TOPK:8], -2.0))
            for t in range(NT):
                step(dve.match_replace(left[:, t, :], top[:, t, :], pr[:, t, :], -1.0))
            step(dve.scalar_tensor_tensor(wt[:, :, 0:E3], left[:, :, :], 0.0, pr[:, :, :], ALU.is_lt, ALU.mult))
            step(dve.tensor_reduce(mx[:, :], wt[:, :, 0:E3], AX.X, ALU.add))
            step(dve.reciprocal(mx[:, :], mx[:, :]))
            step(dve.tensor_tensor(wt[:, :, 0:E3], wt[:, :, 0:E3], wide(mx[:, :]), ALU.mult))
            dve.wait_ge(s_wt, 1)
            step(dve.tensor_copy(wr[:, 0:512], Y_PS[0][0:32, :]))
            dve.tensor_copy(wr[:, 512:1024], Y_PS[1][0:32, :]).then_inc(s_wr, 1)

        @block.sync
        def _(sp):
            for t in range(4):
                sp.dma_start(x[:, 2 * t:2 * t + 2, :],
                             x_in[t * 256:(t + 1) * 256, :].rearrange("(t p) d -> p t d", p=P)).then_inc(s_x, 16)
            for dst, src in ((ident, ident_in), (tri, tri_in), (headmask, headmask_in), (vec, vec_in)):
                sp.dma_start(dst[:, :], src).then_inc(s_const, 16)
            sp.dma_start(bo[:, :], bo_in.partition_broadcast(P)).then_inc(s_const, 16)
            for dst, src in ((wq, wqT_in), (wk, wkT_in), (wv, wvT_in), (wo, woT_in)):
                sp.dma_start(dst[:, :, :], src.rearrange("(q p) n -> p q n", p=P)).then_inc(s_w1, 16)
            sp.dma_start(tid[:, :], tok_in.partition_broadcast(P)).then_inc(s_tid, 16)
            sp.dma_start(ctxT[:, :, :, :].rearrange("p e q n -> p (e q) n"),
                         ctxT_in.rearrange("(g p) n -> p g n", p=P)).then_inc(s_ctx, 16)
            sp.dma_start(gate[:, :, :], gate_in.rearrange("(q p) n -> p q n", p=P)).then_inc(s_gate, 16)
            for a in range(2):
                sp.dma_start(w3[:, a, :, :, :].rearrange("p s q n -> p (s q n)"), ffn_qkv_in[a]).then_inc(s_w3[a], 16)
            sp.dma_start(wo3[:, :, :], ffn_o_in[0]).then_inc(s_wo3, 16)
            with sp.Fori(0, PAIRS - 1) as p:
                for a in range(2):
                    sp.wait_ge(s_f3, 6 * (2 * p + a + 1))
                    sp.dma_start(w3[:, a, :, :, :].rearrange("p s q n -> p (s q n)"),
                                 ffn_qkv_in[bass.ds(2 * p + 2 + a, 1)].rearrange("a p n -> (a p) n"))\
                      .then_inc(s_w3[a], 16)
                sp.wait_ge(s_wd3, 4 * p + 4)
                sp.dma_start(wo3[:, :, :].rearrange("p a n -> p (a n)"),
                             ffn_o_in[bass.ds(p + 1, 1)].rearrange("a p b n -> (a p) (b n)")).then_inc(s_wo3, 16)
            sp_channels(sp)
            for g in range(4):
                sp.wait_ge(s_fin, g + 1)
                sp.dma_start(out[g * 256:(g + 1) * 256, :].rearrange("(t p) d -> p t d", p=P),
                             x[:, 2 * g:2 * g + 2, :]).then_inc(s_out, 16)
            sp.wait_ge(s_out, 64)

        @block.gpsimd
        def _(pool):
            pool.memset(pw[:, :], -0.5).then_inc(s_init, 1)
            pool.memset(vbd[:, :, :, :], 0.0).then_inc(s_init, 1)
            pool.wait_ge(s_init, 1)
            ln_gpsimd(pool, n1)
            pool.memset(zb[:, :], 0.0).then_inc(s_init, 1)
            for i, (s, n) in enumerate(((s_wo1, ONE), (s_zz, ONE), (s_gu, ONE), (s_y, ONE), (s_x2, ONE), (s_am, AM0),
                                        (s_dn, DN0))):
                pool.memset(credit[:, i:i + 1], 0.0).then_inc(s, n)
            pool.memset(wt[:, :, :], 0.0).then_inc(s_init, 1)
            pool.wait_ge(s_init, 4)
            pool.memset(wt[:, :, E3:E3 + 1], 1.0).then_inc(s_init, 1)
            pool.wait_ge(s_const, 16 * 5)
            pool.wait_ge(n1.h, NT)
            pool.tensor_tensor(x[:, :, :], x[:, :, :], bo[:, :].unsqueeze(1).to_broadcast([P, NT, D]),
                               ALU.add).then_inc(s_bo, 1)
            run1(pool, pool_slot1(pool))
            ln_gpsimd(pool, n2)
            ln_gpsimd(pool, n3)
            rms_gpsimd(pool, n3r)
            pool_normalise(pool, u3, 0, 0)
            run3(pool, pool_slot3(pool))
            rms_gpsimd(pool, n4)
            pool.tensor_tensor(x[:, :, :], x[:, :, :], acc[:, :, :], ALU.add).then_inc(s_xh, 1)
            pool_channels(pool)

        @block.scalar
        def _(act):
            act.wait_ge(s_const, 16 * 5)
            act.activation(bqs[:, :], vec[:, 0:2], ACT.Copy, scale=float(HD1) ** -0.5).then_inc(s_castc, 1)
            act.wait_ge(s_castc, 3)
            hT_scalar(act, n1)
            act.wait_ge(s_init, 2)
            act_q1(act, 0, 0)
            act_v1(act, 0, 0)
            act_exp1(act, 0, 0, 0, 0, True)
            run1(act, act_slot1(act))
            act_o1(act, CH * B - 1, CH - 1, B - 1)
            hT_scalar(act, n2)
            act_experts(act)
            rms_scalar(act, n3r, acc, n3)
            hT_scalar(act, n3r, weight=6)
            for part in range(3):
                act_proj3(act, 0, 0, part)
            act_exp(act, u3, 0, 0, True)
            run3(act, act_slot3(act))
            act_o3(act, H3 - 1, 1, 1)
            act.wait_ge(s_acc, 4 * PAIRS)
            rms_scalar(act, n4, acc)
            hT_scalar(act, n4, weight=8, split=True)
            for part in range(2):
                act_split(act, 0, 0, 1, part)
            act.wait_ge(s_rt, 2)
            act.activation(pr[:, :, :], lg[:, :, :], ACT.Exp).then_inc(s_rx, 1)
            act_channels(act)

        @block.tensor
        def _(pe):
            pe.wait_ge(s_castc, 3)
            transposes(pe, n1, h)
            pe.wait_ge(s_w1, 64)
            pe.wait_ge(n1.hT, 4)
            pe_qkv1(pe, 0, 0, 0, first=True)
            pe_s1(pe, 0, 0, 0, 0, 0, True)
            run1(pe, pe_slot1(pe))
            pe_pv1(pe, CH * HC * B - 1, CH * HC - 1, CH * B - 1, CH - 1, HC - 1, False)
            pe_ot1(pe, CH * B - 1, CH - 1)
            pe_wo1(pe, B - 1, 4 * B)
            transposes(pe, n2, h)
            pe_experts(pe)
            transposes(pe, n3r, h)
            pe.wait_ge(s_w3[0], 16)
            pe.wait_ge(n3r.hT, 4)
            for part in range(3):
                pe_proj3(pe, 0, 0, part)
            pe.wait_ge(s_fe3, 4)
            pe_scores(pe, u3, 0, 0, q3[:, 0, 0:T], k3[:, 0, 0:T], True)
            run3(pe, pe_slot3(pe))
            pe_pv3(pe, 4 * H3 - 1, 1, 3, H3 - 1, False)
            pe_wo3(pe, PAIRS - 1, 6 * H3)
            transposes(pe, n4, h)
            pe_routing(pe)
            pe.wait_ge(n4.hl, 4)
            for hf in range(2):
                pe_gate_up(pe, 0, 0, hf)
            pe_routing_transposes(pe)
            pe_channels(pe)

        @block.vector
        def _(dve):
            dve.wait_ge(s_x, 64)
            ln_vector(dve, n1, x, h)
            dve.wait_ge(s_const, 16 * 5)
            dve.tensor_copy(identb[:, :], ident[:, :]).then_inc(s_castc, 1)
            dve.tensor_copy(trib[:, :, :], tri[:, :].unsqueeze(1).to_broadcast([P, 2, P])).then_inc(s_castc, 1)
            dve.wait_ge(n1.hT, 4)
            dve_hb(dve, 0)
            make_kbd(dve, 0, 0)
            dve_max(dve, u1, 0, 0)
            dve_onehot(dve)
            run1(dve, dve_slot1(dve))
            dve_pt(dve, u1, CH * HC * B - 1, 1, False)
            dve_on1(dve, CH * B - 1, CH * HC * B, CH - 1)
            dve_x1(dve, B - 1)
            dve.wait_ge(s_x1, B)
            ln_vector(dve, n2, x, h)
            dve_experts(dve)
            dve.wait_ge(s_x2, ONE + NT)
            ln_vector(dve, n3, x, acc)
            rms_vector(dve, n3r, acc, h)
            dve_max(dve, u3, 0, 0)
            dve_recip(dve, u3, 0, 0)
            run3(dve, dve_slot3(dve))
            dve_pt(dve, u3, 4 * H3 - 1, 1, False)
            dve_wo3(dve, PAIRS - 1)
            rms_vector(dve, n4, acc, h)
            hT_vector(dve, n4)
            dve_routing(dve)
            dve_channels(dve)

        shared.close()


def _constants():
    import numpy as np

    ident = np.eye(P, dtype=np.float32)
    tri = np.where(np.arange(P)[None, :] <= np.arange(P)[:, None], 0.0, MASKED).astype(np.float32)
    headmask = (np.arange(P)[:, None] // HD1 == np.arange(HC)[None, :]).astype(np.float32)
    return {"ident": ident, "tri": tri, "headmask": headmask}


def _layout(i):
    import numpy as np

    a = {k: np.asarray(v) for k, v in i.items()}
    f = {k[len("L0_ffn_"):]: v for k, v in a.items() if k.startswith("L0_ffn_")}

    def chunks(w):
        return w.T.reshape(KC, P, -1).transpose(1, 0, 2)

    q = f["q_w"].reshape(H3, QHD, D)[:, :HD3]
    kv = f["kv_w"]
    k = kv[:H3 * HD3].reshape(H3, HD3, D)
    v = kv[H3 * HD3:2 * H3 * HD3].reshape(H3, HD3, D)
    qkv = np.stack([np.stack([chunks(s[n]) for s in (q, k, v)], 1).reshape(P, -1) for n in range(H3)])
    o = f["o_w"].T.reshape(PAIRS, 2, HD3, D).transpose(0, 2, 1, 3)

    def padded(w):
        out = np.zeros((NCH * P, D), np.float32)
        out[:CHANNELS] = w
        return out

    g = padded(np.concatenate([f["w1"][:, :INNER].reshape(-1, D), f["sh_gu_w"][:SHARED]]))
    u = padded(np.concatenate([f["w1"][:, INNER:].reshape(-1, D), f["sh_gu_w"][SHARED:]]))
    d = padded(np.concatenate([f["w2"].transpose(0, 2, 1).reshape(-1, D), f["sh_down_w"].T]))
    moe = np.stack([np.concatenate([chunks(g[c * P:(c + 1) * P]).reshape(P, -1),
                                    chunks(u[c * P:(c + 1) * P]).reshape(P, -1),
                                    d[c * P:(c + 1) * P]], 1) for c in range(NCH)])
    vec = np.stack([a[n].reshape(KC, P)[c] for n in ("L0_attn_bq", "L0_attn_bk", "L0_attn_bv", "L0_ffn_ln1_w",
                                                     "L0_ffn_ln2_w") for c in range(KC)], 1)
    con = _constants()
    return [a["x"].reshape(N, D), a["itok_BxS_13_99985"].reshape(N),
            a["ctx_2048"].transpose(0, 2, 1).reshape(XE * D, D),
            a["L0_attn_Wq"], a["L0_attn_Wk"], a["L0_attn_Wv"], a["L0_attn_Wo"], vec, a["L0_attn_bo"], qkv, o,
            f["gate_w"].T, moe, con["ident"], con["tri"], con["headmask"]]


def kernel(**inputs):
    import numpy as np
    import concourse.bacc as bacc
    from concourse.bass_utils import run_bass_kernel_spmd

    nc = bacc.Bacc("TRN2", target_bir_lowering=False, num_devices=1)
    arrays, args = {}, []
    for n, v in enumerate(_layout(inputs)):
        name = f"in_{n}"
        arrays[name] = np.ascontiguousarray(v)
        args.append(nc.dram_tensor(name, arrays[name].shape, mybir.dt.from_np(arrays[name].dtype),
                                   kind="ExternalInput").ap())
    out = nc.dram_tensor("out", (N, D), F32, kind="ExternalOutput").ap()
    decoder_kernel(nc, *args, out)
    r = run_bass_kernel_spmd(nc, [arrays], core_ids=[0])
    return r.results[0]["out"].reshape(B, T, D)
```

```python
from contextlib import ExitStack

import concourse.bass as bass
from concourse import mybir

F32 = mybir.dt.float32
F32R = mybir.dt.float32r
BF16 = mybir.dt.bfloat16
I32 = mybir.dt.int32
ALU = mybir.AluOpType
ACT = mybir.ActivationFunctionType
AX = mybir.AxisListType

P = 128
B, T, D = 4, 256, 256
N = B * T
NT = N // P
GT = NT // 2
KC = D // P
LN_EPS, RMS_EPS = 1e-5, 1e-6
H1, HD1 = 16, 16
HC = P // HD1
CH = H1 // HC
VP = HC * (P + HD1)
XE, VOCAB = 4, 12500
PER_EXPERT = VOCAB // XE
XB = 512
H3, HD3, QHD = 16, 128, 192
PAIRS = H3 // 2
E3, INNER, SHARED, TOPK = 16, 176, 352, 4
CHANNELS = E3 * INNER + SHARED
NCH = -(-CHANNELS // P)
HALF = 512
WSLOTS = 2
GROUP = 16
MASKED = -1.0e30


def decoder_kernel(nc, x_in, tok_in, ctxT_in, wqT_in, wkT_in, wvT_in, woT_in, vec_in, bo_in, ffn_qk_in, ffn_v_in, ffn_o_in,
                   gate_in, moe_in, ident_in, tri_in, headmask_in, out):
    with ExitStack() as ctx:
        def sb(name, shape, dt=F32):
            return ctx.enter_context(nc.sbuf_tensor(name, shape, dt))

        def sem(name):
            return ctx.enter_context(nc.semaphore(name))

        shared = ExitStack()

        def tmp(name, shape, dt=F32):
            return shared.enter_context(nc.sbuf_tensor(name, shape, dt))

        bank = [ctx.enter_context(nc.psum_tensor(f"bank{i}", [P, 512], F32)) for i in range(8)]
        S_PS, PT_PS, O_PS, F_PS = bank[0:2], bank[2:4], bank[4:6], bank[6:8]

        ident = sb("ident", [P, P])
        identb = sb("identb", [P, P], BF16)
        tri = sb("tri", [P, P])
        trib = sb("trib", [P, 2, P], BF16)
        headmask = sb("headmask", [P, HC])
        vec = sb("vec", [P, 10])
        bqs = sb("bqs", [P, 2])
        bo = sb("bo", [P, D])
        pw = sb("pw", [P, NT])
        zb = sb("zb", [P, 512], BF16)
        x = sb("x", [P, NT, D])
        h = sb("h", [P, NT, D])
        acc = sb("acc", [P, NT, D])
        hT = sb("hT", [P, KC, N])
        hTh = sb("hTh", [P, KC, N], F32R)
        hTl = sb("hTl", [P, KC, N], F32R)
        st = sb("st", [P, NT, 6])
        mv = sb("mv", [P, NT, 2])
        ve = sb("ve", [P, NT])
        rstd = sb("rstd", [P, NT])
        ve3 = sb("ve3", [P, NT])
        rstd3 = sb("rstd3", [P, NT])
        eps = sb("eps", [P, 2])
        ss = sb("ss", [P, NT])
        sq = sb("sq", [P, D])
        p_sb = sb("p_sb", [P, 2, 384])
        pt_sb = sb("pt_sb", [P, 2, 384])
        nmax = sb("nmax", [P, 2, 2])
        psum_ = sb("psum_", [P, 2, 2])
        prec = sb("prec", [P, 2, 2])

        ctxT = sb("ctxT", [P, XE, KC, D])
        tid = sb("tid", [P, N], I32)
        onehot = sb("onehot", [P, XE, N])
        w3 = sb("w3", [P, 2, 2, KC, HD3])
        wv3 = sb("wv3", [P, KC, 2 * HD3])
        wo3 = sb("wo3", [P, 2, D])
        ctxTh = sb("ctxTh", [P, XE, KC, D], F32R)
        ctxTl = sb("ctxTl", [P, XE, KC, D], F32R)
        w3h = sb("w3h", [P, 2, 2, KC, HD3], F32R)
        w3l = sb("w3l", [P, 2, 2, KC, HD3], F32R)
        wv3h = sb("wv3h", [P, KC, 2 * HD3], F32R)
        wv3l = sb("wv3l", [P, KC, 2 * HD3], F32R)
        wo3h = sb("wo3h", [P, 2, D], F32R)
        wo3l = sb("wo3l", [P, 2, D], F32R)
        wmh = sb("wmh", [P, WSLOTS, 6, P], F32R)
        wml = sb("wml", [P, WSLOTS, 6, P], F32R)
        gate = sb("gate", [P, KC, P])
        wt = sb("wt", [P, NT, 32])
        wm = sb("wm", [P, WSLOTS, 6, P])

        s_const = sem("s_const")
        s_castc = sem("s_castc")
        s_init = sem("s_init")
        ONE, AM0, DN0 = 1, 3, 2
        credit = sb("credit", [P, 3])

        block = ctx.enter_context(nc.Block())

        class Norm:

            def __init__(self, tag, banks, split=True):
                self.split = split
                self.ps = banks
                self.stat = sem(f"{tag}_stat")
                self.var = sem(f"{tag}_var")
                self.h = sem(f"{tag}_h")
                self.tr = sem(f"{tag}_tr")
                self.hT = sem(f"{tag}_hT")
                self.hh = sem(f"{tag}_hh")
                self.hl = sem(f"{tag}_hl")

        n1, n2, n3 = Norm("n1", bank[0:4], split=False), Norm("n2", bank[0:4]), Norm("n3", None)
        n3r, n4 = Norm("n3r", bank[0:4]), Norm("n4", bank[4:8])

        def ln_stats(dve, s, src, g, tiles=range(GT)):
            for t in tiles:
                dve.bn_stats(st[:, GT * g + t, :], src[:, GT * g + t, :]).then_inc(s.stat, 1)
            if tiles[-1] == GT - 1:
                for t in range(GT):
                    dve.wait_ge(s.stat, 2 * GT * g + t + 1)
                    dve.bn_aggr(mv[:, GT * g + t, :], st[:, GT * g + t, :]).then_inc(s.stat, 1)

        def ln_gpsimd(pool, s, g):
            cols = slice(GT * g, GT * g + GT)
            pool.wait_ge(s.stat, 2 * GT * (g + 1))
            pool.tensor_scalar(ve[:, cols], mv[:, cols, 1], LN_EPS, 1.0, ALU.add, ALU.mult).then_inc(s.var, 1)
            pool.wait_ge(s.var, 2 * g + 1)
            pool.tensor_tensor(rstd[:, cols], ve[:, cols], pw[:, cols], ALU.pow).then_inc(s.var, 1)

        def ln_apply(dve, s, src, dst, g, scale=None, tiles=range(GT)):
            dve.wait_ge(s.var, 2 * g + 2)
            scale = rstd if scale is None else scale
            for t in tiles:
                t += GT * g
                dve.tensor_scalar(dst[:, t, :], src[:, t, :], mv[:, t, 0:1], scale[:, t:t + 1],
                                  ALU.subtract, ALU.mult).then_inc(s.h, 1)

        def rms_scalar(act, s, src, g, made, count):
            for t in range(GT * g, GT * g + GT):
                act.wait_ge(made, count(t))
                if t:
                    act.wait_ge(s.stat, t)
                act.activation(sq[:, :], src[:, t, :], ACT.Square, accum_out=ss[:, t:t + 1]).then_inc(s.stat, 1)

        def rms_gpsimd(pool, s, g):
            cols = slice(GT * g, GT * g + GT)
            pool.wait_ge(s.stat, GT * (g + 1))
            pool.tensor_scalar(ve[:, cols], ss[:, cols], 1.0 / D, RMS_EPS, ALU.mult, ALU.add).then_inc(s.var, 1)
            pool.wait_ge(s.var, 2 * g + 1)
            pool.tensor_tensor(rstd[:, cols], ve[:, cols], pw[:, cols], ALU.pow).then_inc(s.var, 1)

        def rms_vector(dve, s, src, dst, g):
            dve.wait_ge(s.var, 2 * g + 2)
            for t in range(GT * g, GT * g + GT):
                dve.tensor_scalar(dst[:, t, :], src[:, t, :], rstd[:, t:t + 1], None, ALU.mult).then_inc(s.h, 1)

        def transposes(pe, s, src, g):
            for c in range(KC):
                for j in range(GT):
                    pe.wait_ge(s.h, GT * g + j + 1)
                    mm = pe.transpose(s.ps[2 * g + c][:, j * P:(j + 1) * P],
                                      src[:, GT * g + j, c * P:(c + 1) * P], ident[:, :])
                mm.then_inc(s.tr, 1)

        def hT_scalar(act, s, g, weight=None, high=False):
            dst, signal = (hTh, s.hh) if high else (hT, s.hT)
            for c in range(KC):
                act.wait_ge(s.tr, 2 * g + c + 1)
                if s.split and not high:
                    act.wait_ge(s.hl, 2 * g + c + 1)
                act.activation(dst[:, c, g * 512:(g + 1) * 512], s.ps[2 * g + c][:, :], ACT.Copy,
                               scale=(1.0 if weight is None else vec[:, weight + c:weight + c + 1])).then_inc(signal, 1)

        def hT_vector(dve, s, g, weight=None):
            for c in range(KC):
                dve.wait_ge(s.hh, 2 * g + c + 1)
                cols = slice(g * 512, (g + 1) * 512)
                ps, hi = s.ps[2 * g + c][:, :], hTh[:, c, cols].bitcast(F32)
                if weight is None:
                    dve.tensor_tensor(hTl[:, c, cols], ps, hi, ALU.subtract).then_inc(s.hl, 1)
                else:
                    dve.scalar_tensor_tensor(hTl[:, c, cols], ps, vec[:, weight + c:weight + c + 1], hi, ALU.mult,
                                             ALU.subtract).then_inc(s.hl, 1)

        def matmul3(pe, out, lhs, rhs, start, stop, check=False):
            for i, (a, b) in enumerate(((0, 0), (0, 1), (1, 0))):
                mm = pe.matmul(out, lhs[a], rhs[b], start=(start and i == 0), stop=(stop and i == 2),
                               skip_group_check=check)
            return mm

        class Unit:
            def __init__(self, tag):
                self.s = sem(f"{tag}_s")
                self.nm = sem(f"{tag}_nm")
                self.ex = sem(f"{tag}_ex")
                self.rs = sem(f"{tag}_rs")
                self.pn = sem(f"{tag}_pn")
                self.t = sem(f"{tag}_t")
                self.pt = sem(f"{tag}_pt")
                self.o = sem(f"{tag}_o")

        def pe_scores(pe, u, n, k, qT, keys, first):
            if not first:
                pe.wait_ge(u.ex, 2 * (n - 1))
            s_ps = S_PS[k]
            pe.matmul(s_ps[:, 0:256], qT[:, P:2 * P], keys, start=True, stop=False, skip_group_check=True)
            pe.matmul(s_ps[:, 256:384], qT[:, 0:P], keys[:, 0:P], start=False, stop=False, skip_group_check=True)
            pe.matmul(s_ps[:, 128:384], identb[:, :], trib[:, :, :].rearrange("p a k -> p (a k)"), start=False,
                      stop=True, skip_group_check=True).then_inc(u.s, 1)

        def dve_max(dve, u, n, k):
            dve.wait_ge(u.s, n + 1)
            dve.tensor_reduce(nmax[:, k, 0:1], S_PS[k][:, 0:256], AX.X, ALU.max, negate=True).then_inc(u.nm, 1)
            dve.tensor_reduce(nmax[:, k, 1:2], S_PS[k][:, 256:384], AX.X, ALU.max, negate=True).then_inc(u.nm, 1)

        def act_exp(act, u, n, k, first, sums=None):
            sums = sums or (psum_[:, k, 0:1], psum_[:, k, 1:2])
            act.wait_ge(u.nm, 2 * n + 2)
            if not first:
                act.wait_ge(u.t, n - 1)
            act.activation(p_sb[:, k, 0:256], S_PS[k][:, 0:256], ACT.Exp, bias=nmax[:, k, 0:1],
                           accum_out=sums[0]).then_inc(u.ex, 1)
            act.activation(p_sb[:, k, 256:384], S_PS[k][:, 256:384], ACT.Exp, bias=nmax[:, k, 1:2],
                           accum_out=sums[1]).then_inc(u.ex, 1)

        def dve_recip(dve, u, n, k):
            dve.wait_ge(u.ex, 2 * n + 2)
            dve.reciprocal(prec[:, k, :], psum_[:, k, :]).then_inc(u.rs, 1)

        def pool_normalise(pool, u, n, k):
            pool.wait_ge(u.rs, n + 1)
            for cols, r in ((slice(0, 256), prec[:, k, 0:1]), (slice(256, 384), prec[:, k, 1:2])):
                p = p_sb[:, k, cols]
                pool.tensor_tensor(p, p, r.to_broadcast(p.shape), ALU.mult).then_inc(u.pn, 1)

        def pe_transpose(pe, u, n, k, first, normalised=True):
            if normalised:
                pe.wait_ge(u.pn, 2 * n + 2)
            else:
                pe.wait_ge(u.ex, 2 * n + 2)
            if not first:
                pe.wait_ge(u.pt, 2 * (n - 1))
            pe.transpose(PT_PS[k][:, 0:128], p_sb[:, k, 256:384], ident[:, :])
            pe.transpose(PT_PS[k][:, 128:256], p_sb[:, k, 0:128], ident[:, :])
            pe.transpose(PT_PS[k][:, 256:384], p_sb[:, k, 128:256], ident[:, :]).then_inc(u.t, 1)

        def dve_pt(dve, u, n, k, first):
            dve.wait_ge(u.t, n + 1)
            if not first:
                dve.wait_ge(u.o, n - 1)
            for cols in (slice(0, 256), slice(256, 384)):
                dve.tensor_copy(pt_sb[:, k, cols], PT_PS[k][:, cols]).then_inc(u.pt, 1)

        def pe_pv(pe, u, n, k, o_ps, v0, v1):
            pe.wait_ge(u.pt, 2 * n + 1)
            pe.matmul(o_ps[:, 0:256], v0, pt_sb[:, k, 0:256], start=True, stop=False, skip_group_check=True)
            pe.wait_ge(u.pt, 2 * n + 2)
            pe.matmul(o_ps[:, 128:256], v1, pt_sb[:, k, 256:384], start=False, stop=True,
                      skip_group_check=True).then_inc(u.o, 1)

        wq = tmp("wq", [P, KC, D])
        wk = tmp("wk", [P, KC, D])
        wv = tmp("wv", [P, KC, D])
        wo = tmp("wo", [P, KC, D])
        hb = tmp("hb", [P, KC, T])
        q1 = tmp("q1", [P, CH, T])
        k1 = tmp("k1", [P, T])
        kbd = tmp("kbd", [P, CH, HC, T])
        vbd = tmp("vbd", [P, CH, 2, VP])
        sums1 = tmp("sums1", [P, CH, 2, HC])
        rec1 = tmp("rec1", [P, CH, 2, HC])
        on1 = tmp("on1", [P, CH, 2, P])
        o1 = tmp("o1", [P, CH, T])

        u1 = Unit("u1")
        s_x = [sem("s_x0"), sem("s_x1_")]
        s_w1 = sem("s_w1")
        s_hb = sem("s_hb")
        s_qk1 = sem("s_qk1")
        s_v1 = sem("s_v1")
        s_qe1 = sem("s_qe1")
        s_kbd = sem("s_kbd")
        s_kb0 = sem("s_kb0")
        FIRST_HEADS = 2
        s_ve1 = sem("s_ve1")
        s_rc1 = sem("s_rc1")
        s_on1 = sem("s_on1")
        s_ot1 = sem("s_ot1")
        s_oe1 = sem("s_oe1")
        s_wo1 = sem("s_wo1")
        s_x1 = sem("s_x1")
        s_bo = sem("s_bo")

        def body1(eng_part, b, first, last):
            for c in range(CH):
                m = CH * b + c
                for j in range(HC):
                    n = (CH * HC) * b + HC * c + j
                    i = HC * c + j
                    end = last and i == CH * HC - 1
                    eng_part(b, m, c, j, n, i % 2, i, first, last, end)

        def pe_qkv1(pe, b, m, c, first=False, x1_before=None):
            cols = slice(c * P, (c + 1) * P)
            if not first:
                pe.wait_ge(s_qe1, 2 * m)
            for q in range(KC):
                pe.matmul(F_PS[0][:, 0:T], wq[:, q, cols], hT[:, q, bass.ds(b * T, T)], start=(q == 0),
                          stop=(q == KC - 1), skip_group_check=True)
            for q in range(KC):
                mm = pe.matmul(F_PS[0][:, T:2 * T], wk[:, q, cols], hT[:, q, bass.ds(b * T, T)], start=(q == 0),
                               stop=(q == KC - 1), skip_group_check=True)
            mm.then_inc(s_qk1, 1)
            pe.wait_ge(s_hb, b + 1)
            if not first:
                pe.wait_ge(s_ve1, 2 * m)
            if x1_before is not None:
                pe.wait_ge(s_x1, x1_before)
            for t in range(2):
                for q in range(KC):
                    mm = pe.matmul(F_PS[1][:, t * P:(t + 1) * P], hb[:, q, t * P:(t + 1) * P], wv[:, q, cols],
                                   start=(q == 0), stop=(q == KC - 1), skip_group_check=True)
            mm.then_inc(s_v1, 1)

        def pe_wo1(pe, b, ve_before):
            pe.wait_ge(s_oe1, 2 * b + 2)
            pe.wait_ge(s_ve1, ve_before)
            for t in range(2):
                for c in range(CH):
                    mm = pe.matmul(F_PS[1][:, t * D:(t + 1) * D], o1[:, c, t * P:(t + 1) * P], wo[:, c, :],
                                   start=(c == 0), stop=(c == CH - 1), skip_group_check=True)
            mm.then_inc(s_wo1, 1)

        def pe_s1(pe, n, i, m, c, j, first):
            if first:
                pe.wait_ge(s_kb0, 1)
            elif j == 0 or (isinstance(n, int) and n == FIRST_HEADS):
                pe.wait_ge(s_kbd, m + 1)
            pe_scores(pe, u1, n, i % 2, q1[:, c, :], kbd[:, c, j, :], first)

        def pe_pv1(pe, n, i, m, c, j, nofree):
            if j == 0:
                pe.wait_ge(s_ve1, 2 * m + 2)
                if not nofree:
                    pe.wait_ge(s_oe1, m - 1)
            pe.wait_ge(u1.pt, 2 * n + 1)
            pt, out0, out1 = pt_sb[:, i % 2, :], O_PS[c][:, 0:P], O_PS[c][:, P:2 * P]
            va, vb = vbd[:, c, 0, j * P:(j + 1) * P], vbd[:, c, 1, j * P:(j + 1) * P]
            stop = j == HC - 1
            pe.matmul(out0, pt[:, 0:128], va, start=(j == 0), stop=stop, skip_group_check=True)
            pe.matmul(out1, pt[:, 128:256], va, start=False, stop=False, skip_group_check=True)
            pe.wait_ge(u1.pt, 2 * n + 2)
            pe.matmul(out1, pt[:, 256:384], vb, start=False, stop=stop, skip_group_check=True).then_inc(u1.o, 1)

        def pe_ot1(pe, m, c):
            pe.wait_ge(s_on1, m + 1)
            for t in range(2):
                mm = pe.transpose(O_PS[c][:, 2 * P + t * P:2 * P + (t + 1) * P], on1[:, c, t, :], ident[:, :])
            mm.then_inc(s_ot1, 1)

        def pe_slot1(pe):
            def slot(b, m, c, j, n, k, i, first, last, end):
                if not end:
                    i2 = (i + 1) % (CH * HC)
                    c2, j2 = divmod(i2, HC)
                    pe_s1(pe, n + 1, i2, (m + 1) if j == HC - 1 else m, c2, j2, first and i == 0)
                if not (first and i == 0):
                    i0 = (i - 1) % (CH * HC)
                    c0, j0 = divmod(i0, HC)
                    pe_pv1(pe, n - 1, i0, (m - 1) if j == 0 else m, c0, j0, first)
                if j == 1 and not (last and c == CH - 1):
                    pe_qkv1(pe, b if c == 0 else b + 1, m + 1, 1 - c,
                            x1_before=b if (c == 1 and not first) else None)
                if j == 2 and not (first and c == 0):
                    pe_ot1(pe, m - 1, 1 - c)
                if j == 5 and c == 0 and not first:
                    pe_wo1(pe, b - 1, 4 * b + 4)
                pe_transpose(pe, u1, n, k, first and i < 2, normalised=False)
            return slot

        def act_q1(act, m, c):
            act.wait_ge(s_qk1, m + 1)
            act.activation(q1[:, c, :], F_PS[0][:, 0:T], ACT.Identity, bias=bqs[:, c:c + 1],
                           scale=float(HD1) ** -0.5).then_inc(s_qe1, 1)
            if not (isinstance(m, int) and m == 0):
                act.wait_ge(s_kbd, m)
            act.activation(k1[:, :], F_PS[0][:, T:2 * T], ACT.Identity, bias=vec[:, 2 + c:3 + c]).then_inc(s_qe1, 1)

        def act_v1(act, m, c):
            act.wait_ge(s_v1, m + 1)
            for t in range(2):
                dst = vbd[:, c, t, :].rearrange("p (j y) -> p j y", y=P + HD1)[:, :, 0:HD1]
                act.activation(dst, F_PS[1][:, t * P:(t + 1) * P].rearrange("p (j d) -> p j d", d=HD1),
                               ACT.Copy).then_inc(s_ve1, 1)

        def act_exp1(act, n, k, c, j, first):
            act_exp(act, u1, n, k, first, sums=(sums1[:, c, 1, j:j + 1], sums1[:, c, 0, j:j + 1]))

        def act_o1(act, m, c, projected):
            act.wait_ge(s_ot1, m + 1)
            if projected is not None:
                act.wait_ge(s_wo1, ONE + projected)
            act.activation(o1[:, c, :], O_PS[c][:, T:2 * T], ACT.Identity, bias=vec[:, 4 + c:5 + c]).then_inc(s_oe1, 1)

        def act_slot1(act):
            def slot(b, m, c, j, n, k, i, first, last, end):
                if not end:
                    c2, j2 = divmod((i + 1) % (CH * HC), HC)
                    act_exp1(act, n + 1, 1 - k, c2, j2, first and i == 0)
                if j == 2 and not (last and c == CH - 1):
                    act_q1(act, m + 1, 1 - c)
                if j == 3 and not (last and c == CH - 1):
                    act_v1(act, m + 1, 1 - c)
                if first and c == 1 and j == 5:
                    act_later_weights(act)
                if j == 3 and not (first and c == 0):
                    act_o1(act, m - 1, 1 - c, None if first else (b if c == 1 else b - 1))
            return slot

        def make_kbd(eng, m, c, heads=(0, HC), signal=None):
            lo, hi = heads
            eng.wait_ge(s_qe1, 2 * m + 2)
            eng.tensor_tensor(kbd[:, c, lo:hi, :], k1[:, :].unsqueeze(1).to_broadcast([P, hi - lo, T]),
                              headmask[:, lo:hi].unsqueeze(2).to_broadcast([P, hi - lo, T]), ALU.mult)\
               .then_inc(signal or s_kbd, 1)

        def dve_hb(dve, b):
            dve.tensor_copy(hb[:, :, :], hT[:, :, bass.ds(b * T, T)]).then_inc(s_hb, 1)

        def dve_on1(dve, m, n_done, c):
            dve.wait_ge(u1.ex, 2 * n_done)
            dve.reciprocal(rec1[:, c, :, :], sums1[:, c, :, :]).then_inc(s_rc1, 1)
            dve.wait_ge(s_rc1, m + 1)
            dve.wait_ge(u1.o, n_done)
            dve.tensor_tensor(on1[:, c, :, :].rearrange("p t (j d) -> p (t j) d", d=HD1),
                              O_PS[c][:, 0:2 * P].rearrange("p (g d) -> p g d", d=HD1),
                              rec1[:, c, :, :].rearrange("p t j -> p (t j)").unsqueeze(2)
                              .to_broadcast([P, 2 * HC, HD1]), ALU.mult).then_inc(s_on1, 1)

        def dve_x1(dve, b):
            dve.wait_ge(s_wo1, ONE + b + 1)
            dve.wait_ge(s_bo, 1)
            xs = x[:, bass.ds(2 * b, 2), :].rearrange("p t d -> p (t d)")
            dve.tensor_tensor(xs, xs, F_PS[1][:, :], ALU.add).then_inc(s_x1, 1)

        STATS2 = {(0, 1): 0, (0, 2): 1, (0, 7): 2}
        APPLY2 = {(0, 4): 0, (0, 5): 1, (1, 2): 2}

        def dve_stats2(dve, b):
            dve.wait_ge(s_x1, b + 1)
            for t in range(2 * b, 2 * b + 2):
                dve.bn_stats(st[:, t, :], x[:, t, :]).then_inc(n2.stat, 1)
            for i in range(2):
                t = 2 * b + i
                dve.wait_ge(n2.stat, 4 * b + i + 1)
                dve.bn_aggr(mv[:, t, :], st[:, t, :]).then_inc(n2.stat, 1)

        def pool_stats2(pool, b):
            cols = slice(2 * b, 2 * b + 2)
            pool.wait_ge(n2.stat, 4 * b + 4)
            pool.tensor_tensor(ve[:, cols], mv[:, cols, 1], eps[:, :], ALU.add).then_inc(n2.var, 1)
            pool.wait_ge(n2.var, 2 * b + 1)
            pool.tensor_tensor(rstd[:, cols], ve[:, cols], pw[:, cols], ALU.pow).then_inc(n2.var, 1)

        def dve_apply2(dve, b):
            dve.wait_ge(n2.var, 2 * b + 2)
            for t in range(2 * b, 2 * b + 2):
                dve.tensor_scalar(h[:, t, :], x[:, t, :], mv[:, t, 0:1], rstd[:, t:t + 1], ALU.subtract, ALU.mult)\
                   .then_inc(n2.h, 1)

        def dve_slot1(dve):
            def slot(b, m, c, j, n, k, i, first, last, end):
                if not (first and i == 0):
                    dve_pt(dve, u1, n - 1, 1 - k, first and i < 3)
                if not end:
                    dve_max(dve, u1, n + 1, 1 - k)
                if j == 5 and c == 0 and not last:
                    dve.wait_ge(s_v1, m + 2)
                    dve_hb(dve, b + 1)
                if j == 1 and not (first and c == 0):
                    dve_on1(dve, m - 1, n - 1, 1 - c)
                if j == 6 and c == 0 and not first:
                    dve_x1(dve, b - 1)
                if first and c == 1 and j < 2 * XE - 2:
                    dve_onehot(dve, j)
                if last and (c, j) in STATS2:
                    dve_stats2(dve, STATS2[c, j])
                if last and (c, j) in APPLY2:
                    dve_apply2(dve, APPLY2[c, j])
            return slot

        def pool_slot1(pool):
            def slot(b, m, c, j, n, k, i, first, last, end):
                if j == 3 and not (last and c == CH - 1):
                    make_kbd(pool, m + 1, 1 - c)
                if last and (c, j) in STATS2:
                    pool_stats2(pool, STATS2[c, j])
                if first and c == 1 and j == 5:
                    pool_later_weights(pool)
            return slot

        def run1(eng, slot):
            body1(slot, 0, True, False)
            with eng.Fori(1, B - 1) as b:
                body1(slot, b, False, False)
            body1(slot, B - 1, False, True)

        GX = XE * KC
        NX = N // XB * GX
        XT = XB // P
        LAG = 2
        shared.close()
        zs = tmp("zs", [P, 2, XB])
        gu = tmp("gu", [P, 2, XB])
        guh = tmp("guh", [P, 4, XB], F32R)
        gul = tmp("gul", [P, 4, XB], F32R)
        s_ctx = sem("s_ctx")
        s_tid = sem("s_tid")
        s_oh = sem("s_oh")
        s_z = sem("s_z")
        s_zs = sem("s_zs")
        s_zz = sem("s_zz")
        s_gu = sem("s_gu")
        s_guh = sem("s_guh")
        s_gul = sem("s_gul")
        s_dx = sem("s_dx")
        s_x2 = sem("s_x2")
        s_ch = sem("s_ch")
        s_cl = sem("s_cl")

        def pe_experts(pe):
            def z(v):
                (t, g), bank_ = divmod(v, GX), F_PS[v % 2]
                e, f = divmod(g, KC)
                if v == 1:
                    pe.wait_ge(s_x1, B)
                if v >= 2:
                    pe.wait_ge(s_zz, v - 1)
                ch, tok = slice(f * P, (f + 1) * P), slice(t * XB, (t + 1) * XB)
                for q in range(KC):
                    mm = matmul3(pe, bank_[:, :], (ctxTh[:, e, q, ch], ctxTl[:, e, q, ch]),
                                 (hTh[:, q, tok], hTl[:, q, tok]), q == 0, q == KC - 1)
                mm.then_inc(s_z, 1)

            def down(v):
                t, g = divmod(v, GX)
                e, f = divmod(g, KC)
                pe.wait_ge(s_gul, v + 1)
                if g == 0 and t:
                    pe.wait_ge(s_x2, XT // 2 * t)
                for i in range(XT):
                    tok = slice(i * P, (i + 1) * P)
                    mm = matmul3(pe, O_PS[i // 2][:, i % 2 * D:(i % 2 + 1) * D], (guh[:, v % 4, tok], gul[:, v % 4, tok]),
                                 (ctxTh[:, e, f, :], ctxTl[:, e, f, :]), g == 0 and i % 2 == 0, g == GX - 1, check=True)
                mm.then_inc(s_dx, 1)

            pe.wait_ge(s_cl, 1)
            for v in range(NX):
                if v % GX == 0:
                    pe.wait_ge(n2.hl, 2 * (v // GX + 1))
                z(v)
                if v >= LAG:
                    down(v - LAG)
                if v == LAG + 1:
                    transposes(pe, n2, h, 1)
            transposes(pe, n3r, h, 0)
            for v in range(NX - LAG, NX):
                down(v)

        def act_later_weights(act):
            act.wait_ge(s_ctx, 16)
            act.activation(ctxTh[:, :, :, :], ctxT[:, :, :, :], ACT.Copy).then_inc(s_ch, 1)
            for a in range(2):
                act_w3(act, a, 0)
            act_wv3(act, 0)

        def pool_later_weights(pool):
            pool.wait_ge(s_ch, 1)
            pool.tensor_tensor(ctxTl[:, :, :, :], ctxT[:, :, :, :], ctxTh[:, :, :, :].bitcast(F32), ALU.subtract)\
                .then_inc(s_cl, 1)
            for a in range(2):
                pool_w3(pool, a, a)
            pool_wv3(pool, 0)

        def act_experts(act):
            def high(v):
                act.wait_ge(s_gu, v + 1)
                if v >= 4:
                    act.wait_ge(s_dx, v - 3)
                act.activation(guh[:, v % 4, :], gu[:, v % 2, :], ACT.Copy).then_inc(s_guh, 1)

            for v in range(NX):
                act.wait_ge(s_z, v + 1)
                if v >= 2:
                    act.wait_ge(s_gu, v - 1)
                act.activation(zs[:, v % 2, :], F_PS[v % 2][:, :], ACT.Silu).then_inc(s_zs, 1)
                if v:
                    high(v - 1)
                if v == LAG + 2:
                    hT_scalar(act, n2, 1, high=True)
            high(NX - 1)

        def dve_onehot(dve, step):
            if step == 0:
                dve.wait_ge(s_tid, 16)
                dve.tensor_scalar(onehot[:, 0, :], tid[:, :], float(PER_EXPERT), None, ALU.is_lt).then_inc(s_oh, 1)
            elif step < XE:
                dve.tensor_scalar(onehot[:, step, :], tid[:, :], float(PER_EXPERT * step), None, ALU.is_ge)\
                   .then_inc(s_oh, 1)
            else:
                e = step - XE + 1
                dve.wait_ge(s_oh, step)
                dve.tensor_tensor(onehot[:, e, :], onehot[:, e, :], onehot[:, e + 1, :], ALU.subtract)\
                   .then_inc(s_oh, 1)

        def dve_experts(dve):
            def low(v):
                dve.wait_ge(s_guh, v + 1)
                dve.tensor_tensor(gul[:, v % 4, :], gu[:, v % 2, :], guh[:, v % 4, :].bitcast(F32), ALU.subtract)\
                   .then_inc(s_gul, 1)

            def residual(t):
                dve.wait_ge(s_dx, GX * (t + 1))
                for i in range(XT // 2):
                    first = XT * t + 2 * i
                    xs = x[:, first:first + 2, :].rearrange("p t d -> p (t d)")
                    dve.tensor_tensor(xs, xs, O_PS[i][:, :], ALU.add).then_inc(s_x2, 1)

            for v in range(NX):
                t, g = divmod(v, GX)
                if g == LAG and t:
                    residual(t - 1)
                dve.wait_ge(s_zs, v + 1)
                dve.tensor_tensor(zs[:, v % 2, :], zs[:, v % 2, :], F_PS[v % 2][:, :], ALU.mult).then_inc(s_zz, 1)
                if v:
                    low(v - 1)
                dve.wait_ge(s_zz, v + 1)
                if v >= 2:
                    dve.wait_ge(s_gul, v - 1)
                dve.tensor_tensor(gu[:, v % 2, :], zs[:, v % 2, :], onehot[:, g // KC, t * XB:(t + 1) * XB],
                                  ALU.mult).then_inc(s_gu, 1)
                if v == LAG + 2:
                    hT_vector(dve, n2, 1)
                if v == GX + LAG + 1:
                    dve.wait_ge(s_x2, GT // 2)
                if v in (GX + LAG + 1, GX + LAG + 2):
                    first = 2 * (v - GX - LAG - 1)
                    ln_stats(dve, n3, x, 0, tiles=range(first, first + 2))
                if v >= NX - 2:
                    first = 2 * (v - NX + 2)
                    apply3(dve, 0, range(first, first + 2))
            low(NX - 1)
            hT_vector(dve, n3r, 0, weight=6)
            residual(N // XB - 1)

        def apply3(dve, g, tiles=range(GT)):
            dve.wait_ge(n3.var, 4 * g + 2)
            for t in tiles:
                t += GT * g
                dve.tensor_scalar(h[:, t, :], x[:, t, :], mv[:, t, 0:1], rstd3[:, t:t + 1],
                                  ALU.subtract, ALU.mult).then_inc(n3r.h, 1)

        def pool_norm3(pool, g):
            cols = slice(GT * g, GT * g + GT)
            pool.wait_ge(n3.stat, 2 * GT * (g + 1))
            for i, (v_, r_, k1_, k0_) in enumerate(((ve3, rstd3, 1.0 + RMS_EPS, LN_EPS * RMS_EPS), (ve, rstd, 1.0, LN_EPS))):
                pool.tensor_scalar(v_[:, cols], mv[:, cols, 1], k1_, k0_, ALU.mult, ALU.add).then_inc(n3.var, 1)
                pool.wait_ge(n3.var, 4 * g + 2 * i + 1)
                pool.tensor_tensor(r_[:, cols], v_[:, cols], pw[:, cols], ALU.pow).then_inc(n3.var, 1)
            pool.wait_ge(n3.var, 4 * g + 4)
            for t in range(GT * g, GT * g + GT):
                pool.tensor_scalar(acc[:, t, :], x[:, t, :], mv[:, t, 0:1], rstd[:, t:t + 1],
                                   ALU.subtract, ALU.mult).then_inc(n3.h, 1)

        shared.close()
        q3 = tmp("q3", [P, 2, N])
        k3 = tmp("k3", [P, 2, N])
        v3 = tmp("v3", [P, 3, NT, HD3])
        o3h = tmp("o3h", [P, 2, N], F32R)
        o3l = tmp("o3l", [P, 2, N], F32R)
        u3 = Unit("u3")
        s_w3 = [sem("s_w3a"), sem("s_w3b")]
        s_wo3 = sem("s_wo3")
        s_wv3 = sem("s_wv3")
        s_wvh = sem("s_wvh")
        s_wvl = sem("s_wvl")
        s_vb = sem("s_vb")
        s_f3 = sem("s_f3")
        s_fe3 = sem("s_fe3")
        s_w3h = sem("s_w3h")
        s_w3l = sem("s_w3l")
        s_woh = sem("s_woh")
        s_wol = sem("s_wol")
        s_oe3 = sem("s_oe3")
        s_ol3 = sem("s_ol3")
        s_wd3 = sem("s_wd3")
        s_acc = sem("s_acc")

        Q_, K_, V_ = range(3)
        BEFORE, PER_PAIR = 8, 12
        FILL = {(0, 0): (0, ((Q_, 0), (Q_, 1))), (0, 1): (2, ((K_, 0), (K_, 1))),
                (1, 0): (4, ((Q_, 0), (Q_, 1))), (1, 1): (6, ((K_, 0), (K_, 1))),
                (1, 2): (8, ((V_, 0), (V_, 1))), (1, 3): (10, ((V_, 2), (V_, 3)))}

        def fill3(eng, bank3, p, a, b, acc_before=None):
            k, banks = FILL[a, b]
            for i, (kind, part) in enumerate(banks):
                if acc_before is not None:
                    eng.wait_ge(s_acc, acc_before - 1 + i)
                bank3(eng, BEFORE + PER_PAIR * p + k + i, F_PS[i], 1 - a, kind, part)

        def pe_bank3(pe, f, ps, a, kind, i):
            if not (isinstance(f, int) and f < 2):
                pe.wait_ge(s_fe3, f - 1)
            for q in range(KC):
                if kind != V_:
                    tok = slice(i * 512, (i + 1) * 512)
                    mm = matmul3(pe, ps[:, :], (w3h[:, a, kind, q, :], w3l[:, a, kind, q, :]),
                                 (hTh[:, q, tok], hTl[:, q, tok]), q == 0, q == KC - 1)
                else:
                    for t in range(2):
                        tok = slice((2 * i + t) * P, (2 * i + t + 1) * P)
                        mm = matmul3(pe, ps[:, t * 2 * HD3:(t + 1) * 2 * HD3], (hTh[:, q, tok], hTl[:, q, tok]),
                                     (wv3h[:, q, :], wv3l[:, q, :]), q == 0 and t == 0, q == KC - 1, check=True)
            mm.then_inc(s_f3, 1)

        def act_w3(act, a, load, after=None):
            act.wait_ge(s_w3[a], 16 * (load + 1))
            if after is not None:
                act.wait_ge(s_f3, after)
            act.activation(w3h[:, a, :, :, :], w3[:, a, :, :, :], ACT.Copy).then_inc(s_w3h, 1)

        def act_wv3(act, p, after=None):
            act.wait_ge(s_wv3, 16 * (p + 1))
            if after is not None:
                act.wait_ge(s_f3, after)
            act.activation(wv3h[:, :, :], wv3[:, :, :], ACT.Copy).then_inc(s_wvh, 1)

        def pool_wv3(pool, p):
            pool.wait_ge(s_wvh, p + 1)
            pool.tensor_tensor(wv3l[:, :, :], wv3[:, :, :], wv3h[:, :, :].bitcast(F32), ALU.subtract)\
                .then_inc(s_wvl, 1)

        def pool_w3(pool, head, a):
            pool.wait_ge(s_w3h, head + 1)
            pool.tensor_tensor(w3l[:, a, :, :, :], w3[:, a, :, :, :], w3h[:, a, :, :, :].bitcast(F32),
                               ALU.subtract).then_inc(s_w3l, 1)

        def act_wo3(act, p, first):
            act.wait_ge(s_wo3, 16 * (p + 1))
            if not first:
                act.wait_ge(s_wd3, 4 * p)
            act.activation(wo3h[:, :, :], wo3[:, :, :], ACT.Copy).then_inc(s_woh, 1)

        def pool_wo3(pool, p):
            pool.wait_ge(s_woh, p + 1)
            pool.tensor_tensor(wo3l[:, :, :], wo3[:, :, :], wo3h[:, :, :].bitcast(F32), ALU.subtract)\
                .then_inc(s_wol, 1)

        def act_bank3(act, f, ps, a, kind, i):
            act.wait_ge(s_f3, f + 1)
            if kind == V_:
                act.activation(v3[:, 0:2, 2 * i:2 * i + 2, :], ps[:, :].rearrange("p (t a d) -> p a t d", t=2, a=2),
                               ACT.Copy).then_inc(s_fe3, 1)
            else:
                act.activation((q3, k3)[kind][:, a, i * 512:(i + 1) * 512], ps[:, :], ACT.Copy,
                               scale=(float(QHD) ** -0.5 if kind == Q_ else 1.0)).then_inc(s_fe3, 1)

        def act_vb(act, p, first):
            if not first:
                act.wait_ge(u3.o, 8 * p)
            act.activation(v3[:, 2, :, :], v3[:, 1, :, :], ACT.Copy).then_inc(s_vb, 1)

        def first3(eng, bank3, i):
            for k, (kind, part) in enumerate(((Q_, i), (K_, i), (V_, 2 * i), (V_, 2 * i + 1))):
                bank3(eng, 4 * i + k, F_PS[k % 2], 0, kind, part)

        def pe_wo3(pe, p, fe_before, banks=range(4)):
            pe.wait_ge(s_wol, p + 1)
            pe.wait_ge(s_ol3, 4 * (p + 1))
            for g in banks:
                if g < 2:
                    pe.wait_ge(s_fe3, fe_before - 1 + g)
                else:
                    pe.wait_ge(s_acc, 4 * p + g - 1)
                for t in range(2):
                    for a in range(2):
                        tok = slice((2 * g + t) * P, (2 * g + t + 1) * P)
                        mm = matmul3(pe, F_PS[g % 2][:, t * D:(t + 1) * D], (o3h[:, a, tok], o3l[:, a, tok]),
                                     (wo3h[:, a, :], wo3l[:, a, :]), a == 0, a == 1, check=True)
                mm.then_inc(s_wd3, 1)

        def dve_wo3(dve, p, banks=range(4)):
            for g in banks:
                dve.wait_ge(s_wd3, 4 * p + g + 1)
                dst = acc[:, 2 * g:2 * g + 2, :].rearrange("p t d -> p (t d)")
                dve.tensor_tensor(dst, dst, F_PS[g % 2][:, :], ALU.add).then_inc(s_acc, 1)

        def body3(slot, p, first, last):
            for a in range(2):
                for b in range(B):
                    u = 4 * a + b
                    slot(p, a, b, u, first, last, last and u == 7)

        def pe_slot3(pe):
            def slot(p, a, b, u, first, last, end):
                n = 8 * p + u
                if not end:
                    a2, b2 = divmod((u + 1) % 8, 4)
                    if b2 == 0:
                        pe.wait_ge(s_fe3, BEFORE + PER_PAIR * p + (4 if a2 else 8))
                    pe_scores(pe, u3, n + 1, (u + 1) % 2, q3[:, a2, b2 * T:(b2 + 1) * T],
                              k3[:, a2, b2 * T:(b2 + 1) * T], first and u == 0)
                if not (first and u == 0):
                    a0, b0 = divmod((u - 1) % 8, 4)
                    head0 = 2 * p + (u - 1) // 4
                    pe_pv3(pe, n - 1, p if u else p - 1, a0, b0, head0, first and 0 < u <= 4)
                if (a, b) in wo_slots(last) and not first:
                    pe_wo3(pe, p - 1, BEFORE + PER_PAIR * p + 4, wo_slots(last)[a, b])
                if (a, b) in FILL and not (last and a == 1):
                    if b == 0:
                        pe.wait_ge(s_w3l, 2 * p + a + 2)
                    if (a, b) == (1, 2):
                        pe.wait_ge(s_wvl, p + 2)
                    fill3(pe, pe_bank3, p, a, b, acc_before=(4 * p if (a == 1 and b == 0 and not first) else None))
                pe_transpose(pe, u3, n, u % 2, first and u < 2)
            return slot

        def pe_pv3(pe, n, p, a, b, head, nofree):
            if b == 0 and a == 0:
                pe.wait_ge(s_fe3, BEFORE + PER_PAIR * p)
            if b == 0 and a == 1:
                pe.wait_ge(s_vb, p + 1)
            if b % 2 == 0 and not nofree:
                pe.wait_ge(s_ol3, 2 * head + b // 2 - 1)
            o_ps = O_PS[b // 2][:, (b % 2) * T:(b % 2 + 1) * T]
            pe_pv(pe, u3, n, (n_par(b)), o_ps, v3[:, 2 * a, 2 * b, :], v3[:, 2 * a, 2 * b + 1, :])

        def n_par(b):
            return b % 2

        def wo_slots(last):
            if last:
                return {(0, 2): range(0, 1), (0, 3): range(1, 2), (1, 0): range(2, 3), (1, 1): range(3, 4)}
            return {(0, 2): range(0, 2), (0, 3): range(2, 4)}

        def outputs3(p, a, b, first, last):
            if a == 0:
                return [(2 * p - 1, 1, 1)] if b == 0 and not first else []
            if last:
                return {0: [(2 * p, 0, 0)], 2: [(2 * p, 0, 1), (2 * p + 1, 1, 0)]}.get(b, [])
            return {0: [(2 * p, 0, 0), (2 * p, 0, 1)], 2: [(2 * p + 1, 1, 0)]}.get(b, [])

        def act_o3(act, head, a, i):
            act.wait_ge(u3.o, 4 * head + 2 * i + 2)
            act.activation(o3h[:, a, i * 512:(i + 1) * 512], O_PS[i][:, :], ACT.Copy).then_inc(s_oe3, 1)

        def dve_o3(dve, head, a, i):
            dve.wait_ge(s_oe3, 2 * head + i + 1)
            cols = slice(i * 512, (i + 1) * 512)
            dve.tensor_tensor(o3l[:, a, cols], O_PS[i][:, :], o3h[:, a, cols].bitcast(F32), ALU.subtract)\
               .then_inc(s_ol3, 1)

        def act_slot3(act):
            def slot(p, a, b, u, first, last, end):
                n = 8 * p + u
                if not end:
                    act_exp(act, u3, n + 1, (u + 1) % 2, first and u == 0)
                for head, a2, half in outputs3(p, a, b, first, last):
                    if last and (a, b) == (1, 2):
                        act.wait_ge(s_wd3, 4 * p)
                    act_o3(act, head, a2, half)
                if (a, b) in FILL and not (last and a == 1):
                    fill3(act, act_bank3, p, a, b)
                if (a, b) == (0, 1):
                    act_vb(act, p, first)
                if (a, b) == (0, 2) and not last:
                    act_wv3(act, p + 1, after=BEFORE + PER_PAIR * p)
                if b == 3 and not last:
                    act_w3(act, a, p + 1, after=PER_PAIR * p + (12 if a else 4))
                if a == 1 and b == 2:
                    act_wo3(act, p, first)
            return slot

        def dve_slot3(dve):
            def slot(p, a, b, u, first, last, end):
                n = 8 * p + u
                if not (first and u == 0):
                    dve_pt(dve, u3, n - 1, (u + 1) % 2, first and u < 3)
                if not end:
                    dve_max(dve, u3, n + 1, (u + 1) % 2)
                    dve_recip(dve, u3, n + 1, (u + 1) % 2)
                for head, a2, half in outputs3(p, a, b, first, last):
                    dve_o3(dve, head, a2, half)
                if (a, b) in wo_slots(last) and not first:
                    dve_wo3(dve, p - 1, wo_slots(last)[a, b])
            return slot

        def pool_slot3(pool):
            def slot(p, a, b, u, first, last, end):
                if not end:
                    pool_normalise(pool, u3, 8 * p + u + 1, (u + 1) % 2)
                if b == 3 and not last:
                    pool_w3(pool, 2 * p + a + 2, a)
                if (a, b) == (0, 2) and not last:
                    pool_wv3(pool, p + 1)
                if a == 1 and b == 2:
                    pool_wo3(pool, p)
            return slot

        def run3(eng, slot):
            body3(slot, 0, True, False)
            with eng.Fori(1, PAIRS - 1) as p:
                body3(slot, p, False, False)
            body3(slot, PAIRS - 1, False, True)

        shared.close()
        lg = tmp("lg", [P, NT, E3])
        mx = tmp("mx", [P, NT])
        sums = tmp("sums", [P, NT])
        pr = tmp("pr", [P, NT, E3])
        top = tmp("top", [P, NT, 8])
        left = tmp("left", [P, NT, E3])
        wr = tmp("wr", [32, N])
        wb = tmp("wb", [P, WSLOTS, N])
        gs = tmp("gs", [P, 2, HALF])
        am = tmp("am", [P, 2, HALF])
        amh = tmp("amh", [P, 2, HALF], F32R)
        aml = tmp("aml", [P, 2, HALF], F32R)
        yT = tmp("yT", [P, KC, N])
        by_expert = nc.dram_tensor("by_expert", [32, N], F32, kind="Internal").ap()
        by_group = nc.dram_tensor("by_group", [NCH * P // GROUP, N], F32, kind="Internal").ap()
        G_PS, U_PS, Y_PS = bank[0:2], bank[2:4], bank[4:8]
        s_gate = sem("s_gate")
        s_gz = sem("s_gz")
        s_lg = sem("s_lg")
        s_rt = sem("s_rt")
        s_rx = sem("s_rx")
        s_wt = sem("s_wt")
        s_wr = sem("s_wr")
        s_be = sem("s_be")
        s_bg = sem("s_bg")
        s_wb = [sem(f"s_wb{i}") for i in range(WSLOTS)]
        s_wm = [sem(f"s_wm{i}") for i in range(WSLOTS)]
        s_wh = sem("s_wh")
        s_wl = sem("s_wl")
        s_gu3 = sem("s_gu3")
        s_gs = sem("s_gs")
        s_gm = sem("s_gm")
        s_am = sem("s_am")
        s_ah = sem("s_ah")
        s_al = sem("s_al")
        s_dn = sem("s_dn")
        s_yT = sem("s_yT")
        s_yt = sem("s_yt")
        s_fin = sem("s_fin")
        s_one = sem("s_one")
        s_xh = sem("s_xh")
        s_out = sem("s_out")
        TURNS = (NCH - 1) // WSLOTS
        ALONE = WSLOTS
        assert NCH == TURNS * WSLOTS + 1 and ALONE * P <= SHARED

        def channels(eng, work):
            with eng.Fori(1, TURNS) as i:
                for r in range(WSLOTS):
                    work(WSLOTS * i + r, r, i, False)
            work(NCH - 1, 0, TURNS, True)

        def sp_channels(sp):
            def weights(c, r):
                sp.dma_start(wm[:, r, :, :].rearrange("p s n -> p (s n)"),
                             moe_in[bass.ds(c, 1)].rearrange("a p n -> (a p) n")).then_inc(s_wm[r], 16)

            def routing(c, r):
                n = P // GROUP
                sp.dma_start(wb[:, r, :], by_group[bass.ds(c * n, n), :].unsqueeze(1).to_broadcast([n, GROUP, N]))\
                  .then_inc(s_wb[r], 16)

            for c in range(WSLOTS):
                weights(c, c)
            for c in range(ALONE):
                sp.wait_ge(s_wl, 2 * (c + 1))
                weights(c + WSLOTS, c)
            sp.wait_ge(s_wr, 1)
            sp.dma_start(by_expert[0:E3 + 1, :], wr[0:E3 + 1, :]).then_inc(s_be, 16)
            sp.wait_ge(s_be, 16)
            for c in range(ALONE, ALONE + WSLOTS):
                assert max(c * P, SHARED) < SHARED + INNER and (c + 1) * P <= SHARED + INNER
                rows = max(0, SHARED - c * P)
                sp.dma_start(wb[rows:P, c % WSLOTS, :], by_expert[0:1, :].to_broadcast([P - rows, N]))\
                  .then_inc(s_wb[c % WSLOTS], 16)
            n, first = INNER // GROUP, SHARED // GROUP
            end = first + E3 * n
            sp.dma_start(by_group[first:end, :].rearrange("(e g) t -> e g t", g=n),
                         by_expert[0:E3, :].unsqueeze(1).to_broadcast([E3, n, N])).then_inc(s_bg, 16)
            for lo, hi in ((0, first), (end, NCH * P // GROUP)):
                sp.dma_start(by_group[lo:hi, :], by_expert[E3:E3 + 1, :].to_broadcast([hi - lo, N])).then_inc(s_bg, 16)
            sp.wait_ge(s_bg, 48)

            def refill(c, r):
                sp.wait_ge(s_wl, 2 * (c + 1))
                weights(c + WSLOTS, r)
                sp.wait_ge(s_am, AM0 + 2 * (c + 1))
                routing(c + WSLOTS, r)
            with sp.Fori(1, TURNS - 1) as i:
                for r in range(WSLOTS):
                    refill(WSLOTS * i + r, r)
            refill(NCH - 1 - WSLOTS, 0)

        def act_split(act, c, r, load, part):
            if part == 0:
                act.wait_ge(s_wm[r], 16 * load)
                cols = slice(0, 4)
            else:
                if not (isinstance(c, int) and c == 0):
                    act.wait_ge(s_dn, DN0 + 2 * (c - 1))
                cols = slice(4, 6)
            act.activation(wmh[:, r, cols, :], wm[:, r, cols, :], ACT.Copy).then_inc(s_wh, 1)

        def pool_split(pool, c, r):
            for part, cols in enumerate((slice(0, 4), slice(4, 6))):
                pool.wait_ge(s_wh, 2 * c + part + 1)
                pool.tensor_tensor(wml[:, r, cols, :], wm[:, r, cols, :], wmh[:, r, cols, :].bitcast(F32),
                                   ALU.subtract).then_inc(s_wl, 1)

        def pool_channels(pool):
            for c in range(1, ALONE):
                pool_split(pool, c, c)
            channels(pool, lambda c, r, i, last: pool_split(pool, c, r))

        def act_channels(act):
            def half(c, r, hf):
                v = 2 * c + hf
                act.wait_ge(s_gu3, v + 1)
                act.wait_ge(s_am, AM0 + v - 1)
                act.activation(gs[:, hf, :], G_PS[hf][:, :], ACT.Silu).then_inc(s_gs, 1)

            def high(c, r, hf):
                v = 2 * c + hf
                act.wait_ge(s_am, AM0 + v + 1)
                act.wait_ge(s_dn, DN0 + v - 1)
                act.activation(amh[:, hf, :], am[:, hf, :], ACT.Copy).then_inc(s_ah, 1)

            def work(c, r, i, last):
                nxt = (1 - r, i + 1 + r)
                half(c, r, 0)
                if isinstance(c, int) and c == 0:
                    act.wait_ge(s_rt, 4)
                    act.activation(pr[:, :, :], lg[:, :, :], ACT.Exp).then_inc(s_rx, 1)
                if not last:
                    act_split(act, c + 1, *nxt, 0)
                high(c, r, 0)
                half(c, r, 1)
                high(c, r, 1)
                if not last:
                    act_split(act, c + 1, *nxt, 1)
            for c in range(ALONE):
                work(c, c, 0, False)
            channels(act, work)
            for hf in range(2):
                act.wait_ge(s_dn, DN0 + 2 * (NCH - 1) + hf + 1)
                for q in range(KC):
                    act.activation(yT[:, q, hf * HALF:(hf + 1) * HALF], Y_PS[2 * hf + q][:, :],
                                   ACT.Copy).then_inc(s_yT, 1)

        def pe_gate_up(pe, c, r, hf):
            v = 2 * c + hf
            pe.wait_ge(s_wl, 2 * c + 1)
            if isinstance(c, int) and c == 0:
                pe.wait_ge(n4.hl, 2 * hf + 2)
            if not isinstance(v, int) or v >= 2 + 2 * ALONE:
                pe.wait_ge(s_gm, v - 1 - 2 * ALONE)
            elif v >= 2:
                pe.wait_ge(s_am, AM0 + v - 1)
            cols = slice(hf * HALF, (hf + 1) * HALF)
            for ps, w in ((G_PS[hf], 0), (U_PS[hf], 2)):
                for q in range(KC):
                    mm = matmul3(pe, ps[:, :], (wmh[:, r, w + q, :], wml[:, r, w + q, :]),
                                 (hTh[:, q, cols], hTl[:, q, cols]), q == 0, q == KC - 1)
            mm.then_inc(s_gu3, 1)

        def pe_down(pe, c, r, hf):
            pe.wait_ge(s_al, 2 * c + hf + 1)
            pe.wait_ge(s_wl, 2 * c + 2)
            for q in range(KC):
                mm = matmul3(pe, Y_PS[2 * hf + q][:, :], (wmh[:, r, 4 + q, :], wml[:, r, 4 + q, :]),
                             (amh[:, hf, :], aml[:, hf, :]), False, False, check=True)
            mm.then_inc(s_dn, 1)

        def pe_channels(pe):
            pe.wait_ge(s_rt, 4)
            for q in range(4):
                pe.matmul(Y_PS[q][:, :], zb[:, 0:P], zb[:, :], start=True, stop=False, skip_group_check=True)
            for hf in range(2):
                pe_gate_up(pe, 1, 1, hf)
                pe_down(pe, 0, 0, hf)
            pe_routing_transposes(pe)
            pe_down(pe, 1, 1, 0)
            pe.wait_ge(s_wr, 1)
            for hf in range(2):
                pe_gate_up(pe, 2, 0, hf)
            pe_down(pe, 1, 1, 1)

            def work(c, r, i, last):
                for hf in range(2):
                    if not last:
                        pe_gate_up(pe, c + 1, 1 - r, hf)
                    pe_down(pe, c, r, hf)
            channels(pe, work)
            pe.wait_ge(s_gm, 2 * (NCH - ALONE))
            for g in range(4):
                pe.wait_ge(s_yT, KC * (g // 2 + 1))
                for t in range(2):
                    for q in range(KC):
                        mm = pe.transpose(bank[g][:, t * D + q * P:t * D + (q + 1) * P],
                                          yT[:, q, (2 * g + t) * P:(2 * g + t + 1) * P], ident[:, :])
                mm.then_inc(s_yt, 1)

        def dve_parts(dve, v, hf):
            dve.wait_ge(s_ah, v + 1)
            dve.wait_ge(s_dn, DN0 + v - 1)
            dve.tensor_tensor(aml[:, hf, :], am[:, hf, :], amh[:, hf, :].bitcast(F32), ALU.subtract).then_inc(s_al, 1)

        def dve_alone(dve, c, hf):
            v = 2 * c + hf
            dve.wait_ge(s_gs, v + 1)
            if v >= 2:
                dve.wait_ge(s_al, v - 1)
            dve.tensor_tensor(am[:, hf, :], gs[:, hf, :], U_PS[hf][:, :], ALU.mult).then_inc(s_am, 1)
            dve_parts(dve, v, hf)

        def dve_channels(dve):
            def work(c, r, i, last):
                for hf in range(2):
                    v = 2 * c + hf
                    dve.wait_ge(s_gs, v + 1)
                    dve.tensor_tensor(gs[:, hf, :], gs[:, hf, :], U_PS[hf][:, :], ALU.mult).then_inc(s_gm, 1)
                    dve.wait_ge(s_gm, v + 1 - 2 * ALONE)
                    if hf == 0:
                        dve.wait_ge(s_wb[r], 16 * i)
                    dve.tensor_tensor(am[:, hf, :], gs[:, hf, :], wb[:, r, hf * HALF:(hf + 1) * HALF],
                                      ALU.mult).then_inc(s_am, 1)
                    dve_parts(dve, v, hf)
            channels(dve, work)
            dve.wait_ge(s_xh, 1)
            for g in range(4):
                dve.wait_ge(s_yt, g + 1)
                xs = x[:, 2 * g:2 * g + 2, :].rearrange("p t d -> p (t d)")
                dve.tensor_tensor(xs, xs, bank[g][:, :], ALU.add).then_inc(s_fin, 1)

        LG_PS = (bank[4], bank[5])
        WT_PS = (bank[0], bank[2])

        def pe_logits(pe, g):
            pe.wait_ge(n4.hT, 2 * (g + 1))
            for j in range(GT):
                t = GT * g + j
                for q in range(KC):
                    mm = pe.matmul(LG_PS[g][:, j * P:(j + 1) * P], hT[:, q, t * P:(t + 1) * P], gate[:, q, :],
                                   start=(q == 0), stop=(q == KC - 1), skip_group_check=True)
            mm.then_inc(s_lg, 1)

        def pe_routing_transposes(pe):
            pe.wait_ge(s_rt, 4 + ROUTED)
            pe.wait_ge(s_am, AM0 + 2 * ALONE - 1)
            for t in range(NT):
                mm = pe.transpose(WT_PS[t // GT][0:32, (t % GT) * P:(t % GT + 1) * P], wt[:, t, :], ident[:, :])
            mm.then_inc(s_wt, 1)

        ROUTED = 3 + NT + 1 + NT + 4

        def wide(a, tiles=NT):
            return a.unsqueeze(2).to_broadcast([P, tiles, E3])

        def dve_logits(dve, g):
            tiles = slice(GT * g, GT * g + GT)
            logits = LG_PS[g][:, :].rearrange("p (t e) -> p t e", e=P)[:, :, 0:E3]
            dve.wait_ge(s_lg, g + 1)
            dve.tensor_reduce(mx[:, tiles], logits, AX.X, ALU.max).then_inc(s_rt, 1)
            dve.wait_ge(s_rt, 2 * g + 1)
            dve.tensor_tensor(lg[:, tiles, :], logits, wide(mx[:, tiles], GT), ALU.subtract).then_inc(s_rt, 1)

        def dve_probs(dve):
            dve.wait_ge(s_rx, 1)
            dve.tensor_reduce(sums[:, :], pr[:, :, :], AX.X, ALU.add).then_inc(s_rt, 1)
            dve.wait_ge(s_rt, 5)
            dve.reciprocal(sums[:, :], sums[:, :]).then_inc(s_rt, 1)
            dve.wait_ge(s_rt, 6)
            dve.tensor_tensor(pr[:, :, :], pr[:, :, :], wide(sums[:, :]), ALU.mult).then_inc(s_rt, 1)
            dve.wait_ge(s_rt, 7)
            for t in range(NT):
                dve.max(top[:, t, :], pr[:, t, :]).then_inc(s_rt, 1)

        def dve_top(dve):
            dve.wait_ge(s_rt, 7 + NT)
            dve.memset(top[:, :, TOPK:8], -2.0).then_inc(s_rt, 1)
            dve.wait_ge(s_rt, 8 + NT)
            for t in range(NT):
                dve.match_replace(left[:, t, :], top[:, t, :], pr[:, t, :], -1.0).then_inc(s_rt, 1)

        def dve_weights(dve):
            dve.wait_ge(s_rt, 8 + 2 * NT)
            chosen = wt[:, :, 0:E3]
            dve.scalar_tensor_tensor(chosen, left[:, :, :], 0.0, pr[:, :, :], ALU.is_lt, ALU.mult).then_inc(s_rt, 1)
            dve.wait_ge(s_rt, 9 + 2 * NT)
            dve.tensor_reduce(sums[:, :], chosen, AX.X, ALU.add).then_inc(s_rt, 1)
            dve.wait_ge(s_rt, 10 + 2 * NT)
            dve.reciprocal(sums[:, :], sums[:, :]).then_inc(s_rt, 1)
            dve.wait_ge(s_rt, 11 + 2 * NT)
            dve.tensor_tensor(chosen, chosen, wide(sums[:, :]), ALU.mult).then_inc(s_rt, 1)

        def dve_by_expert(dve):
            dve.wait_ge(s_wt, 1)
            dve.tensor_copy(wr[:, 0:512], WT_PS[0][0:32, :]).then_inc(s_rt, 1)
            dve.wait_ge(s_rt, 13 + 2 * NT)
            dve.tensor_copy(wr[:, 512:1024], WT_PS[1][0:32, :]).then_inc(s_wr, 1)

        @block.sync
        def _(sp):
            for t in range(4):
                sp.dma_start(x[:, 2 * t:2 * t + 2, :],
                             x_in[t * 256:(t + 1) * 256, :].rearrange("(t p) d -> p t d", p=P)).then_inc(s_x[t // 2], 16)
            for dst, src in ((wq, wqT_in), (wk, wkT_in), (wv, wvT_in), (wo, woT_in)):
                sp.dma_start(dst[:, :, :], src.rearrange("(q p) n -> p q n", p=P)).then_inc(s_w1, 16)
            sp.dma_start(tid[:, :], tok_in.partition_broadcast(P)).then_inc(s_tid, 16)
            sp.dma_start(ctxT[:, :, :, :].rearrange("p e q n -> p (e q) n"),
                         ctxT_in.rearrange("(g p) n -> p g n", p=P)).then_inc(s_ctx, 16)
            sp.wait_ge(s_gz, 1)
            sp.dma_start(gate[:, :, 0:E3], gate_in.rearrange("(q p) n -> p q n", p=P)).then_inc(s_gate, 16)
            for a in range(2):
                sp.dma_start(w3[:, a, :, :, :].rearrange("p s q n -> p (s q n)"), ffn_qk_in[a]).then_inc(s_w3[a], 16)
            sp.dma_start(wv3[:, :, :], ffn_v_in[0]).then_inc(s_wv3, 16)
            sp.dma_start(wo3[:, :, :], ffn_o_in[0]).then_inc(s_wo3, 16)
            with sp.Fori(0, PAIRS - 1) as p:
                for a in range(2):
                    sp.wait_ge(s_w3l, 2 * p + a + 1)
                    sp.dma_start(w3[:, a, :, :, :].rearrange("p s q n -> p (s q n)"),
                                 ffn_qk_in[bass.ds(2 * p + 2 + a, 1)].rearrange("a p n -> (a p) n"))\
                      .then_inc(s_w3[a], 16)
                sp.wait_ge(s_wvl, p + 1)
                sp.dma_start(wv3[:, :, :].rearrange("p q n -> p (q n)"),
                             ffn_v_in[bass.ds(p + 1, 1)].rearrange("a p q n -> (a p) (q n)")).then_inc(s_wv3, 16)
                sp.wait_ge(s_wol, p + 1)
                sp.dma_start(wo3[:, :, :].rearrange("p a n -> p (a n)"),
                             ffn_o_in[bass.ds(p + 1, 1)].rearrange("a p b n -> (a p) (b n)")).then_inc(s_wo3, 16)
            sp_channels(sp)
            for g in range(4):
                sp.wait_ge(s_fin, g + 1)
                sp.dma_start(out[g * 256:(g + 1) * 256, :].rearrange("(t p) d -> p t d", p=P),
                             x[:, 2 * g:2 * g + 2, :]).then_inc(s_out, 16)
            sp.wait_ge(s_out, 64)

        @block.gpsimd
        def _(pool):
            pool.memset(pw[:, :], -0.5).then_inc(s_init, 1)
            pool.memset(vbd[:, :, :, :], 0.0).then_inc(s_init, 1)
            pool.wait_ge(s_init, 1)
            pool.memset(eps[:, :], LN_EPS).then_inc(s_init, 1)
            for g in range(2):
                ln_gpsimd(pool, n1, g)
            pool.memset(zb[:, :], 0.0).then_inc(s_init, 1)
            for i, (s, n) in enumerate(((s_wo1, ONE), (s_am, AM0), (s_dn, DN0))):
                pool.memset(credit[:, i:i + 1], 0.0).then_inc(s, n)
            pool.memset(gate[:, :, :], 0.0).then_inc(s_gz, 1)
            pool.memset(wt[:, :, :], 0.0).then_inc(s_init, 1)
            pool.wait_ge(s_init, 5)
            pool.memset(wt[:, :, E3:E3 + 1], 1.0).then_inc(s_init, 1)
            pool.wait_ge(s_const, 16 * 5)
            pool.wait_ge(n1.h, NT)
            pool.tensor_tensor(x[:, :, :], x[:, :, :], bo[:, :].unsqueeze(1).to_broadcast([P, NT, D]),
                               ALU.add).then_inc(s_bo, 1)
            run1(pool, pool_slot1(pool))
            pool_stats2(pool, B - 1)
            for g in range(2):
                pool_norm3(pool, g)
            pool_normalise(pool, u3, 0, 0)
            run3(pool, pool_slot3(pool))
            pool_split(pool, 0, 0)
            for g in range(2):
                rms_gpsimd(pool, n4, g)
            pool.memset(wb[0:SHARED - ALONE * P, ALONE % WSLOTS, :], 1.0).then_inc(s_one, 1)
            pool.tensor_tensor(x[:, :, :], x[:, :, :], acc[:, :, :], ALU.add).then_inc(s_xh, 1)
            pool_channels(pool)

        @block.scalar
        def _(act):
            for dst, src in ((ident, ident_in), (tri, tri_in), (headmask, headmask_in), (vec, vec_in)):
                act.dma_start(dst[:, :], src).then_inc(s_const, 16)
            act.dma_start(bo[:, :], bo_in.partition_broadcast(P)).then_inc(s_const, 16)
            act.wait_ge(s_const, 16 * 5)
            act.activation(bqs[:, :], vec[:, 0:2], ACT.Copy, scale=float(HD1) ** -0.5).then_inc(s_castc, 1)
            act.wait_ge(s_castc, 3)
            hT_scalar(act, n1, 0)
            act.wait_ge(s_init, 2)
            act_q1(act, 0, 0)
            act_v1(act, 0, 0)
            hT_scalar(act, n1, 1)
            act_exp1(act, 0, 0, 0, 0, True)
            run1(act, act_slot1(act))
            hT_scalar(act, n2, 0, high=True)
            act_o1(act, CH * B - 1, CH - 1, B - 1)
            act_experts(act)
            hT_scalar(act, n3r, 0, weight=6, high=True)
            first3(act, act_bank3, 0)
            hT_scalar(act, n3r, 1, weight=6, high=True)
            act_exp(act, u3, 0, 0, True)
            first3(act, act_bank3, 1)
            run3(act, act_slot3(act))
            for part in range(2):
                act_split(act, 0, 0, 1, part)
            act_o3(act, H3 - 1, 1, 1)
            for g in range(2):
                rms_scalar(act, n4, acc, g, s_acc, lambda t: 4 * (PAIRS - 1) + t // 2 + 1)
            for g in range(2):
                hT_scalar(act, n4, g, weight=8, high=True)
                hT_scalar(act, n4, g, weight=8)
            act_channels(act)

        @block.tensor
        def _(pe):
            pe.wait_ge(s_const, 16 * 5)
            transposes(pe, n1, h, 0)
            pe.wait_ge(s_w1, 64)
            pe.wait_ge(n1.hT, 2)
            pe_qkv1(pe, 0, 0, 0, first=True)
            transposes(pe, n1, h, 1)
            pe.wait_ge(s_castc, 3)
            pe_s1(pe, 0, 0, 0, 0, 0, True)
            pe.wait_ge(n1.hT, 4)
            run1(pe, pe_slot1(pe))
            pe_pv1(pe, CH * HC * B - 1, CH * HC - 1, CH * B - 1, CH - 1, HC - 1, False)
            transposes(pe, n2, h, 0)
            pe_ot1(pe, CH * B - 1, CH - 1)
            pe_wo1(pe, B - 1, 4 * B)
            pe_experts(pe)
            pe.wait_ge(s_w3l, 1)
            pe.wait_ge(s_wvl, 1)
            pe.wait_ge(n3r.hl, 2)
            first3(pe, pe_bank3, 0)
            pe.wait_ge(s_fe3, 2)
            pe_scores(pe, u3, 0, 0, q3[:, 0, 0:T], k3[:, 0, 0:T], True)
            transposes(pe, n3r, h, 1)
            pe.wait_ge(n3r.hl, 4)
            first3(pe, pe_bank3, 1)
            run3(pe, pe_slot3(pe))
            pe_pv3(pe, 4 * H3 - 1, PAIRS - 1, 1, 3, H3 - 1, False)
            pe_wo3(pe, PAIRS - 1, BEFORE + PER_PAIR * (PAIRS - 1) + 4)
            pe.wait_ge(s_gate, 16)
            transposes(pe, n4, h, 0)
            pe_gate_up(pe, 0, 0, 0)
            pe_logits(pe, 0)
            transposes(pe, n4, h, 1)
            pe_logits(pe, 1)
            pe_gate_up(pe, 0, 0, 1)
            pe_channels(pe)

        @block.vector
        def _(dve):
            dve.wait_ge(s_x[0], 32)
            ln_stats(dve, n1, x, 0)
            ln_apply(dve, n1, x, h, 0)
            dve.wait_ge(s_x[1], 32)
            ln_stats(dve, n1, x, 1)
            dve.wait_ge(s_const, 16 * 5)
            dve.tensor_copy(identb[:, :], ident[:, :]).then_inc(s_castc, 1)
            dve.tensor_copy(trib[:, :, :], tri[:, :].unsqueeze(1).to_broadcast([P, 2, P])).then_inc(s_castc, 1)
            dve.wait_ge(n1.hT, 2)
            dve_hb(dve, 0)
            ln_apply(dve, n1, x, h, 1)
            make_kbd(dve, 0, 0, (0, FIRST_HEADS), s_kb0)
            dve_max(dve, u1, 0, 0)
            make_kbd(dve, 0, 0, (FIRST_HEADS, HC))
            run1(dve, dve_slot1(dve))
            dve_pt(dve, u1, CH * HC * B - 1, 1, False)
            dve_on1(dve, CH * B - 1, CH * HC * B, CH - 1)
            hT_vector(dve, n2, 0)
            dve_x1(dve, B - 1)
            dve_stats2(dve, B - 1)
            dve_apply2(dve, B - 1)
            dve_experts(dve)
            dve.wait_ge(s_x2, NT // 2)
            ln_stats(dve, n3, x, 1)
            apply3(dve, 1)
            dve_max(dve, u3, 0, 0)
            hT_vector(dve, n3r, 1, weight=6)
            dve_recip(dve, u3, 0, 0)
            dve.wait_ge(n3.h, NT)
            run3(dve, dve_slot3(dve))
            dve_pt(dve, u3, 4 * H3 - 1, 1, False)
            dve_o3(dve, H3 - 1, 1, 1)
            dve_wo3(dve, PAIRS - 1)
            rms_vector(dve, n4, acc, h, 0)
            hT_vector(dve, n4, 0, weight=8)
            rms_vector(dve, n4, acc, h, 1)
            dve_logits(dve, 0)
            hT_vector(dve, n4, 1, weight=8)
            dve_logits(dve, 1)
            dve_alone(dve, 0, 0)
            dve_probs(dve)
            dve_top(dve)
            dve_alone(dve, 0, 1)
            dve_weights(dve)
            dve_alone(dve, 1, 0)
            dve_by_expert(dve)
            dve_alone(dve, 1, 1)
            dve.wait_ge(s_one, 1)
            dve_channels(dve)

        shared.close()


def _constants():
    import numpy as np

    ident = np.eye(P, dtype=np.float32)
    tri = np.where(np.arange(P)[None, :] <= np.arange(P)[:, None], 0.0, MASKED).astype(np.float32)
    headmask = (np.arange(P)[:, None] // HD1 == np.arange(HC)[None, :]).astype(np.float32)
    return {"ident": ident, "tri": tri, "headmask": headmask}


def _layout(i):
    import numpy as np

    a = {k: np.asarray(v) for k, v in i.items()}
    f = {k[len("L0_ffn_"):]: v for k, v in a.items() if k.startswith("L0_ffn_")}

    def chunks(w):
        return w.T.reshape(KC, P, -1).transpose(1, 0, 2)

    q = f["q_w"].reshape(H3, QHD, D)[:, :HD3]
    kv = f["kv_w"]
    k = kv[:H3 * HD3].reshape(H3, HD3, D)
    v = kv[H3 * HD3:2 * H3 * HD3].reshape(H3, HD3, D)
    qk = np.stack([np.stack([chunks(s[n]) for s in (q, k)], 1).reshape(P, -1) for n in range(H3)])
    v = np.stack([np.concatenate([chunks(v[2 * n]), chunks(v[2 * n + 1])], 2) for n in range(PAIRS)])
    o = f["o_w"].T.reshape(PAIRS, 2, HD3, D).transpose(0, 2, 1, 3)

    def padded(w):
        out = np.zeros((NCH * P, D), np.float32)
        out[:CHANNELS] = w
        return out

    g = padded(np.concatenate([f["sh_gu_w"][:SHARED], f["w1"][:, :INNER].reshape(-1, D)]))
    u = padded(np.concatenate([f["sh_gu_w"][SHARED:], f["w1"][:, INNER:].reshape(-1, D)]))
    d = padded(np.concatenate([f["sh_down_w"].T, f["w2"].transpose(0, 2, 1).reshape(-1, D)]))
    moe = np.stack([np.concatenate([chunks(g[c * P:(c + 1) * P]).reshape(P, -1),
                                    chunks(u[c * P:(c + 1) * P]).reshape(P, -1),
                                    d[c * P:(c + 1) * P]], 1) for c in range(NCH)])
    vec = np.stack([a[n].reshape(KC, P)[c] for n in ("L0_attn_bq", "L0_attn_bk", "L0_attn_bv", "L0_ffn_ln1_w",
                                                     "L0_ffn_ln2_w") for c in range(KC)], 1)
    con = _constants()
    return [a["x"].reshape(N, D), a["itok_BxS_13_99985"].reshape(N),
            a["ctx_2048"].transpose(0, 2, 1).reshape(XE * D, D),
            a["L0_attn_Wq"], a["L0_attn_Wk"], a["L0_attn_Wv"], a["L0_attn_Wo"], vec, a["L0_attn_bo"], qk, v, o,
            f["gate_w"].T, moe, con["ident"], con["tri"], con["headmask"]]


def kernel(**inputs):
    import numpy as np
    import concourse.bacc as bacc
    from concourse.bass_utils import run_bass_kernel_spmd

    nc = bacc.Bacc("TRN2", target_bir_lowering=False, num_devices=1)
    arrays, args = {}, []
    for n, v in enumerate(_layout(inputs)):
        name = f"in_{n}"
        arrays[name] = np.ascontiguousarray(v)
        args.append(nc.dram_tensor(name, arrays[name].shape, mybir.dt.from_np(arrays[name].dtype),
                                   kind="ExternalInput").ap())
    out = nc.dram_tensor("out", (N, D), F32, kind="ExternalOutput").ap()
    decoder_kernel(nc, *args, out)
    r = run_bass_kernel_spmd(nc, [arrays], core_ids=[0])
    return r.results[0]["out"].reshape(B, T, D)
```
